# Optimizing a Trainium2 kernel written in Bass

```python
import numpy as np
import jax
import jax.numpy as jnp

def _softmax(x, axis=-1):
    return jax.nn.softmax(x, axis=axis)

def _gelu(x):
    return jax.nn.gelu(x, approximate=True)

def _silu(x):
    return jax.nn.silu(x)

def _sigmoid(x):
    return jax.nn.sigmoid(x)

def _layernorm(x, axis=-1, eps=1e-05):
    m = jnp.mean(x, axis=axis, keepdims=True)
    v = jnp.var(x, axis=axis, keepdims=True)
    return (x - m) / jnp.sqrt(v + eps)

def _scatter_add(tgt, idx, src, axis=0):
    return tgt.at[idx].add(src)

def _segment_sum(src, seg, n):
    return jax.ops.segment_sum(src, seg, n)
kernel_name = 'mk_perceiver_d4_seqx_r8_6789c5'

def setup_inputs(seed: int=0):
    np.random.seed(seed)
    _w = jnp.asarray

    def _rec_inputs():
        import jax
        import jax.numpy as jnp
        _rk = jax.random.key(seed)
        x = 7.22e-05 + 1 * jax.random.normal(jax.random.fold_in(_rk, 1), (4, 32, 128), jnp.float32)
        _lenS = 32 - jax.random.randint(jax.random.fold_in(_rk, 7), (4,), 0, max(1, 32 // 4) + 1, jnp.int32)
        _lenS2 = 512 - jax.random.randint(jax.random.fold_in(_rk, 8), (4,), 0, max(1, 512 // 4) + 1, jnp.int32)
        _ctx_768P = jax.random.normal(jax.random.fold_in(_rk, 11), (4, 16, 96), jnp.float32)
        _ctx_768c = jax.random.dirichlet(jax.random.fold_in(_rk, 511), 0.3 * jnp.ones((16,), jnp.float32), (4, 512))
        _ctx_768t = jnp.einsum('bsk,bkd->bsd', _ctx_768c, _ctx_768P)
        _ctx_768t = _ctx_768t * jax.lax.rsqrt(jnp.mean(jnp.square(_ctx_768t)) + 1e-12) * 0.953939
        ctx_768 = -0.000191848 + 0.999787 * (_ctx_768t + 0.3 * jax.random.normal(jax.random.fold_in(_rk, 611), (4, 512, 96), jnp.float32))
        _validS = jnp.arange(32)[None, :] < _lenS[:, None]
        _validS2 = jnp.arange(512)[None, :] < _lenS2[:, None]
        _causal = jnp.tril(jnp.ones((32, 32), dtype=bool))
        mask_BxS2_bk0 = jnp.logical_not(jnp.broadcast_to(_validS2[:, :], (4, 512)))
        return (x, ctx_768, mask_BxS2_bk0)
    x, ctx_768, mask_BxS2_bk0 = _rec_inputs()

    def _L0_xattn_setup():
        import jax, jax.numpy as jnp
        import numpy as np
        NUM_HEADS = 16
        CLAMP = 10000.0
        key = jax.random.key(seed)
        ks = jax.random.split(key, 8)
        B, Nq, Nkv, Cq, Ckv = (4, 256, 256, 128, 96)
        s_q = 1.0 / np.sqrt(Cq)
        s_kv = 1.0 / np.sqrt(Ckv)
        return {'query': jax.random.normal(ks[0], (B, Nq, Cq), jnp.float32), 'key_value': jax.random.normal(ks[1], (B, Nkv, Ckv), jnp.float32), 'Wq': jax.random.normal(ks[2], (Cq, Cq), jnp.float32) * s_q, 'bq': jnp.zeros((Cq,), jnp.float32), 'Wk': jax.random.normal(ks[3], (Ckv, Cq), jnp.float32) * s_kv, 'bk': jnp.zeros((Cq,), jnp.float32), 'Wv': jax.random.normal(ks[4], (Ckv, Cq), jnp.float32) * s_kv, 'bv': jnp.zeros((Cq,), jnp.float32), 'Wo': jax.random.normal(ks[5], (Cq, Cq), jnp.float32) * s_q, 'bo': jnp.zeros((Cq,), jnp.float32)}
    _L0_xattn_all = _L0_xattn_setup()
    _L0_xattn_in = {k: v for k, v in _L0_xattn_all.items() if k in ('Wq', 'bq', 'Wk', 'bk', 'Wv', 'bv', 'Wo', 'bo')}
    del _L0_xattn_all

    def _L0_attn_setup():
        import jax, jax.numpy as jnp
        import numpy as np
        D_MODEL = 128
        N_HEADS = 16
        HEAD_DIM = D_MODEL // N_HEADS
        EPS = 1e-06

        def _feature_map(t):
            return jax.nn.relu(t) + EPS
        key = jax.random.key(seed)
        ks = jax.random.split(key, 5)
        b, s = (2, 256)
        x = jax.random.normal(ks[0], (b, s, D_MODEL), dtype=jnp.float32)
        scale = 1.0 / np.sqrt(D_MODEL)
        Wq = jax.random.normal(ks[1], (D_MODEL, D_MODEL), dtype=jnp.float32) * scale
        Wk = jax.random.normal(ks[2], (D_MODEL, D_MODEL), dtype=jnp.float32) * scale
        Wv = jax.random.normal(ks[3], (D_MODEL, D_MODEL), dtype=jnp.float32) * scale
        Wo = jax.random.normal(ks[4], (D_MODEL, D_MODEL), dtype=jnp.float32) * scale
        return {'x': x, 'Wq': Wq, 'Wk': Wk, 'Wv': Wv, 'Wo': Wo}
    _L0_attn_all = _L0_attn_setup()
    _L0_attn_in = {k: v for k, v in _L0_attn_all.items() if k in ('Wq', 'Wk', 'Wv', 'Wo')}
    del _L0_attn_all

    def _L0_ffn_setup():
        import jax, jax.numpy as jnp
        import numpy as np
        B, S, H, E, K = (2, 128, 128, 8, 2)
        D = 2 * H
        key = jax.random.key(seed)
        ks = jax.random.split(key, 7)
        x = jax.random.normal(ks[0], (B, S, H), dtype=jnp.float32)
        Wr = jax.random.normal(ks[1], (H, E), dtype=jnp.float32) / np.sqrt(H)
        br = jnp.zeros((E,), dtype=jnp.float32)
        W1 = jax.random.normal(ks[2], (E, H, D), dtype=jnp.float32) / np.sqrt(H)
        b1 = jnp.zeros((E, D), dtype=jnp.float32)
        W2 = jax.random.normal(ks[3], (E, D, H), dtype=jnp.float32) / np.sqrt(D)
        b2 = jnp.zeros((E, H), dtype=jnp.float32)
        return {'x': x, 'Wr': Wr, 'br': br, 'W1': W1, 'b1': b1, 'W2': W2, 'b2': b2}
    _L0_ffn_all = _L0_ffn_setup()
    _L0_ffn_in = {k: v for k, v in _L0_ffn_all.items() if k in ('Wr', 'br', 'W1', 'b1', 'W2', 'b2')}
    del _L0_ffn_all

    def _L1_xattn_setup():
        import jax, jax.numpy as jnp
        import numpy as np
        N_HEADS = 16
        key = jax.random.key(seed)
        ks = jax.random.split(key, 8)
        b, l, m = (8, 128, 128)
        d_embed, d_cross = (128, 96)
        s_q = 1.0 / np.sqrt(d_embed)
        s_kv = 1.0 / np.sqrt(d_cross)
        return {'x': jax.random.normal(ks[0], (b, l, d_embed), jnp.float32), 'y': jax.random.normal(ks[1], (b, m, d_cross), jnp.float32), 'Wq': jax.random.normal(ks[2], (d_embed, d_embed), jnp.float32) * s_q, 'bq': jax.random.normal(ks[3], (d_embed,), jnp.float32) * 0.01, 'Wkv': jax.random.normal(ks[4], (2 * d_embed, d_cross), jnp.float32) * s_kv, 'bkv': jax.random.normal(ks[5], (2 * d_embed,), jnp.float32) * 0.01, 'Wo': jax.random.normal(ks[6], (d_embed, d_embed), jnp.float32) * s_q, 'bo': jax.random.normal(ks[7], (d_embed,), jnp.float32) * 0.01}
    _L1_xattn_all = _L1_xattn_setup()
    _L1_xattn_in = {k: v for k, v in _L1_xattn_all.items() if k in ('Wq', 'bq', 'Wkv', 'bkv', 'Wo', 'bo')}
    del _L1_xattn_all

    def _L1_attn_setup():
        import jax, jax.numpy as jnp
        import numpy as np
        D_MODEL = 128
        NUM_HEADS = 16
        D_K = D_MODEL // NUM_HEADS
        ROPE_THETA = 10000.0

        def apply_rope(x, pos):
            d = x.shape[-1]
            inv_freq = ROPE_THETA ** (-jnp.arange(0, d, 2, dtype=jnp.float32) / d)
            ang = pos.astype(jnp.float32)[:, None] * inv_freq[None, :]
            cos, sin = (jnp.cos(ang), jnp.sin(ang))
            x1, x2 = (x[..., 0::2], x[..., 1::2])
            out_even = x1 * cos - x2 * sin
            out_odd = x1 * sin + x2 * cos
            return jnp.stack([out_even, out_odd], axis=-1).reshape(x.shape)
        key = jax.random.key(seed)
        kx, kq, kk, kv, ko = jax.random.split(key, 5)
        B, S = (4, 256)
        std = np.sqrt(2.0 / (D_MODEL + D_MODEL))
        x = jax.random.normal(kx, (B, S, D_MODEL), dtype=jnp.float32)
        q_proj = jax.random.normal(kq, (D_MODEL, D_MODEL), dtype=jnp.float32) * std
        k_proj = jax.random.normal(kk, (D_MODEL, D_MODEL), dtype=jnp.float32) * std
        v_proj = jax.random.normal(kv, (D_MODEL, D_MODEL), dtype=jnp.float32) * std
        o_proj = jax.random.normal(ko, (D_MODEL, D_MODEL), dtype=jnp.float32) * std
        return {'x': x, 'q_proj': q_proj, 'k_proj': k_proj, 'v_proj': v_proj, 'o_proj': o_proj}
    _L1_attn_all = _L1_attn_setup()
    _L1_attn_in = {k: v for k, v in _L1_attn_all.items() if k in ('q_proj', 'k_proj', 'v_proj', 'o_proj')}
    del _L1_attn_all

    def _L1_ffn_setup():
        import jax, jax.numpy as jnp
        import numpy as np
        N_EXPERTS = 8
        N_GROUP = 4
        TOPK_GROUP = 2
        TOP_K = 2
        HIDDEN = 128
        INTER = 256
        B, S = (1, 128)

        def _grouped_topk(scores):
            T, E = scores.shape
            per_group = E // N_GROUP
            group_scores = scores.reshape(T, N_GROUP, per_group).max(-1)
            _, gidx = jax.lax.top_k(group_scores, TOPK_GROUP)
            gmask = jnp.zeros((T, N_GROUP), scores.dtype).at[jnp.arange(T)[:, None], gidx].set(1.0)
            smask = jnp.repeat(gmask, per_group, axis=1)
            masked = jnp.where(smask > 0, scores, 0.0)
            topk_w, topk_ids = jax.lax.top_k(masked, TOP_K)
            topk_w = topk_w / topk_w.sum(-1, keepdims=True)
            return (topk_ids, topk_w)
        key = jax.random.key(seed)
        k1, k2, k3, k4 = jax.random.split(key, 4)
        return {'hidden_states': jax.random.normal(k1, (B, S, HIDDEN), jnp.float32), 'gate_w': jax.random.normal(k2, (N_EXPERTS, HIDDEN), jnp.float32) * 0.02, 'w13_weight': jax.random.normal(k3, (N_EXPERTS, 2 * INTER, HIDDEN), jnp.float32) * 0.02, 'w2_weight': jax.random.normal(k4, (N_EXPERTS, HIDDEN, INTER), jnp.float32) * 0.02}
    _L1_ffn_all = _L1_ffn_setup()
    _L1_ffn_in = {k: v for k, v in _L1_ffn_all.items() if k in ('gate_w', 'w13_weight', 'w2_weight')}
    del _L1_ffn_all

    def _L2_xattn_setup():
        import jax, jax.numpy as jnp
        import numpy as np
        N_HEADS = 16
        D_HEAD = 64
        key = jax.random.key(seed)
        ks = jax.random.split(key, 7)
        B, SQ, SKV = (2, 256, 256)
        D_MODEL, D_COND, D_ATTN = (128, 96, N_HEADS * D_HEAD)
        return {'x': jax.random.normal(ks[0], (B, SQ, D_MODEL), jnp.float32), 'cond': jax.random.normal(ks[1], (B, SKV, D_COND), jnp.float32), 'w_q': jax.random.normal(ks[2], (D_MODEL, D_ATTN), jnp.float32) * D_MODEL ** (-0.5), 'w_k': jax.random.normal(ks[3], (D_COND, D_ATTN), jnp.float32) * D_COND ** (-0.5), 'w_v': jax.random.normal(ks[4], (D_COND, D_ATTN), jnp.float32) * D_COND ** (-0.5), 'w_out': jax.random.normal(ks[5], (D_ATTN, D_MODEL), jnp.float32) * D_ATTN ** (-0.5), 'b_out': jnp.zeros((D_MODEL,), jnp.float32)}
    _L2_xattn_all = _L2_xattn_setup()
    _L2_xattn_in = {k: v for k, v in _L2_xattn_all.items() if k in ('w_q', 'w_k', 'w_v', 'w_out', 'b_out')}
    del _L2_xattn_all

    def _L2_attn_setup():
        import jax, jax.numpy as jnp
        import numpy as np
        import math
        INPUT_SIZE = 128
        HIDDEN = 128
        SEQ_LEN = 32
        BATCH = 128

        def _lstm(input_seq, w, u, bias):
            H = u.shape[0]
            B = input_seq.shape[1]
            x_proj = jnp.einsum('sbi,ih->sbh', input_seq, w) + bias

            def step(carry, xp_t):
                h_prev, c_prev = carry
                g = xp_t + h_prev @ u
                gates = jax.nn.sigmoid(g[:, :3 * H])
                c_cand = jnp.tanh(g[:, 3 * H:])
                ig, fg, og = (gates[:, :H], gates[:, H:2 * H], gates[:, 2 * H:])
                c = fg * c_prev + ig * c_cand
                h = og * jnp.tanh(c)
                return ((h, c), h)
            init = (jnp.zeros((B, H), dtype=input_seq.dtype), jnp.zeros((B, H), dtype=input_seq.dtype))
            _, hs = jax.lax.scan(step, init, x_proj)
            return hs
        key = jax.random.key(seed)
        k1, k2, k3, k4 = jax.random.split(key, 4)
        stddev = 1.0 / math.sqrt(HIDDEN)
        input_seq = jax.random.normal(k1, (SEQ_LEN, BATCH, INPUT_SIZE), dtype=jnp.float32)
        w = jax.random.uniform(k2, (INPUT_SIZE, 4 * HIDDEN), minval=-stddev, maxval=stddev, dtype=jnp.float32)
        u = jax.random.uniform(k3, (HIDDEN, 4 * HIDDEN), minval=-stddev, maxval=stddev, dtype=jnp.float32)
        bias = jax.random.uniform(k4, (4 * HIDDEN,), minval=-stddev, maxval=stddev, dtype=jnp.float32)
        return {'input_seq': input_seq, 'w': w, 'u': u, 'bias': bias}
    _L2_attn_all = _L2_attn_setup()
    _L2_attn_in = {k: v for k, v in _L2_attn_all.items() if k in ('w', 'u', 'bias')}
    del _L2_attn_all

    def _L2_ffn_setup():
        import jax, jax.numpy as jnp
        import numpy as np
        S, B, H, I, E = (64, 2, 128, 352, 8)
        key = jax.random.key(seed)
        ks = jax.random.split(key, 5)
        return {'hidden_states': jax.random.normal(ks[0], (S, B, H), dtype=jnp.float32), 'router_w': jax.random.normal(ks[1], (E, H), dtype=jnp.float32) * 0.02, 'gate_w': jax.random.normal(ks[2], (E, I, H), dtype=jnp.float32) * 0.02, 'up_w': jax.random.normal(ks[3], (E, I, H), dtype=jnp.float32) * 0.02, 'down_w': jax.random.normal(ks[4], (E, H, I), dtype=jnp.float32) * 0.02}
    _L2_ffn_all = _L2_ffn_setup()
    _L2_ffn_in = {k: v for k, v in _L2_ffn_all.items() if k in ('router_w', 'gate_w', 'up_w', 'down_w')}
    del _L2_ffn_all

    def _L3_xattn_setup():
        import jax, jax.numpy as jnp
        import numpy as np
        DIM_IN, DIM_LAT, DIM_HEAD = (96, 128, 64)
        INNER = max(DIM_LAT, DIM_IN)
        HEADS = INNER // DIM_HEAD
        SCALE = DIM_HEAD ** (-0.5)
        RMS_EPS = 1e-08
        LN_EPS = 1e-05

        def layernorm(x, g, b):
            mu = jnp.mean(x, axis=-1, keepdims=True)
            var = jnp.mean((x - mu) ** 2, axis=-1, keepdims=True)
            return (x - mu) * jax.lax.rsqrt(var + LN_EPS) * g + b

        def rmsnorm(x, gamma):
            norm = jnp.sqrt(jnp.sum(x * x, axis=-1, keepdims=True)) * x.shape[-1] ** (-0.5)
            return x / jnp.maximum(norm, RMS_EPS) * gamma
        key = jax.random.key(seed)
        ks = jax.random.split(key, 12)
        b, n, m = (4, 512, 64)
        x = jax.random.normal(ks[0], (b, n, DIM_IN), jnp.float32)
        latents = jax.random.normal(ks[1], (b, m, DIM_LAT), jnp.float32)
        mask = jax.random.randint(ks[2], (b, n), 0, 2).astype(bool)
        s = lambda k, sh, fan: jax.random.normal(k, sh, jnp.float32) * fan ** (-0.5)
        return {'x': x, 'latents': latents, 'mask': mask, 'ln_x_g': jnp.ones((DIM_IN,), jnp.float32), 'ln_x_b': jnp.zeros((DIM_IN,), jnp.float32), 'ln_l_g': jnp.ones((DIM_LAT,), jnp.float32), 'ln_l_b': jnp.zeros((DIM_LAT,), jnp.float32), 'qn_g': jnp.ones((DIM_HEAD,), jnp.float32), 'kn_g': jnp.ones((DIM_HEAD,), jnp.float32), 'Wq': s(ks[3], (INNER, DIM_LAT), DIM_LAT), 'Wkv': s(ks[4], (2 * INNER, DIM_IN), DIM_IN), 'Wlkv': s(ks[5], (2 * INNER, DIM_LAT), DIM_LAT), 'Wo': s(ks[6], (DIM_LAT, INNER), INNER), 'bo': jnp.zeros((DIM_LAT,), jnp.float32)}
    _L3_xattn_all = _L3_xattn_setup()
    _L3_xattn_in = {k: v for k, v in _L3_xattn_all.items() if k in ('ln_x_g', 'ln_x_b', 'ln_l_g', 'ln_l_b', 'qn_g', 'kn_g', 'Wq', 'Wkv', 'Wlkv', 'Wo', 'bo')}
    del _L3_xattn_all

    def _L3_attn_setup():
        import jax, jax.numpy as jnp
        import numpy as np
        D_MODEL = 128
        D_STATE = 64
        D_CONV = 7
        EXPAND = 2
        HEADDIM = 64
        NGROUPS = 1
        D_INNER = EXPAND * D_MODEL
        NHEADS = D_INNER // HEADDIM
        D_IN_PROJ = 2 * D_INNER + 2 * (2 * NGROUPS * D_STATE) + 2 * NHEADS
        CONV_DIM = D_INNER + 2 * (2 * NGROUPS * D_STATE)
        BATCH = 2
        SEQLEN = 256
        EPS = 1e-05
        key = jax.random.key(seed)
        ks = jax.random.split(key, 8)
        u = jax.random.normal(ks[0], (BATCH, SEQLEN, D_MODEL), jnp.float32)
        W_in = jax.random.normal(ks[1], (D_IN_PROJ, D_MODEL), jnp.float32) * 0.02
        conv_w = jax.random.normal(ks[2], (CONV_DIM, 1, D_CONV), jnp.float32) * 0.2
        conv_b = jax.random.normal(ks[3], (CONV_DIM,), jnp.float32) * 0.02
        dt = jnp.exp(jax.random.uniform(ks[4], (NHEADS,)) * (np.log(0.1) - np.log(0.001)) + np.log(0.001))
        dt = jnp.clip(dt, 0.0001)
        dt_bias = dt + jnp.log(-jnp.expm1(-dt))
        A_log = jnp.zeros((NHEADS,), jnp.float32)
        Dp = jnp.ones((NHEADS,), jnp.float32)
        fc_D_w = jax.random.normal(ks[5], (NHEADS, D_INNER), jnp.float32) * 0.02
        norm_w = jnp.ones((D_INNER,), jnp.float32)
        W_out = jax.random.normal(ks[6], (D_MODEL, D_INNER), jnp.float32) * 0.02
        return dict(u=u, W_in=W_in, conv_w=conv_w, conv_b=conv_b, dt_bias=dt_bias, A_log=A_log, Dp=Dp, fc_D_w=fc_D_w, norm_w=norm_w, W_out=W_out)
    _L3_attn_all = _L3_attn_setup()
    _L3_attn_in = {k: v for k, v in _L3_attn_all.items() if k in ('W_in', 'conv_w', 'conv_b', 'dt_bias', 'A_log', 'Dp', 'fc_D_w', 'norm_w', 'W_out')}
    del _L3_attn_all

    def _L3_ffn_setup():
        import jax, jax.numpy as jnp
        import numpy as np
        TOP_K = 2
        CAPACITY_FACTOR = 1.25

        def _moe_forward(x, gate_w, wi_gate, wi_up, wo):
            B, S, D = x.shape
            E = wi_gate.shape[0]
            N = B * S
            capacity = max(int(N / E * CAPACITY_FACTOR), 1)
            x_flat = x.reshape(N, D)
            router_logits = x_flat @ gate_w.T
            router_probs = jax.nn.softmax(router_logits, axis=-1)
            top_k_probs, top_k_idx = jax.lax.top_k(router_probs, TOP_K)
            top_k_probs = top_k_probs / jnp.sum(top_k_probs, axis=-1, keepdims=True)
            out = jnp.zeros_like(x_flat)
            experts = jnp.arange(E, dtype=jnp.int32)
            for k in range(TOP_K):
                eid = top_k_idx[:, k]
                ew = top_k_probs[:, k]
                onehot = (eid[:, None] == experts[None, :]).astype(jnp.int32)
                pos_all = jnp.cumsum(onehot, axis=0) - 1
                pos = jnp.take_along_axis(pos_all, eid[:, None].astype(jnp.int32), axis=1)[:, 0]
                valid = pos < capacity
                pos_c = jnp.where(valid, pos, 0)
                disp = jnp.zeros((E, capacity, D), x_flat.dtype).at[eid, pos_c].add(jnp.where(valid[:, None], x_flat, 0.0))
                gate = jax.nn.silu(jnp.einsum('ecd,efd->ecf', disp, wi_gate))
                up = jnp.einsum('ecd,efd->ecf', disp, wi_up)
                expert_out = jnp.einsum('ecf,edf->ecd', gate * up, wo)
                tok_out = expert_out[eid, pos_c]
                out = out + jnp.where(valid[:, None], ew[:, None] * tok_out, 0.0)
            return out.reshape(B, S, D)
        key = jax.random.key(seed)
        k1, k2, k3, k4, k5 = jax.random.split(key, 5)
        B, S, D, F, E = (4, 256, 128, 512, 8)
        return {'x': jax.random.normal(k1, (B, S, D), dtype=jnp.float32), 'gate_w': jax.random.normal(k2, (E, D), dtype=jnp.float32) * 0.02, 'wi_gate': jax.random.normal(k3, (E, F, D), dtype=jnp.float32) * 0.02, 'wi_up': jax.random.normal(k4, (E, F, D), dtype=jnp.float32) * 0.02, 'wo': jax.random.normal(k5, (E, D, F), dtype=jnp.float32) * 0.02}
    _L3_ffn_all = _L3_ffn_setup()
    _L3_ffn_in = {k: v for k, v in _L3_ffn_all.items() if k in ('gate_w', 'wi_gate', 'wi_up', 'wo')}
    del _L3_ffn_all
    return {'x': x, 'ctx_768': ctx_768, 'mask_BxS2_bk0': mask_BxS2_bk0, 'L0_xattn_Wq': _L0_xattn_in['Wq'], 'L0_xattn_bq': _L0_xattn_in['bq'], 'L0_xattn_Wk': _L0_xattn_in['Wk'], 'L0_xattn_bk': _L0_xattn_in['bk'], 'L0_xattn_Wv': _L0_xattn_in['Wv'], 'L0_xattn_bv': _L0_xattn_in['bv'], 'L0_xattn_Wo': _L0_xattn_in['Wo'], 'L0_xattn_bo': _L0_xattn_in['bo'], 'L0_attn_Wq': _L0_attn_in['Wq'], 'L0_attn_Wk': _L0_attn_in['Wk'], 'L0_attn_Wv': _L0_attn_in['Wv'], 'L0_attn_Wo': _L0_attn_in['Wo'], 'L0_ffn_Wr': _L0_ffn_in['Wr'], 'L0_ffn_br': _L0_ffn_in['br'], 'L0_ffn_W1': _L0_ffn_in['W1'], 'L0_ffn_b1': _L0_ffn_in['b1'], 'L0_ffn_W2': _L0_ffn_in['W2'], 'L0_ffn_b2': _L0_ffn_in['b2'], 'L1_xattn_Wq': _L1_xattn_in['Wq'], 'L1_xattn_bq': _L1_xattn_in['bq'], 'L1_xattn_Wkv': _L1_xattn_in['Wkv'], 'L1_xattn_bkv': _L1_xattn_in['bkv'], 'L1_xattn_Wo': _L1_xattn_in['Wo'], 'L1_xattn_bo': _L1_xattn_in['bo'], 'L1_attn_q_proj': _L1_attn_in['q_proj'], 'L1_attn_k_proj': _L1_attn_in['k_proj'], 'L1_attn_v_proj': _L1_attn_in['v_proj'], 'L1_attn_o_proj': _L1_attn_in['o_proj'], 'L1_ffn_gate_w': _L1_ffn_in['gate_w'], 'L1_ffn_w13_weight': _L1_ffn_in['w13_weight'], 'L1_ffn_w2_weight': _L1_ffn_in['w2_weight'], 'L2_xattn_w_q': _L2_xattn_in['w_q'], 'L2_xattn_w_k': _L2_xattn_in['w_k'], 'L2_xattn_w_v': _L2_xattn_in['w_v'], 'L2_xattn_w_out': _L2_xattn_in['w_out'], 'L2_xattn_b_out': _L2_xattn_in['b_out'], 'L2_attn_w': _L2_attn_in['w'], 'L2_attn_u': _L2_attn_in['u'], 'L2_attn_bias': _L2_attn_in['bias'], 'L2_ffn_router_w': _L2_ffn_in['router_w'], 'L2_ffn_gate_w': _L2_ffn_in['gate_w'], 'L2_ffn_up_w': _L2_ffn_in['up_w'], 'L2_ffn_down_w': _L2_ffn_in['down_w'], 'L3_xattn_ln_x_g': _L3_xattn_in['ln_x_g'], 'L3_xattn_ln_x_b': _L3_xattn_in['ln_x_b'], 'L3_xattn_ln_l_g': _L3_xattn_in['ln_l_g'], 'L3_xattn_ln_l_b': _L3_xattn_in['ln_l_b'], 'L3_xattn_qn_g': _L3_xattn_in['qn_g'], 'L3_xattn_kn_g': _L3_xattn_in['kn_g'], 'L3_xattn_Wq': _L3_xattn_in['Wq'], 'L3_xattn_Wkv': _L3_xattn_in['Wkv'], 'L3_xattn_Wlkv': _L3_xattn_in['Wlkv'], 'L3_xattn_Wo': _L3_xattn_in['Wo'], 'L3_xattn_bo': _L3_xattn_in['bo'], 'L3_attn_W_in': _L3_attn_in['W_in'], 'L3_attn_conv_w': _L3_attn_in['conv_w'], 'L3_attn_conv_b': _L3_attn_in['conv_b'], 'L3_attn_dt_bias': _L3_attn_in['dt_bias'], 'L3_attn_A_log': _L3_attn_in['A_log'], 'L3_attn_Dp': _L3_attn_in['Dp'], 'L3_attn_fc_D_w': _L3_attn_in['fc_D_w'], 'L3_attn_norm_w': _L3_attn_in['norm_w'], 'L3_attn_W_out': _L3_attn_in['W_out'], 'L3_ffn_gate_w': _L3_ffn_in['gate_w'], 'L3_ffn_wi_gate': _L3_ffn_in['wi_gate'], 'L3_ffn_wi_up': _L3_ffn_in['wi_up'], 'L3_ffn_wo': _L3_ffn_in['wo']}

def reference(x, ctx_768, mask_BxS2_bk0, L0_xattn_Wq, L0_xattn_bq, L0_xattn_Wk, L0_xattn_bk, L0_xattn_Wv, L0_xattn_bv, L0_xattn_Wo, L0_xattn_bo, L0_attn_Wq, L0_attn_Wk, L0_attn_Wv, L0_attn_Wo, L0_ffn_Wr, L0_ffn_br, L0_ffn_W1, L0_ffn_b1, L0_ffn_W2, L0_ffn_b2, L1_xattn_Wq, L1_xattn_bq, L1_xattn_Wkv, L1_xattn_bkv, L1_xattn_Wo, L1_xattn_bo, L1_attn_q_proj, L1_attn_k_proj, L1_attn_v_proj, L1_attn_o_proj, L1_ffn_gate_w, L1_ffn_w13_weight, L1_ffn_w2_weight, L2_xattn_w_q, L2_xattn_w_k, L2_xattn_w_v, L2_xattn_w_out, L2_xattn_b_out, L2_attn_w, L2_attn_u, L2_attn_bias, L2_ffn_router_w, L2_ffn_gate_w, L2_ffn_up_w, L2_ffn_down_w, L3_xattn_ln_x_g, L3_xattn_ln_x_b, L3_xattn_ln_l_g, L3_xattn_ln_l_b, L3_xattn_qn_g, L3_xattn_kn_g, L3_xattn_Wq, L3_xattn_Wkv, L3_xattn_Wlkv, L3_xattn_Wo, L3_xattn_bo, L3_attn_W_in, L3_attn_conv_w, L3_attn_conv_b, L3_attn_dt_bias, L3_attn_A_log, L3_attn_Dp, L3_attn_fc_D_w, L3_attn_norm_w, L3_attn_W_out, L3_ffn_gate_w, L3_ffn_wi_gate, L3_ffn_wi_up, L3_ffn_wo):
    import jax
    import jax.numpy as jnp

    def _L0_xattn_ref(query, key_value, Wq, bq, Wk, bk, Wv, bv, Wo, bo):
        import jax, jax.numpy as jnp
        import numpy as np
        NUM_HEADS = 16
        CLAMP = 10000.0
        B, Nq, Cq = query.shape
        Nkv = key_value.shape[1]
        H = NUM_HEADS
        D = Cq // H
        scale = D ** (-0.5)
        q = (query @ Wq + bq).reshape(B, Nq, H, D).transpose(0, 2, 1, 3)
        k = (key_value @ Wk + bk).reshape(B, Nkv, H, D).transpose(0, 2, 1, 3)
        v = (key_value @ Wv + bv).reshape(B, Nkv, H, D).transpose(0, 2, 1, 3)
        attn = jnp.einsum('bhqd,bhkd->bhqk', q, k) * scale
        attn = jnp.clip(attn, -CLAMP, CLAMP)
        attn = jax.nn.softmax(attn, axis=-1)
        attn = jnp.where(jnp.any(jnp.isnan(attn)), jnp.asarray(1.0 / Nkv, attn.dtype), attn)
        x = jnp.einsum('bhqk,bhkd->bqhd', attn, v).reshape(B, Nq, Cq)
        return x @ Wo + bo

    def _L0_attn_ref(x, Wq, Wk, Wv, Wo):
        import jax, jax.numpy as jnp
        import numpy as np
        D_MODEL = 128
        N_HEADS = 16
        HEAD_DIM = D_MODEL // N_HEADS
        EPS = 1e-06

        def _feature_map(t):
            return jax.nn.relu(t) + EPS
        b, s, _ = x.shape
        q = (x @ Wq.T).reshape(b, s, N_HEADS, HEAD_DIM)
        k = (x @ Wk.T).reshape(b, s, N_HEADS, HEAD_DIM)
        v = (x @ Wv.T).reshape(b, s, N_HEADS, HEAD_DIM)
        q = _feature_map(q).transpose(0, 2, 1, 3)
        k = _feature_map(k).transpose(0, 2, 1, 3)
        v = v.transpose(0, 2, 1, 3)
        kv = jnp.einsum('bhsd,bhsm->bhsdm', k, v)
        kv_cum = jnp.cumsum(kv, axis=2)
        out = jnp.einsum('bhsd,bhsdm->bhsm', q, kv_cum)
        k_cum = jnp.cumsum(k, axis=2)
        z = 1.0 / (jnp.einsum('bhsd,bhsd->bhs', q, k_cum) + EPS)
        out = out * z[..., None]
        out = out.transpose(0, 2, 1, 3).reshape(b, s, D_MODEL)
        return out @ Wo.T

    def _L0_ffn_ref(x, Wr, br, W1, b1, W2, b2):
        import jax, jax.numpy as jnp
        import numpy as np
        B, S, H, E, K = (2, 128, 128, 8, 2)
        D = 2 * H
        logits = jnp.einsum('bsh,he->bse', x, Wr) + br
        probs = jax.nn.softmax(logits, axis=-1)
        top_p, top_i = jax.lax.top_k(probs, K)
        cw = jnp.sum(jax.nn.one_hot(top_i, E, dtype=x.dtype) * top_p[..., None], axis=-2)
        h = jax.nn.relu(jnp.einsum('bsh,ehd->bsed', x, W1) + b1)
        y = jnp.einsum('bsed,edh->bseh', h, W2) + b2
        out = jnp.einsum('bseh,bse->bsh', y, cw)
        return out

    def _L1_xattn_ref(x, y, Wq, bq, Wkv, bkv, Wo, bo):
        import jax, jax.numpy as jnp
        import numpy as np
        N_HEADS = 16
        b, l, d = x.shape
        m = y.shape[1]
        h = N_HEADS
        dh = d // h
        q = (jnp.einsum('bld,ed->ble', x, Wq) + bq).reshape(b, l, h, dh)
        kv = (jnp.einsum('bmc,ec->bme', y, Wkv) + bkv).reshape(b, m, h, 2 * dh)
        k, v = (kv[..., :dh], kv[..., dh:])
        scale = 1.0 / jnp.sqrt(jnp.asarray(dh, x.dtype))
        att = jax.nn.softmax(jnp.einsum('blhd,bmhd->blmh', q, k) * scale, axis=2)
        out = jnp.einsum('blmh,bmhd->blhd', att, v).reshape(b, l, d)
        return jnp.einsum('bld,ed->ble', out, Wo) + bo

    def _L1_attn_ref(x, q_proj, k_proj, v_proj, o_proj):
        import jax, jax.numpy as jnp
        import numpy as np
        D_MODEL = 128
        NUM_HEADS = 16
        D_K = D_MODEL // NUM_HEADS
        ROPE_THETA = 10000.0

        def apply_rope(x, pos):
            d = x.shape[-1]
            inv_freq = ROPE_THETA ** (-jnp.arange(0, d, 2, dtype=jnp.float32) / d)
            ang = pos.astype(jnp.float32)[:, None] * inv_freq[None, :]
            cos, sin = (jnp.cos(ang), jnp.sin(ang))
            x1, x2 = (x[..., 0::2], x[..., 1::2])
            out_even = x1 * cos - x2 * sin
            out_odd = x1 * sin + x2 * cos
            return jnp.stack([out_even, out_odd], axis=-1).reshape(x.shape)
        B, S, D = x.shape
        nh, dk = (NUM_HEADS, D // NUM_HEADS)

        def split_heads(t):
            return t.reshape(B, S, nh, dk).transpose(0, 2, 1, 3)
        q = split_heads(x @ q_proj.T)
        k = split_heads(x @ k_proj.T)
        v = split_heads(x @ v_proj.T)
        pos = jnp.arange(S)
        q = apply_rope(q, pos)
        k = apply_rope(k, pos)
        scores = jnp.einsum('bhqd,bhkd->bhqk', q, k) / jnp.sqrt(jnp.float32(dk))
        causal = jnp.tril(jnp.ones((S, S), dtype=bool))
        scores = jnp.where(causal, scores, -jnp.inf)
        attn = jax.nn.softmax(scores, axis=-1)
        out = jnp.einsum('bhqk,bhkd->bhqd', attn, v)
        out = out.transpose(0, 2, 1, 3).reshape(B, S, D)
        return out @ o_proj.T

    def _L1_ffn_ref(hidden_states, gate_w, w13_weight, w2_weight):
        import jax, jax.numpy as jnp
        import numpy as np
        N_EXPERTS = 8
        N_GROUP = 4
        TOPK_GROUP = 2
        TOP_K = 2
        HIDDEN = 128
        INTER = 256
        B, S = (1, 128)

        def _grouped_topk(scores):
            T, E = scores.shape
            per_group = E // N_GROUP
            group_scores = scores.reshape(T, N_GROUP, per_group).max(-1)
            _, gidx = jax.lax.top_k(group_scores, TOPK_GROUP)
            gmask = jnp.zeros((T, N_GROUP), scores.dtype).at[jnp.arange(T)[:, None], gidx].set(1.0)
            smask = jnp.repeat(gmask, per_group, axis=1)
            masked = jnp.where(smask > 0, scores, 0.0)
            topk_w, topk_ids = jax.lax.top_k(masked, TOP_K)
            topk_w = topk_w / topk_w.sum(-1, keepdims=True)
            return (topk_ids, topk_w)
        Bm, Sm, H = hidden_states.shape
        x = hidden_states.reshape(-1, H)
        T = x.shape[0]
        scores = jax.nn.softmax(x @ gate_w.T, axis=-1)
        topk_ids, topk_w = _grouped_topk(scores)
        combine = jnp.zeros((T, N_EXPERTS), x.dtype).at[jnp.arange(T)[:, None], topk_ids].add(topk_w)
        gu = jnp.einsum('th,eih->tei', x, w13_weight)
        gate, up = (gu[..., :INTER], gu[..., INTER:])
        act = jax.nn.silu(gate) * up
        act = act * combine[:, :, None]
        out = jnp.einsum('tei,ehi->th', act, w2_weight)
        return out.reshape(Bm, Sm, H)

    def _L2_xattn_ref(x, cond, w_q, w_k, w_v, w_out, b_out):
        import jax, jax.numpy as jnp
        import numpy as np
        N_HEADS = 16
        D_HEAD = 64
        B, SQ, _ = x.shape
        SKV = cond.shape[1]
        scale = D_HEAD ** (-0.5)
        q = (x @ w_q).reshape(B, SQ, N_HEADS, D_HEAD)
        k = (cond @ w_k).reshape(B, SKV, N_HEADS, D_HEAD)
        v = (cond @ w_v).reshape(B, SKV, N_HEADS, D_HEAD)
        attn = jnp.einsum('bqhd,bkhd->bhqk', q, k) * scale
        attn = jax.nn.softmax(attn, axis=-1)
        out = jnp.einsum('bhqk,bkhd->bqhd', attn, v).reshape(B, SQ, N_HEADS * D_HEAD)
        return out @ w_out + b_out

    def _L2_attn_ref(input_seq, w, u, bias):
        import jax, jax.numpy as jnp
        import numpy as np
        import math
        INPUT_SIZE = 128
        HIDDEN = 128
        SEQ_LEN = 32
        BATCH = 128

        def _lstm(input_seq, w, u, bias):
            H = u.shape[0]
            B = input_seq.shape[1]
            x_proj = jnp.einsum('sbi,ih->sbh', input_seq, w) + bias

            def step(carry, xp_t):
                h_prev, c_prev = carry
                g = xp_t + h_prev @ u
                gates = jax.nn.sigmoid(g[:, :3 * H])
                c_cand = jnp.tanh(g[:, 3 * H:])
                ig, fg, og = (gates[:, :H], gates[:, H:2 * H], gates[:, 2 * H:])
                c = fg * c_prev + ig * c_cand
                h = og * jnp.tanh(c)
                return ((h, c), h)
            init = (jnp.zeros((B, H), dtype=input_seq.dtype), jnp.zeros((B, H), dtype=input_seq.dtype))
            _, hs = jax.lax.scan(step, init, x_proj)
            return hs
        return _lstm(input_seq, w, u, bias)

    def _L2_ffn_ref(hidden_states, router_w, gate_w, up_w, down_w):
        import jax, jax.numpy as jnp
        import numpy as np
        S, B, H, I, E = (64, 2, 128, 352, 8)
        router_logits = jnp.einsum('sbh,eh->sbe', hidden_states, router_w)
        routing_indices = jnp.argmax(router_logits, axis=-1)
        out = jnp.zeros_like(hidden_states)
        for e in range(E):
            mask = (routing_indices == e)[..., None]
            xe = jnp.where(mask, hidden_states, 0.0)
            g = jnp.einsum('sbh,ih->sbi', xe, gate_w[e])
            u = jnp.einsum('sbh,ih->sbi', xe, up_w[e])
            ye = jnp.einsum('sbi,hi->sbh', jax.nn.silu(g) * u, down_w[e])
            out = out + jnp.where(mask, ye, 0.0)
        return out

    def _L3_xattn_ref(x, latents, mask, ln_x_g, ln_x_b, ln_l_g, ln_l_b, qn_g, kn_g, Wq, Wkv, Wlkv, Wo, bo):
        import jax, jax.numpy as jnp
        import numpy as np
        DIM_IN, DIM_LAT, DIM_HEAD = (96, 128, 64)
        INNER = max(DIM_LAT, DIM_IN)
        HEADS = INNER // DIM_HEAD
        SCALE = DIM_HEAD ** (-0.5)
        RMS_EPS = 1e-08
        LN_EPS = 1e-05

        def layernorm(x, g, b):
            mu = jnp.mean(x, axis=-1, keepdims=True)
            var = jnp.mean((x - mu) ** 2, axis=-1, keepdims=True)
            return (x - mu) * jax.lax.rsqrt(var + LN_EPS) * g + b

        def rmsnorm(x, gamma):
            norm = jnp.sqrt(jnp.sum(x * x, axis=-1, keepdims=True)) * x.shape[-1] ** (-0.5)
            return x / jnp.maximum(norm, RMS_EPS) * gamma
        b, n, _ = x.shape
        m = latents.shape[1]
        xn = layernorm(x, ln_x_g, ln_x_b)
        ln = layernorm(latents, ln_l_g, ln_l_b)
        q = ln @ Wq.T
        kv = jnp.concatenate([xn @ Wkv.T, ln @ Wlkv.T], axis=1)
        k, v = (kv[..., :INNER], kv[..., INNER:])
        split_heads = lambda t: t.reshape(t.shape[0], t.shape[1], HEADS, DIM_HEAD).transpose(0, 2, 1, 3)
        q, k, v = (split_heads(q), split_heads(k), split_heads(v))
        qn = rmsnorm(q, qn_g) * SCALE
        kn = rmsnorm(k, kn_g)
        attn = jnp.einsum('bhid,bhjd->bhij', qn, kn)
        full_mask = jnp.pad(mask, ((0, 0), (0, m)), constant_values=True)
        attn = jnp.where(full_mask[:, None, None, :], attn, -jnp.finfo(attn.dtype).max)
        attn = jax.nn.softmax(attn, axis=-1)
        out = jnp.einsum('bhij,bhjd->bhid', attn, v)
        out = out.transpose(0, 2, 1, 3).reshape(b, m, INNER)
        return out @ Wo.T + bo

    def _L3_attn_ref(u, W_in, conv_w, conv_b, dt_bias, A_log, Dp, fc_D_w, norm_w, W_out):
        import jax, jax.numpy as jnp
        import numpy as np
        D_MODEL = 128
        D_STATE = 64
        D_CONV = 7
        EXPAND = 2
        HEADDIM = 64
        NGROUPS = 1
        D_INNER = EXPAND * D_MODEL
        NHEADS = D_INNER // HEADDIM
        D_IN_PROJ = 2 * D_INNER + 2 * (2 * NGROUPS * D_STATE) + 2 * NHEADS
        CONV_DIM = D_INNER + 2 * (2 * NGROUPS * D_STATE)
        BATCH = 2
        SEQLEN = 256
        EPS = 1e-05
        b, L, _ = u.shape
        gn = NGROUPS * D_STATE
        zxbcdt = jnp.einsum('bld,ed->ble', u, W_in)
        A = -jnp.exp(A_log)
        z = zxbcdt[..., :D_INNER]
        xBC = zxbcdt[..., D_INNER:D_INNER + CONV_DIM]
        dt_raw = zxbcdt[..., D_INNER + CONV_DIM:]
        dt = jnp.concatenate([dt_raw[..., :NHEADS], dt_raw[..., NHEADS:][:, ::-1]], axis=0)
        dt = jax.nn.softplus(dt + dt_bias)
        xc = jnp.transpose(xBC, (0, 2, 1))
        xc = jax.lax.conv_general_dilated(xc, conv_w, (1,), [(D_CONV // 2, D_CONV // 2)], dimension_numbers=('NCH', 'OIH', 'NCH'), feature_group_count=CONV_DIM)
        xc = xc + conv_b[None, :, None]
        xBC = jax.nn.silu(jnp.transpose(xc, (0, 2, 1)))
        x = xBC[..., :D_INNER]
        BC = xBC[..., D_INNER:]
        x_og = x
        x2 = jnp.concatenate([x, x[:, ::-1]], axis=0)
        BC2 = jnp.concatenate([BC[..., :2 * gn], BC[..., 2 * gn:][:, ::-1]], axis=0)
        Bm = BC2[..., :gn].reshape(2 * b, L, NGROUPS, D_STATE)
        Cm = BC2[..., gn:].reshape(2 * b, L, NGROUPS, D_STATE)
        x_scan = x2.reshape(2 * b, L, NHEADS, HEADDIM)
        hpg = NHEADS // NGROUPS
        Bh = jnp.repeat(Bm, hpg, axis=2)
        Ch = jnp.repeat(Cm, hpg, axis=2)

        def step(state, ins):
            x_t, dt_t, B_t, C_t = ins
            ex = jnp.exp(A[None, :, None, None] * dt_t[:, :, None, None])
            state = state * ex + x_t[..., None] * B_t[:, :, None, :]
            y_t = jnp.sum(state * C_t[:, :, None, :], axis=-1)
            return (state, y_t)
        xs = (jnp.moveaxis(x_scan, 1, 0), jnp.moveaxis(dt, 1, 0), jnp.moveaxis(Bh, 1, 0), jnp.moveaxis(Ch, 1, 0))
        state0 = jnp.zeros((2 * b, NHEADS, HEADDIM, D_STATE), u.dtype)
        _, ys = jax.lax.scan(step, state0, xs)
        y = jnp.moveaxis(ys, 0, 1).reshape(2 * b, L, D_INNER)
        y = jnp.concatenate([jnp.zeros_like(y[:, :1]), y[:, :-1]], axis=1)
        y_fw, y_bw = (y[:b], y[b:][:, ::-1])
        diag_heads = jnp.einsum('bld,hd->blh', x_og, fc_D_w) + Dp
        diag = jnp.repeat(diag_heads, HEADDIM, axis=-1)
        y = y_fw + y_bw + x_og * diag
        rms = jnp.sqrt(jnp.mean(y * y, axis=-1, keepdims=True) + EPS)
        y = norm_w * (y / rms) * jax.nn.silu(z)
        return jnp.einsum('ble,de->bld', y, W_out)

    def _L3_ffn_ref(x, gate_w, wi_gate, wi_up, wo):
        import jax, jax.numpy as jnp
        import numpy as np
        TOP_K = 2
        CAPACITY_FACTOR = 1.25

        def _moe_forward(x, gate_w, wi_gate, wi_up, wo):
            B, S, D = x.shape
            E = wi_gate.shape[0]
            N = B * S
            capacity = max(int(N / E * CAPACITY_FACTOR), 1)
            x_flat = x.reshape(N, D)
            router_logits = x_flat @ gate_w.T
            router_probs = jax.nn.softmax(router_logits, axis=-1)
            top_k_probs, top_k_idx = jax.lax.top_k(router_probs, TOP_K)
            top_k_probs = top_k_probs / jnp.sum(top_k_probs, axis=-1, keepdims=True)
            out = jnp.zeros_like(x_flat)
            experts = jnp.arange(E, dtype=jnp.int32)
            for k in range(TOP_K):
                eid = top_k_idx[:, k]
                ew = top_k_probs[:, k]
                onehot = (eid[:, None] == experts[None, :]).astype(jnp.int32)
                pos_all = jnp.cumsum(onehot, axis=0) - 1
                pos = jnp.take_along_axis(pos_all, eid[:, None].astype(jnp.int32), axis=1)[:, 0]
                valid = pos < capacity
                pos_c = jnp.where(valid, pos, 0)
                disp = jnp.zeros((E, capacity, D), x_flat.dtype).at[eid, pos_c].add(jnp.where(valid[:, None], x_flat, 0.0))
                gate = jax.nn.silu(jnp.einsum('ecd,efd->ecf', disp, wi_gate))
                up = jnp.einsum('ecd,efd->ecf', disp, wi_up)
                expert_out = jnp.einsum('ecf,edf->ecd', gate * up, wo)
                tok_out = expert_out[eid, pos_c]
                out = out + jnp.where(valid[:, None], ew[:, None] * tok_out, 0.0)
            return out.reshape(B, S, D)
        return _moe_forward(x, gate_w, wi_gate, wi_up, wo)
    x = x + _L0_xattn_ref(_layernorm(x, axis=-1), ctx_768, L0_xattn_Wq, L0_xattn_bq, L0_xattn_Wk, L0_xattn_bk, L0_xattn_Wv, L0_xattn_bv, L0_xattn_Wo, L0_xattn_bo)
    x = x + _L0_attn_ref(_layernorm(x, axis=-1), L0_attn_Wq, L0_attn_Wk, L0_attn_Wv, L0_attn_Wo)
    x = x + _L0_ffn_ref(_layernorm(x, axis=-1), L0_ffn_Wr, L0_ffn_br, L0_ffn_W1, L0_ffn_b1, L0_ffn_W2, L0_ffn_b2)
    x = x + _L1_xattn_ref(_layernorm(x, axis=-1), ctx_768, L1_xattn_Wq, L1_xattn_bq, L1_xattn_Wkv, L1_xattn_bkv, L1_xattn_Wo, L1_xattn_bo)
    x = x + _L1_attn_ref(_layernorm(x, axis=-1), L1_attn_q_proj, L1_attn_k_proj, L1_attn_v_proj, L1_attn_o_proj)
    x = x + _L1_ffn_ref(_layernorm(x, axis=-1), L1_ffn_gate_w, L1_ffn_w13_weight, L1_ffn_w2_weight)
    x = x + _L2_xattn_ref(_layernorm(x, axis=-1), ctx_768, L2_xattn_w_q, L2_xattn_w_k, L2_xattn_w_v, L2_xattn_w_out, L2_xattn_b_out)
    x = x + _L2_attn_ref(_layernorm(x, axis=-1), L2_attn_w, L2_attn_u, L2_attn_bias)
    x = x + _L2_ffn_ref(_layernorm(x, axis=-1), L2_ffn_router_w, L2_ffn_gate_w, L2_ffn_up_w, L2_ffn_down_w)
    x = x + _L3_xattn_ref(ctx_768, _layernorm(x, axis=-1), mask_BxS2_bk0, L3_xattn_ln_x_g, L3_xattn_ln_x_b, L3_xattn_ln_l_g, L3_xattn_ln_l_b, L3_xattn_qn_g, L3_xattn_kn_g, L3_xattn_Wq, L3_xattn_Wkv, L3_xattn_Wlkv, L3_xattn_Wo, L3_xattn_bo)
    x = x + _L3_attn_ref(_layernorm(x, axis=-1), L3_attn_W_in, L3_attn_conv_w, L3_attn_conv_b, L3_attn_dt_bias, L3_attn_A_log, L3_attn_Dp, L3_attn_fc_D_w, L3_attn_norm_w, L3_attn_W_out)
    x = x + _L3_ffn_ref(_layernorm(x, axis=-1), L3_ffn_gate_w, L3_ffn_wi_gate, L3_ffn_wi_up, L3_ffn_wo)
    return x

_drawn_inputs = setup_inputs


def setup_inputs(seed=0):
    import zlib

    import numpy as np

    out = dict(_drawn_inputs(seed))
    spreads = {'L0_xattn_bq': (0.0, 0.1),
     'L0_xattn_bk': (0.0, 2.0),
     'L0_xattn_bv': (0.0, 0.1),
     'L0_xattn_bo': (0.0, 0.1),
     'L0_ffn_br': (0.0, 0.1),
     'L0_ffn_b1': (0.0, 0.345),
     'L0_ffn_b2': (0.0, 0.1),
     'L2_xattn_b_out': (0.0, 0.1),
     'L3_xattn_ln_x_g': (1.0, 0.6),
     'L3_xattn_ln_x_b': (0.0, 0.1),
     'L3_xattn_ln_l_g': (1.0, 0.2),
     'L3_xattn_ln_l_b': (0.0, 0.352),
     'L3_xattn_qn_g': (1.0, 0.6),
     'L3_xattn_kn_g': (1.0, 0.6),
     'L3_xattn_bo': (0.0, 0.507),
     'L3_attn_A_log': (0.0, 0.8),
     'L3_attn_Dp': (1.0, 0.6),
     'L3_attn_norm_w': (1.0, 0.6)}
    factors = {'L1_xattn_bq': 8.0,
     'L1_xattn_bkv': 7.805,
     'L1_xattn_bo': 8.0,
     'L1_ffn_gate_w': 8.0,
     'L1_ffn_w13_weight': 8.0,
     'L1_ffn_w2_weight': 8.0,
     'L2_attn_u': 6.245,
     'L2_attn_bias': 6.529,
     'L2_ffn_router_w': 8.0,
     'L2_ffn_gate_w': 8.0,
     'L2_ffn_up_w': 8.0,
     'L2_ffn_down_w': 8.0,
     'L3_attn_conv_w': 13.47,
     'L3_attn_conv_b': 33.491,
     'L3_attn_dt_bias': 8.0,
     'L3_attn_fc_D_w': 200.0,
     'L3_ffn_gate_w': 8.0,
     'L3_ffn_wi_gate': 8.0,
     'L3_ffn_wi_up': 8.0,
     'L3_ffn_wo': 8.0,
     'L3_attn_W_in': 4.677}
    for name, (base, spread) in spreads.items():
        noise = np.random.default_rng([zlib.crc32(name.encode()), seed]).standard_normal(out[name].shape)
        drawn = base * np.exp(spread * noise) if base else spread * noise
        out[name] = jnp.asarray(drawn.astype(out[name].dtype))
    for name, factor in factors.items():
        out[name] = (out[name] * factor).astype(out[name].dtype)
    return out
```

```python
from contextlib import ExitStack

import numpy as np

import concourse.bass as bass
from concourse import mybir

F32 = mybir.dt.float32
U32 = mybir.dt.uint32
I32 = mybir.dt.int32
U8 = mybir.dt.uint8
ALU = mybir.AluOpType
ACT = mybir.ActivationFunctionType
AX = mybir.AxisListType

STAGES = 12

B, S, D = 4, 32, 128
T = B * S
H = 16
DH = D // H
SK, DC = 512, 96
CK = SK // 128
NC = B * CK
CA = DC + 1
E = 8
HG = H // 4
NG = B * HG
LN_EPS = 1e-5
BIG = 3.0e38
CAP = int(T / E * 1.25)
RSQRT_MAGIC = float(0x5F3759DF)
H2, D2 = 16, 64
H3, D3 = 2, 64
DI, NS_, NH = 256, 64, 4
TAPS = 7
PAD = TAPS // 2
SP = S + 2 * PAD
FFN_CHUNKS = {0: 2, 1: 2, 2: 3, 3: 4}

EARLY = [("ident", 128), ("head16", 16), ("head4", 4), ("fold", 32), ("ones", 128), ("causal_ts", 128),
         ("wq0", 128), ("bq0", 1), ("wkT0", CA), ("wv0", 128), ("wo0", 128)]
LATE = [("causal_add", 32), ("fold4", 4), ("rope_cos", 128), ("rope_sin", 128), ("cum", 128),
        ("m_fw", 128), ("m_bw", 128), ("l_fw", 128), ("l_bw", 128), ("batch_add", 128), ("iota", 8),
        ("a_wq", 128), ("a_wk", 128), ("a_wv", 128), ("a_wo", 128),
        ("f0_wr", 8), ("f0_b1", 16), ("f0_b2", 128),
        ("wq1", 128), ("bq1", 1), ("wkT1", CA), ("wv1", 128), ("wo1", 128),
        ("r_wq", 256), ("r_wk", 256), ("r_wv", 128), ("r_wo", 128), ("f1_wr", 8),
        ("lstm_w", 512), ("lstm_u", 512), ("f2_wr", 8),
        ("x3_g", 1), ("x3_b", 1), ("l3_g", 1), ("l3_b", 1), ("qn_g", 1), ("kn_g", 1),
        ("x3_wqkv", 384), ("x3_wkv", 256), ("x3_wo", 128),
        ("m_in", 776), ("m_cw", 28), ("m_cb", 4), ("m_fc", 8), ("m_nw", 2), ("m_out", 256), ("f3_wr", 8)]
ROWS = [("bo0", 128), ("bo1", 128), ("bo2", 128), ("bo3", 128), ("f0_br", 8), ("dtb", 4), ("alog", 4), ("dp", 4),
        ("lstm_b", 512)]


def columns(table):
    at, out = 0, {}
    for name, n in table:
        out[name] = (at, n)
        at += n
    return out, at


def build(nc, dram):
    with ExitStack() as ctx:
        def sb(name, shape, dt=F32):
            return ctx.enter_context(nc.sbuf_tensor(name, shape, dt))

        def sem(name):
            return ctx.enter_context(nc.semaphore(name))

        early_at, n_early = columns(EARLY)
        late_at, n_late = columns(LATE)
        row_at, n_rows = columns(ROWS)
        early = sb("early", [128, n_early])
        late = sb("late", [128, n_late])
        rows = sb("rows", [128, n_rows])

        def w(name, rows_=128, a=0, b=None):
            tile, at = (early, early_at) if name in early_at else (late, late_at)
            start, n = at[name]
            return tile[0:rows_, start + a:start + (n if b is None else b)]

        def row(name, a=0, b=None, p=128):
            start, n = row_at[name]
            return rows[0:p, start + a:start + (n if b is None else b)]

        ident = w("ident")
        ctxT = sb("ctxT", [CA, B * SK])
        ctxk = sb("ctxk", [128, NC, CA])
        f0_w1 = sb("f0_w1", [128, E, 256])
        f0_w2 = sb("f0_w2", [128, E, 256])
        f1_w13 = sb("f1_w13", [128, E, 512])
        f1_w2 = sb("f1_w2", [128, E, 256])
        f2_wg = sb("f2_wg", [128, E, 384])
        f2_wu = sb("f2_wu", [128, E, 384])
        f2_wd = sb("f2_wd", [128, E, 384])
        x2_wqo = sb("x2_wqo", [128, 2, 1024])
        x2_wq = x2_wqo[:, 0, :]
        x2_wkT = sb("x2_wkT", [128, 8, DC])
        x2_v = sb("x2_v", [128, H2 * D2])
        x2_wv = x2_v[0:DC, :]
        x2_wo = x2_wqo[:, 1, :].rearrange("p (a n) -> p a n", a=8)

        f3_wg = f1_w13
        f3_wd = [f0_w1[:, :, :].rearrange("p (e a) f -> p e (a f)", a=2), f0_w2[:, :, :].rearrange("p (e a) f -> p e (a f)", a=2)]
        f3_wu = [f1_w2[:, :, :].rearrange("p (e a) f -> p e (a f)", a=2), x2_wqo[:, :, :].rearrange("p a (e f) -> p (a e) f", e=2)]

        x = sb("x", [128, D])
        xb = sb("xb", [128, D])
        xn = sb("xn", [128, D])
        xnT = sb("xnT", [128, T])
        stats = sb("stats", [128, 6])
        mv = sb("mv", [128, 2])
        nw = sb("nw", [128, 8])
        z2 = sb("z2", [128, D])

        big_a = sb("big_a", [128, 2048])
        big_b = sb("big_b", [128, 2048])
        big_c = sb("big_c", [128, 2048])
        kv3 = sb("kv3", [128, NC, 256])
        q2bd = kv3[:, 0:8, :].rearrange("p a (h t) -> p a h t", h=2)
        o2T = kv3[:, 8:12, :].rearrange("p a (h t) -> p (a h) t", h=2)
        k3T = sb("k3T", [128, B * SK])
        clipped = k3T[:, 0:1024].rearrange("p (a k) -> p a k", a=2)
        guard_out = k3T[:, 1024:1536]
        s_sb = k3T[:, 1024:1536].rearrange("p (h t) -> p h t", h=H)
        pT_sb = k3T[:, 1536:2048].rearrange("p (h t) -> p h t", h=H)
        probs = sb("probs", [128, 2, SK])
        probsT = sb("probsT", [128, 2, SK])
        qT = sb("qT", [128, T])
        negmax = sb("negmax", [128, NG])
        nan_sum = sb("nan_sum", [128, NG])
        nan_hit = sb("nan_hit", [128, NG])
        nan_any = sb("nan_any", [128, 1])
        mean_col = sb("mean_col", [128, 1])
        mean_cT = sb("mean_cT", [CA, B])
        mean_vT = sb("mean_vT", [128, B])
        rden = sb("rden", [128, NG])
        pcn = sb("pcn", [128, 2, CA])
        om = sb("om", [128, NG, 32])
        oT = sb("oT", [128, T])

        hid, tg = probs, probsT
        act_a = om[:, :, :].rearrange("p g n -> p (g n)")
        lg = sb("lg", [128, 8])
        sc8 = sb("sc8", [128, 8])
        top8 = sb("top8", [128, 8])
        idx8 = sb("idx8", [128, 8], U32)
        idxf = sb("idxf", [128, 8])
        oh = sb("oh", [128, 2, 8])
        cw = sb("cw", [128, 8])
        cwT = sb("cwT", [8, T])
        rt = sb("rt", [128, 8])
        grp8 = sb("grp8", [128, 8])

        vaug = sb("vaug", [128, H, DH + 1])
        qk_ = sb("qk_", [128, 4, T])
        ktA = sb("ktA", [128, T])
        den16 = sb("den16", [128, H])
        o_tok = sb("o_tok", [128, D])

        u_half = sb("u_half", [128, 512])
        h2T = ktA
        gates = qk_[:, 0, :].rearrange("p (g b) -> p g b", g=4)
        cst = qk_[:, 1:3, :].rearrange("p a (g b) -> p (a g) b", g=4)

        mask_u8 = sb("mask_u8", [128, SK], U8)
        mask_add = x2_v[:, 0:SK]
        st3 = sb("st3", [128, NC, 6])
        mv3 = sb("mv3", [128, NC, 2])
        n3 = sb("n3", [128, 5, 2 * NC])
        qkv3 = qk_[:, 0:3, :].rearrange("p a t -> p (a t)")
        kl3T = qk_[:, 3, :]
        q3bd = x2_v[:, SK + 2 * T:SK + 4 * T].rearrange("p (h t) -> p h t", h=2)
        d3 = sb("d3", [128, 8])

        convp = x2_wkT[:, :, :].rearrange("p a c -> p (a c)")[:, 0:4 * B * SP].rearrange("p (j b l) -> p j b l", j=4, b=B)
        cbd = x2_v[:, SK:SK + 2 * T].rearrange("p (d t) -> p d t", d=2)
        dts = sb("dts", [128, 6, 8])

        banks = [ctx.enter_context(nc.psum_tensor(f"bank{i}", [128, 512], F32)) for i in range(8)]

        load = {n: sem("load_" + n) for n in
                ("early", "rows", "x", "ctxT", "ctxk", "late", "f0", "f1", "f2", "x2", "f3up", "f3gate", "f3down", "mask")}
        pool_set = sem("pool_set")
        pool_step = sem("pool_step")
        dve_step = sem("dve_step")
        act_step = sem("act_step")
        out_stored = sem("out_stored")

        xn_ready = sem("xn_ready")
        xnT_in_psum = sem("xnT_in_psum")
        xnT_ready = sem("xnT_ready")
        x_ready = sem("x_ready")
        y_full = sem("y_full")

        q_in_psum = sem("q_in_psum")
        qbd_ready = sem("qbd_ready")
        qw_in_psum = sem("qw_in_psum")
        qw_act = sem("qw_act")
        qw_dve = sem("qw_dve")
        scores_in_psum = sem("scores_in_psum")
        negmax_ready = sem("negmax_ready")
        clip_ready = sem("clip_ready")
        guard_read = sem("guard_read")
        probs_ready = sem("probs_ready")
        probsT_in_psum = sem("probsT_in_psum")
        probsT_ready = sem("probsT_ready")
        pc_in_psum = sem("pc_in_psum")
        pcn_ready = sem("pcn_ready")
        pcnT_in_psum = sem("pcnT_in_psum")
        pcnT_ready = sem("pcnT_ready")
        o_in_psum = sem("o_in_psum")
        om_ready = sem("om_ready")
        oT_in_psum = sem("oT_in_psum")
        oT_ready = sem("oT_ready")
        nan_ready = sem("nan_ready")
        nan_in_psum = sem("nan_in_psum")
        mean_in_psum = sem("mean_in_psum")
        mean_ready = sem("mean_ready")

        logits_in_psum = sem("logits_in_psum")
        lneg_ready = sem("lneg_ready")
        lexp_ready = sem("lexp_ready")
        gate_in_psum = sem("gate_in_psum")
        up_in_psum = sem("up_in_psum")
        tanh_ready = sem("tanh_ready")
        hid_ready = sem("hid_ready")
        hid_act = sem("hid_act")
        y_in_psum = sem("y_in_psum")
        y_added = sem("y_added")
        cw_ready = sem("cw_ready")
        cwT_in_psum = sem("cwT_in_psum")
        cwT_ready = sem("cwT_ready")
        mix_pe = sem("mix_pe")
        mix_dve = sem("mix_dve")
        mix_act = sem("mix_act")
        c3_pe = sem("c3_pe")
        c3_dve = sem("c3_dve")
        c3_act = sem("c3_act")

        block = ctx.enter_context(nc.Block())

        class Steps:

            def __init__(self, engine, semaphore):
                self.engine, self.semaphore, self.n = engine, semaphore, 0

            def done(self, ins):
                ins.then_inc(self.semaphore, 1)
                self.n += 1
                self.engine.wait_ge(self.semaphore, self.n)

        class Count:

            def __init__(self):
                self.n = 0

        @block.sync
        def _(sp):
            sp.dma_start(early[:, :], dram["early"]).then_inc(load["early"], 16)
            sp.dma_start(x[:, :], dram["x"]).then_inc(load["x"], 16)
            sp.dma_start(ctxT[0:DC, :], dram["ctxT"]).then_inc(load["ctxT"], 16)
            sp.dma_start(ctxk[:, :, 0:DC], dram["ctxk"]).then_inc(load["ctxk"], 16)
            sp.dma_start(rows[:, :], dram["rows"].partition_broadcast(128)).then_inc(load["rows"], 16)
            sp.dma_start(late[:, :], dram["late"]).then_inc(load["late"], 16)
            sp.dma_start(f0_w1[:, :, :], dram["f0_w1"]).then_inc(load["f0"], 16)
            sp.dma_start(f0_w2[:, :, :], dram["f0_w2"]).then_inc(load["f0"], 16)
            sp.dma_start(f1_w13[:, :, :], dram["f1_w13"]).then_inc(load["f1"], 16)
            sp.dma_start(f1_w2[:, :, :], dram["f1_w2"]).then_inc(load["f1"], 16)
            for tile, name in ((x2_wq, "x2_wq"), (x2_wkT[:, :, :], "x2_wkT"), (x2_wv, "x2_wv"), (x2_wo, "x2_wo")):
                sp.dma_start(tile, dram[name]).then_inc(load["x2"], 16)
            for tile, name in ((f2_wg, "f2_wg"), (f2_wu, "f2_wu"), (f2_wd, "f2_wd")):
                sp.dma_start(tile[:, :, :], dram[name]).then_inc(load["f2"], 16)
            for b in range(B):
                sp.dma_start(mask_u8[b * S:(b + 1) * S, :],
                             dram["mask"][b:b + 1, :].partition_broadcast(S)).then_inc(load["mask"], 16)
            if STAGES >= 3:
                sp.wait_ge(y_in_psum, E)
                for i in range(2):
                    sp.dma_start(f3_wd[i], dram["f3_wd"][:, 4 * i:4 * i + 4, :]).then_inc(load["f3down"], 16)
            if STAGES >= 6:
                sp.wait_ge(y_in_psum, 2 * E)
                sp.dma_start(f3_wg[:, :, :], dram["f3_wg"]).then_inc(load["f3gate"], 16)
                sp.dma_start(f3_wu[0], dram["f3_wu"][:, 0:4, :]).then_inc(load["f3up"], 16)
            if STAGES >= 7:
                sp.wait_ge(y_full, 3)
                sp.dma_start(f3_wu[1], dram["f3_wu"][:, 4:8, :]).then_inc(load["f3up"], 16)
            sp.wait_ge(x_ready, STAGES)
            sp.dma_start(dram["out"], x[:, :]).then_inc(out_stored, 16)
            sp.wait_ge(out_stored, 16)

        @block.gpsimd
        def _(pool):
            pool.memset(ctxT[DC:CA, :], 1.0).then_inc(pool_set, 1)
            pool.wait_ge(pool_set, 1)
            pool.memset(ctxk[:, :, DC:CA], 1.0).then_inc(pool_set, 1)
            pool.wait_ge(pool_set, 2)
            pool.memset(mean_col[:, :], 1.0 / SK).then_inc(pool_set, 1)
            pool.wait_ge(pool_set, 3)
            pool.memset(vaug[:, :, DH:DH + 1], 1.0).then_inc(pool_set, 1)
            pool.wait_ge(pool_set, 4)
            pool.memset(grp8[:, :], -1.0).then_inc(pool_set, 1)
            pool.wait_ge(pool_set, 5)
            pool.memset(q2bd[:, :, :, :], 0.0).then_inc(pool_set, 1)
            pool.wait_ge(pool_set, 6)
            pool.wait_ge(load["late"], 16)
            pool.tensor_scalar(u_half[:, :], w("lstm_u"), 0.5, None, ALU.mult).then_inc(pool_set, 1)
            pool.wait_ge(pool_set, 7)
            if STAGES >= 7:
                pool.wait_ge(load["mask"], 64)
                pool.wait_ge(y_full, 3)
                pool.tensor_scalar(mask_add, mask_u8[:, :], 1.0, BIG, ALU.subtract, ALU.mult).then_inc(pool_set, 1)
                pool.wait_ge(pool_set, 8)
                pool.memset(convp, 0.0).then_inc(pool_set, 1)
                pool.wait_ge(pool_set, 9)
                pool.memset(cbd, 0.0).then_inc(pool_set, 1)
                pool.wait_ge(pool_set, 10)
                pool.memset(q3bd, 0.0).then_inc(pool_set, 1)
                pool.wait_ge(pool_set, 11)

        SET_Q, SET_U, SET_L3 = 6, 7, 11

        @block.scalar
        def _(act):
            st = Steps(act, act_step)

            def turn_norm(n):
                act.wait_ge(xnT_in_psum, n + 1)
                act.copy(xnT[:, :], banks[7][:, 0:T]).then_inc(xnT_ready, 1)

            def context_attention(layer):
                K = CA if layer < 2 else DC
                if layer == 2:
                    act.wait_ge(q_in_psum, 3)
                    act.wait_ge(pool_set, SET_Q)
                    for half in range(2):
                        p = slice(64 * half, 64 * half + 64)
                        ins = act.activation(q2bd[p, 0:4, half, :], banks[0][p, :].rearrange("p (a t) -> p a t", a=4),
                                             ACT.Copy, scale=D2 ** -0.5)
                    ins.then_inc(qw_act, 1)
                    act.wait_ge(qw_in_psum, 8 + 4)
                for i in (0, 2):
                    act.wait_ge(qw_in_psum, 4 * layer + i + 1)
                    if layer < 2:
                        act.copy(big_b[0:K, i * 512:i * 512 + 512], banks[i][0:K, :]).then_inc(qw_act, 1)
                    else:
                        out = big_b[0:K, :].rearrange("p (b g h q) -> p g h b q", b=B, g=HG, h=4)[:, i]
                        act.copy(out, banks[2 + i][0:K, :].rearrange("p (h b q) -> p h b q", h=4, b=B)).then_inc(qw_act, 1)
                g0 = NG * layer
                for i in range(NG + 4):
                    if i < NG:
                        g = g0 + i
                        if layer == 0:
                            act.wait_ge(clip_ready, g + 1)
                            if g >= 1:
                                act.wait_ge(guard_read, g)
                            act.activation(guard_out[:, :], banks[i % 2][:, :], ACT.Tanh,
                                           accum_out=nan_sum[:, i:i + 1]).then_inc(guard_read, 1)
                        act.wait_ge(negmax_ready, g + 1)
                        if g >= 2:
                            act.wait_ge(probsT_in_psum, g - 1)
                        src = clipped[:, i % 2, :] if layer == 0 else banks[i % 2][:, :]
                        act.activation(probs[:, i % 2, :], src, ACT.Exp,
                                       bias=negmax[:, i:i + 1]).then_inc(probs_ready, 1)
                    if layer == 0 and 1 <= i <= NG:
                        j = i - 1
                        act.wait_ge(probsT_in_psum, g0 + j + 1)
                        if j >= 2:
                            act.wait_ge(pc_in_psum, g0 + j - 1)
                        act.copy(probsT[:, j % 2, :], banks[2 + j % 2][:, :]).then_inc(probsT_ready, 1)
                    j = i - 4
                    if j >= 0 and j % 4 == 3:
                        b = j // 4
                        act.wait_ge(pcnT_in_psum, g0 + j + 1)
                        act.copy(big_c[0:CA, b * 512:b * 512 + 512],
                                 banks[6 + b % 2][0:CA, :]).then_inc(pcnT_ready, 1)
                if layer == 2:
                    act.wait_ge(o_in_psum, 3)
                    act.copy(o2T[:, 0:4, :], banks[0][:, :].rearrange("p (a t) -> p a t", a=4)).then_inc(qw_act, 1)

            def feed_forward(layer):
                e0 = E * layer
                C = FFN_CHUNKS[layer] * 128
                k = {0: 0, 1: 1, 3: 2}.get(layer)
                for e in range(E):
                    n = e0 + e
                    if e == 1 and k is not None:
                        act.wait_ge(lneg_ready, k + 1)
                        act.activation(sc8[:, :], lg[:, :], ACT.Exp, bias=rt[:, 0:1],
                                       accum_out=rt[:, 1:2]).then_inc(lexp_ready, 1)
                    if layer == 0:
                        act.wait_ge(gate_in_psum, n + 1)
                        if e >= 2:
                            act.wait_ge(y_in_psum, n - 1)
                        act.activation(hid[:, e % 2, 0:T], banks[e % 2][:, 0:T], ACT.Relu,
                                       bias=w("f0_b1", 128, 2 * e, 2 * e + 1)).then_inc(hid_act, 1)
                    else:
                        act.wait_ge(gate_in_psum, n + 1)
                        if e >= 2:
                            act.wait_ge(hid_ready, n - 1)
                        act.activation(tg[:, e % 2, 0:C], banks[e % 2][:, 0:C], ACT.Tanh, scale=0.5).then_inc(tanh_ready, 1)

            def linear_attention():
                act.wait_ge(mix_pe, 1)
                act.copy(vaug[:, :, 0:DH], banks[2][:, 0:D].rearrange("p (h d) -> p h d", h=H)).then_inc(mix_act, 1)

            def causal_attention():
                act.wait_ge(mix_pe, 8 + 1)
                act.copy(o_tok[:, :], banks[4][:, 0:D]).then_inc(mix_act, 1)
                act.wait_ge(mix_dve, 8 + 3)
                act.activation(s_sb[:, :, :], s_sb[:, :, :], ACT.Exp).then_inc(mix_act, 1)

            def lstm():
                for t in range(B):
                    act.wait_ge(mix_pe, 13 + 1 + t)
                    g = banks[0][:, t * 128:(t + 1) * 128]
                    act.activation(gates[:, 0:3, :], g[:, 0:96].rearrange("p (g b) -> p g b", g=3), ACT.Tanh, scale=0.5)
                    act.activation(gates[:, 3, :], g[:, 96:128], ACT.Tanh).then_inc(mix_act, 1)
                    act.wait_ge(mix_dve, 13 + 2 * t + 1)
                    act.activation(cst[:, 3, :], cst[:, 2, :], ACT.Tanh, scale=0.5).then_inc(mix_act, 1)

            def context3():
                act.wait_ge(load["late"], 16)
                for i in range(4):
                    act.wait_ge(c3_pe, i + 1)
                    act.activation(big_c[0:DC, i * 512:i * 512 + 512], banks[i][0:DC, :], ACT.Identity,
                                   bias=w("x3_b", DC), scale=w("x3_g", DC)).then_inc(c3_act, 1)
                for i in range(8):
                    act.wait_ge(c3_pe, 4 + i + 1)
                    act.copy(kv3[:, 2 * i:2 * i + 2, :],
                             banks[4 + i % 4][:, :].rearrange("p (a n) -> p a n", a=2)).then_inc(c3_act, 1)
                for i in range(4):
                    act.wait_ge(c3_pe, 12 + i + 1)
                    act.copy(k3T[:, i * 512:i * 512 + 512], banks[i][:, :]).then_inc(c3_act, 1)

            def cross3():
                act.wait_ge(c3_pe, 16 + 1)
                act.copy(qkv3, banks[0][:, 0:384]).then_inc(c3_act, 1)
                act.wait_ge(c3_dve, 5 + 5)
                for h in range(H3):
                    act.activation(big_a[:, h * 640:h * 640 + 640], big_a[:, h * 640:h * 640 + 640], ACT.Exp,
                                   bias=d3[:, h:h + 1], accum_out=d3[:, 2 + h:3 + h]).then_inc(c3_act, 1)
                act.wait_ge(c3_pe, 16 + 4)
                act.copy(big_b[:, 0:512], banks[0][:, :]).then_inc(c3_act, 1)
                act.wait_ge(c3_pe, 16 + 6)
                act.copy(big_b[:, 1024:1280], banks[2][:, 0:256]).then_inc(c3_act, 1)

            def state_space():
                a0 = ACT0
                act.wait_ge(mix_dve, DV0 + 1)
                st.done(act.activation(dts[:, 1, :], dts[:, 0, :], ACT.Abs))
                act.activation(dts[:, 1, :], dts[:, 1, :], ACT.Exp, scale=-1.0).then_inc(mix_act, 1)
                act.activation(dts[:, 5, 0:4], row("alog"), ACT.Exp).then_inc(mix_act, 1)
                act.wait_ge(mix_act, a0 + 1)
                act.activation(dts[:, 2, :], dts[:, 1, :], ACT.Ln, bias=1.0).then_inc(mix_act, 1)
                act.wait_ge(mix_pe, PE0 + 2)
                act.activation(big_c[:, 0:256], banks[1][:, 0:256], ACT.Tanh, scale=0.5).then_inc(mix_act, 1)
                act.wait_ge(mix_dve, DV0 + 3)
                act.activation(big_b[:, 512:1024], big_b[:, 0:512], ACT.Tanh).then_inc(mix_act, 1)
                for i in range(2):
                    act.wait_ge(mix_pe, PE0 + 3 + i)
                    act.activation(big_a[:, 1024 + 512 * i:1536 + 512 * i], banks[2 + i][:, :], ACT.Exp,
                                   scale=-1.0).then_inc(mix_act, 1)

            ACT0, DV0, PE0 = 3 + 2 * B, 13 + 2 * B, 13 + B + 1

            turn_norm(0)
            context_attention(0)
            if STAGES >= 2:
                turn_norm(1); linear_attention()
            if STAGES >= 3:
                turn_norm(2); feed_forward(0)
            if STAGES >= 4:
                turn_norm(3); context_attention(1)
            if STAGES >= 5:
                turn_norm(4); causal_attention()
            if STAGES >= 6:
                turn_norm(5); feed_forward(1)
            if STAGES >= 7:
                turn_norm(6); context_attention(2)
            if STAGES >= 8:
                turn_norm(7); lstm()
            if STAGES >= 9:
                turn_norm(8); feed_forward(2)
            if STAGES >= 10:
                context3()
                cross3()
            if STAGES >= 11:
                turn_norm(9); state_space()
            if STAGES >= 12:
                turn_norm(10); feed_forward(3)

        @block.tensor
        def _(pe):
            def turn_norm(n):
                pe.wait_ge(xn_ready, n + 1)
                pe.transpose(banks[7][:, 0:T], xn[:, :], ident).then_inc(xnT_in_psum, 1)
                pe.wait_ge(xnT_ready, n + 1)

            def context_attention(layer):
                K = CA if layer < 2 else DC
                g0 = NG * layer
                if layer < 2:
                    wq, wkT, wv, wo = (w(f"{n}{layer}") for n in ("wq", "wkT", "wv", "wo"))
                    pe.matmul(banks[6][:, 0:T], wq, xnT[:, :], start=True, stop=True).then_inc(q_in_psum, 1)
                    if layer == 0:
                        pe.wait_ge(load["ctxk"], 16)
                        pe.wait_ge(pool_set, 3)
                        for b in range(B):
                            for c in range(CK):
                                ins = pe.matmul(banks[5][0:CA, b:b + 1], ctxk[:, b * CK + c, :], mean_col[:, :],
                                                start=c == 0, stop=c == CK - 1)
                        ins.then_inc(mean_in_psum, 1)
                        pe.wait_ge(mean_ready, 1)
                        pe.matmul(banks[5][:, 8:8 + B], w("wv0", CA), mean_cT[:, :], start=True, stop=True).then_inc(mean_in_psum, 1)
                    pe.wait_ge(qbd_ready, layer + 1)
                    for b in range(B):
                        pe.matmul(banks[b][0:CA, :], wkT, big_a[:, b * 512:b * 512 + 512],
                                  start=True, stop=True).then_inc(qw_in_psum, 1)
                else:
                    pe.wait_ge(load["x2"], 64)
                    for p in range(8):
                        ins = pe.matmul(banks[p // 4][:, (p % 4) * 128:(p % 4) * 128 + 128], x2_wq[:, p * 128:(p + 1) * 128],
                                        xnT[:, :], start=True, stop=True)
                    ins.then_inc(q_in_psum, 1)
                    pe.wait_ge(qw_act, 4 + 1)
                    pe.wait_ge(qw_dve, 4 + 1)
                    for p in range(8):
                        ins = pe.matmul(banks[2 + p // 2][0:DC, (p % 2) * 256:(p % 2) * 256 + 256], x2_wkT[:, p, :],
                                        q2bd[:, p, :, :], start=True, stop=True)
                        if p % 2:
                            ins.then_inc(qw_in_psum, 1)

                def scores(i):
                    b, hg = i // HG, i % HG
                    if layer < 2:
                        if hg == 0:
                            pe.wait_ge(qw_act, 2 * layer + (1 if b < 2 and 0 else 2))
                            pe.wait_ge(qw_dve, 2 * layer + 2)
                    elif i == 0:
                        pe.wait_ge(qw_act, 4 + 3)
                        pe.wait_ge(qw_dve, 4 + 3)
                    if i >= 2:
                        if layer == 0:
                            pe.wait_ge(guard_read, g0 + i - 1)
                        else:
                            pe.wait_ge(probs_ready, g0 + i - 1)
                    pe.matmul(banks[i % 2][:, :], big_b[0:K, i * 128:(i + 1) * 128], ctxT[0:K, b * SK:(b + 1) * SK],
                              start=True, stop=True).then_inc(scores_in_psum, 1)

                def turn_probs(i):
                    pe.wait_ge(probs_ready, g0 + i + 1)
                    if i >= 2:
                        pe.wait_ge(probsT_ready, g0 + i - 1)
                    for c in range(CK):
                        ins = pe.transpose(banks[2 + i % 2][:, c * 128:(c + 1) * 128], probs[:, i % 2, c * 128:(c + 1) * 128], ident)
                    ins.then_inc(probsT_in_psum, 1)

                def weighted_context(i):
                    pe.wait_ge(probsT_ready, g0 + i + 1)
                    if i >= 2:
                        pe.wait_ge(pcn_ready, g0 + i - 1)
                    for c in range(CK):
                        ins = pe.matmul(banks[4 + i % 2][:, 0:CA], probsT[:, i % 2, c * 128:(c + 1) * 128],
                                        ctxk[:, (i // HG) * CK + c, :], start=c == 0, stop=c == CK - 1)
                    ins.then_inc(pc_in_psum, 1)

                def turn_weighted(i):
                    pe.wait_ge(pcn_ready, g0 + i + 1)
                    b = i // HG
                    if i % HG == 0 and b >= 2:
                        pe.wait_ge(pcnT_ready, B * layer + b - 1)
                    pe.transpose(banks[6 + b % 2][0:CA, (i % HG) * 128:(i % HG) * 128 + 128],
                                 pcn[:, i % 2, :], ident).then_inc(pcnT_in_psum, 1)

                for i in range(NG + 3):
                    if i < NG:
                        scores(i)
                    if 1 <= i <= NG:
                        turn_probs(i - 1)
                    if 2 <= i <= NG + 1:
                        weighted_context(i - 2)
                    if i >= 3:
                        turn_weighted(i - 3)
                pe.wait_ge(pcnT_ready, B * (layer + 1))
                if layer == 0:
                    pe.wait_ge(nan_ready, 1)
                    pe.matmul(banks[5][:, 0:NG], w("ones"), nan_hit[:, :], start=True, stop=True).then_inc(nan_in_psum, 1)
                if layer < 2:
                    for i in range(NG):
                        hg = i % HG
                        ins = pe.matmul(banks[0][:, i * 32:(i + 1) * 32], big_c[0:CA, i * 128:(i + 1) * 128],
                                        w(f"wv{layer}", CA, hg * 32, hg * 32 + 32), start=True, stop=True)
                    ins.then_inc(o_in_psum, 1)
                    pe.wait_ge(om_ready, layer + 1)
                    for b in range(B):
                        ins = pe.matmul(banks[1][:, b * S:(b + 1) * S], om[:, b * HG:(b + 1) * HG, :], w("fold"),
                                        start=True, stop=True)
                    ins.then_inc(oT_in_psum, 1)
                    pe.wait_ge(oT_ready, layer + 1)
                    pe.matmul(banks[2][:, 0:D], oT[:, :], wo, start=True, stop=True).then_inc(y_full, 1)
                else:
                    pc = big_c[0:DC, :].rearrange("p (b h q) -> p h b q", b=B, h=H2)
                    for h in range(H2):
                        p, half = h // 2, h % 2
                        ins = pe.matmul(banks[p // 4][64 * half:64 * half + 64, (p % 4) * 128:(p % 4) * 128 + 128],
                                        x2_wv[:, h * D2:(h + 1) * D2], pc[:, h], start=True, stop=True)
                    ins.then_inc(o_in_psum, 1)
                    pe.wait_ge(qw_act, 4 + 4)
                    pe.wait_ge(qw_dve, 4 + 4)
                    for p in range(8):
                        ins = pe.matmul(banks[2][:, 0:D], o2T[:, p, :], x2_wo[:, p, :], start=p == 0, stop=p == 7)
                    ins.then_inc(y_full, 1)

            def feed_forward(layer):
                e0 = E * layer
                C = FFN_CHUNKS[layer]
                pe.wait_ge(load["late"], 16)
                pe.matmul(banks[7][:, 256:264], xnT[:, :], w(f"f{layer}_wr"), start=True, stop=True).then_inc(logits_in_psum, 1)
                if layer == 0:
                    pe.wait_ge(load["f0"], 32)
                elif layer == 1:
                    pe.wait_ge(load["f1"], 32)
                elif layer == 2:
                    pe.wait_ge(load["f2"], 48)
                else:
                    pe.wait_ge(load["f3up"], 32)
                    pe.wait_ge(load["f3gate"], 16)
                    pe.wait_ge(load["f3down"], 32)

                def gate_w(e, c):
                    if layer == 1:
                        return f1_w13[:, e, c * 128:(c + 1) * 128]
                    return (f2_wg if layer == 2 else f3_wg)[:, e, c * 128:(c + 1) * 128]

                def up_w(e, c):
                    if layer == 1:
                        return f1_w13[:, e, 256 + c * 128:256 + (c + 1) * 128]
                    return (f2_wu[:, e, :] if layer == 2 else f3_wu[e // 4][:, e % 4, :])[:, c * 128:(c + 1) * 128]

                def down_w(e, c):
                    if layer == 3:
                        return f3_wd[e // 4][:, e % 4, c * 128:(c + 1) * 128]
                    return {0: f0_w2, 1: f1_w2, 2: f2_wd}[layer][:, e, c * 128:(c + 1) * 128]

                def up(e):
                    n = e0 + e
                    if e >= 2:
                        pe.wait_ge(hid_ready, n - 1)
                        if layer == 0:
                            pe.wait_ge(hid_act, n - 1)
                    if layer == 0:
                        pe.matmul(banks[e % 2][:, 0:T], f0_w1[:, e, 0:128], xnT[:, :], start=True, stop=True).then_inc(gate_in_psum, 1)
                        pe.matmul(banks[2 + e % 2][:, 0:T], f0_w1[:, e, 128:256], xnT[:, :], start=True, stop=True).then_inc(up_in_psum, 1)
                        return
                    for wt, bank, s in ((gate_w, banks[e % 2], gate_in_psum), (up_w, banks[2 + e % 2], up_in_psum)):
                        for c in range(C):
                            ins = pe.matmul(bank[:, c * T:(c + 1) * T], wt(e, c), xnT[:, :], start=True, stop=True)
                        ins.then_inc(s, 1)

                def down(e):
                    n = e0 + e
                    pe.wait_ge(hid_ready, n + 1)
                    if layer == 0:
                        pe.wait_ge(hid_act, n + 1)
                    if e >= 2:
                        pe.wait_ge(y_added, n - 1)
                    for c in range(C):
                        ins = pe.matmul(banks[4 + e % 2][:, 0:D], hid[:, e % 2, c * T:(c + 1) * T], down_w(e, c),
                                        start=c == 0, stop=c == C - 1)
                    ins.then_inc(y_in_psum, 1)

                for e in range(E + 1):
                    if e < E:
                        up(e)
                    if layer == 3 and e == 1:
                        pe.wait_ge(cw_ready, 2)
                        pe.matmul(banks[6][:, 0:16], w("cum"), oh[:, :, :], start=True, stop=True).then_inc(cwT_in_psum, 1)
                    if e >= 1:
                        down(e - 1)
                if layer == 0:
                    pe.wait_ge(cw_ready, 1)
                    pe.transpose(banks[6][0:8, 0:T], cw[:, :], ident).then_inc(cwT_in_psum, 1)
                    pe.wait_ge(cwT_ready, 1)
                    pe.matmul(banks[6][:, 256:256 + D], cwT[:, :], w("f0_b2", 8), start=True, stop=True).then_inc(cwT_in_psum, 1)

            def linear_attention():
                pe.wait_ge(load["late"], 16)
                pe.matmul(banks[0][:, 0:T], w("a_wq"), xnT[:, :], start=True, stop=True)
                pe.matmul(banks[1][:, 0:T], w("a_wk"), xnT[:, :], start=True, stop=True)
                pe.matmul(banks[2][:, 0:D], xnT[:, :], w("a_wv"), start=True, stop=True).then_inc(mix_pe, 1)
                pe.wait_ge(mix_dve, 1)
                for i in range(4):
                    pe.matmul(banks[3 + i][:, :], ktA[:, :], big_a[:, i * 512:i * 512 + 512],
                              start=True, stop=True).then_inc(mix_pe, 1)
                pe.wait_ge(mix_act, 1)
                pe.wait_ge(pool_set, SET_Q)
                for i in range(4):
                    pe.wait_ge(mix_dve, 2 + i)
                    for h in range(4 * i, 4 * i + 4):
                        ins = pe.matmul(banks[0][:, h * 9:h * 9 + 9], big_b[:, h * T:(h + 1) * T], vaug[:, h, :],
                                        start=True, stop=True)
                ins.then_inc(mix_pe, 1)
                pe.wait_ge(mix_dve, 6)
                pe.transpose(banks[1][:, 0:T], o_tok[:, :], ident).then_inc(mix_pe, 1)
                pe.wait_ge(mix_dve, 7)
                pe.matmul(banks[2][:, 0:D], oT[:, :], w("a_wo"), start=True, stop=True).then_inc(mix_pe, 1)

            def causal_attention():
                for i, (name, a) in enumerate((("r_wq", 0), ("r_wq", 128), ("r_wk", 0), ("r_wk", 128))):
                    pe.matmul(banks[i][:, 0:T], w(name, 128, a, a + 128), xnT[:, :], start=True, stop=True)
                pe.matmul(banks[4][:, 0:D], xnT[:, :], w("r_wv"), start=True, stop=True).then_inc(mix_pe, 1)
                pe.wait_ge(mix_dve, 8 + 1)
                for b in range(B):
                    ins = pe.matmul(banks[5][b * S:(b + 1) * S, :], qT[:, b * S:(b + 1) * S],
                                    big_a[:, b * 512:(b + 1) * 512], start=True, stop=True)
                ins.then_inc(mix_pe, 1)
                pe.wait_ge(mix_dve, 8 + 4)
                pe.wait_ge(mix_act, 2)
                for h in range(H):
                    ins = pe.matmul(banks[0][:, h * DH:(h + 1) * DH], big_b[:, h * T:(h + 1) * T],
                                    o_tok[:, h * DH:(h + 1) * DH], start=True, stop=True)
                ins.then_inc(mix_pe, 1)
                pe.wait_ge(mix_dve, 8 + 5)
                pe.transpose(banks[1][:, 0:T], z2[:, :], ident).then_inc(mix_pe, 1)
                pe.wait_ge(oT_ready, 3)
                pe.matmul(banks[2][:, 0:D], oT[:, :], w("r_wo"), start=True, stop=True).then_inc(mix_pe, 1)

            def lstm():
                pe.wait_ge(pool_set, SET_U)
                pe.wait_ge(load["rows"], 16)
                g = banks[0][:, :].rearrange("p (t g b) -> p g t b", t=B, g=4)
                for k in range(4):
                    pe.matmul(g[:, k], row("lstm_b", k * 128, k * 128 + 128, 1), w("ones", 1),
                              start=k == 0, stop=False, skip_group_check=True)
                for k in range(4):
                    ins = pe.matmul(g[:, k], w("lstm_w", 128, k * 128, k * 128 + 128), xnT[:, :],
                                    start=False, stop=k == 3, skip_group_check=True)
                ins.then_inc(mix_pe, 1)
                for t in range(1, B):
                    pe.wait_ge(mix_dve, 13 + 2 * t)
                    for k in range(4):
                        ins = pe.matmul(banks[0][:, t * 128 + k * S:t * 128 + (k + 1) * S], u_half[:, k * 128:(k + 1) * 128],
                                        h2T[:, (t - 1) * S:t * S], start=False, stop=True, skip_group_check=True)
                    ins.then_inc(mix_pe, 1)
                pe.wait_ge(mix_dve, 13 + 2 * B)
                pe.transpose(banks[1][:, 0:D], h2T[:, :], ident).then_inc(mix_pe, 1)

            def context3():
                for i in range(4):
                    pe.wait_ge(c3_dve, 1)
                    for c in range(4):
                        ins = pe.transpose(banks[i][0:DC, c * 128:(c + 1) * 128], big_a[:, (4 * i + c) * DC:(4 * i + c + 1) * DC], ident)
                    ins.then_inc(c3_pe, 1)
                for i in range(8):
                    pe.wait_ge(c3_act, i // 2 + 1 if i < 4 else 4 + i - 3)
                    if i >= 4:
                        pe.wait_ge(c3_act, 4 + i - 3)
                    for c in range(2):
                        k = 2 * i + c
                        ins = pe.matmul(banks[4 + i % 4][:, c * 256:(c + 1) * 256], big_c[0:DC, k * 128:(k + 1) * 128],
                                        w("x3_wkv", DC), start=True, stop=True)
                    ins.then_inc(c3_pe, 1)
                pe.wait_ge(c3_dve, 2)
                for i in range(4):
                    for c in range(4):
                        ins = pe.transpose(banks[i][:, c * 128:(c + 1) * 128], kv3[:, 4 * i + c, 0:128], ident)
                    ins.then_inc(c3_pe, 1)

            def cross3():
                pe.wait_ge(c3_dve, 3)
                pe.transpose(banks[7][:, 0:T], z2[:, :], ident).then_inc(q_in_psum, 1)
                pe.wait_ge(c3_dve, 4)
                pe.wait_ge(c3_act, 16)
                pe.matmul(banks[0][:, 0:384], xnT[:, :], w("x3_wqkv"), start=True, stop=True).then_inc(c3_pe, 1)
                pe.wait_ge(c3_dve, 5)
                pe.transpose(banks[1][:, 0:T], xn[:, :], ident)
                pe.transpose(banks[2][:, 0:T], z2[:, :], ident).then_inc(c3_pe, 1)
                pe.wait_ge(c3_dve, 6)
                for h in range(H3):
                    for b in range(B):
                        pe.matmul(banks[3 + h][b * S:(b + 1) * S, :], q3bd[:, h, b * S:(b + 1) * S],
                                  k3T[:, b * SK:(b + 1) * SK], start=True, stop=True)
                for h in range(H3):
                    ins = pe.matmul(banks[5][:, h * T:(h + 1) * T], q3bd[:, h, :], kl3T, start=True, stop=True)
                ins.then_inc(c3_pe, 1)
                for h in range(H3):
                    pe.wait_ge(c3_dve, 11 + h)
                    for c in range(4):
                        ins = pe.transpose(banks[h][:, c * 128:(c + 1) * 128],
                                           big_a[:, h * 640 + c * 128:h * 640 + (c + 1) * 128], ident)
                    ins.then_inc(c3_pe, 1)
                for h in range(H3):
                    ins = pe.transpose(banks[2][:, h * T:(h + 1) * T], big_a[:, h * 640 + 512:h * 640 + 640], ident)
                ins.then_inc(c3_pe, 1)
                pe.wait_ge(c3_act, 21)
                pe.wait_ge(c3_dve, 13)
                for h in range(H3):
                    p = slice(64 * h, 64 * h + 64)
                    pe.matmul(banks[6][p, 0:T], qkv3[:, 256 + 64 * h:320 + 64 * h], big_b[:, 1024 + h * T:1024 + (h + 1) * T],
                              start=True, stop=False, skip_group_check=True)
                    for b in range(B):
                        for c in range(CK):
                            ins = pe.matmul(banks[6][p, b * S:(b + 1) * S], kv3[:, b * CK + c, 128 + 64 * h:192 + 64 * h],
                                            big_b[:, h * 512 + c * 128 + b * S:h * 512 + c * 128 + (b + 1) * S],
                                            start=False, stop=c == CK - 1, skip_group_check=True)
                ins.then_inc(c3_pe, 1)
                pe.wait_ge(c3_dve, 14)
                pe.matmul(banks[0][:, 0:D], oT[:, :], w("x3_wo"), start=True, stop=True).then_inc(y_full, 1)

            def state_space():
                m = 13 + B + 1
                pe.matmul(banks[7][:, 256:264], xnT[:, :], w("m_in", 128, 768, 776), start=True, stop=True)
                for j in range(4):
                    ins = pe.matmul(banks[0][:, j * T:(j + 1) * T], w("m_in", 128, 256 + j * 128, 384 + j * 128), xnT[:, :],
                                    start=True, stop=True)
                ins.then_inc(mix_pe, 1)
                pe.matmul(banks[1][:, 0:256], xnT[:, :], w("m_in", 128, 0, 256), start=True, stop=True).then_inc(mix_pe, 1)
                pe.wait_ge(mix_dve, 13 + 2 * B + 4)
                for i, name in enumerate(("l_fw", "l_bw")):
                    pe.matmul(banks[2 + i][:, :], w(name), big_a[:, i * 512:i * 512 + 512], start=True, stop=True).then_inc(mix_pe, 1)
                pe.wait_ge(mix_dve, 13 + 2 * B + 5)
                for j in range(2):
                    pe.transpose(banks[4][:, j * 128:(j + 1) * 128], big_b[:, 1024 + j * 128:1024 + (j + 1) * 128], ident)
                for j in range(2):
                    pe.matmul(banks[6][:, 0:4], big_b[:, 1024 + j * 128:1024 + (j + 1) * 128], w("m_fc", 128, 4 * j, 4 * j + 4),
                              start=j == 0, stop=j == 1)
                pe.wait_ge(mix_dve, 13 + 2 * B + 6)
                pe.matmul(banks[5][:, 0:256], big_b[:, 1280:1408], cbd, start=True, stop=True).then_inc(mix_pe, 1)
                pe.wait_ge(mix_dve, 13 + 2 * B + 7)
                for h in range(NH):
                    for d in range(2):
                        ins = pe.matmul(banks[0][:, h * 64:(h + 1) * 64],
                                        big_a[:, 1024 + d * 512 + h * T:1024 + d * 512 + (h + 1) * T],
                                        big_c[:, 256 + h * 64:256 + (h + 1) * 64], start=d == 0, stop=d == 1)
                ins.then_inc(mix_pe, 1)
                pe.wait_ge(mix_dve, 13 + 2 * B + 8)
                for j in range(2):
                    ins = pe.transpose(banks[1][:, j * 128:(j + 1) * 128], big_c[:, 1024 + j * 128:1024 + (j + 1) * 128], ident)
                ins.then_inc(mix_pe, 1)
                pe.wait_ge(mix_dve, 13 + 2 * B + 9)
                for j in range(2):
                    ins = pe.matmul(banks[2][:, 0:D], big_c[:, 1280 + j * 128:1280 + (j + 1) * 128],
                                    w("m_out", 128, j * 128, (j + 1) * 128), start=j == 0, stop=j == 1)
                ins.then_inc(mix_pe, 1)

            pe.wait_ge(load["early"], 16)
            turn_norm(0)
            pe.wait_ge(load["ctxT"], 16)
            context_attention(0)
            if STAGES >= 2:
                turn_norm(1); linear_attention()
            if STAGES >= 3:
                turn_norm(2); feed_forward(0)
            if STAGES >= 4:
                turn_norm(3); context_attention(1)
            if STAGES >= 5:
                turn_norm(4); causal_attention()
            if STAGES >= 6:
                turn_norm(5); feed_forward(1)
            if STAGES >= 7:
                turn_norm(6); context_attention(2)
            if STAGES >= 8:
                turn_norm(7); lstm()
            if STAGES >= 9:
                turn_norm(8); feed_forward(2)
            if STAGES >= 10:
                context3()
                cross3()
            if STAGES >= 11:
                turn_norm(9); state_space()
            if STAGES >= 12:
                turn_norm(10); feed_forward(3)

        @block.vector
        def _(v):
            st = Steps(v, dve_step)

            def rsqrt(y, a, t1, t2):
                st.done(v.tensor_single_scalar(t1.bitcast(U32), a.bitcast(U32), 1, op=ALU.logical_shift_right))
                st.done(v.tensor_scalar(y.bitcast(I32), t1.bitcast(I32), -1.0, RSQRT_MAGIC, ALU.mult, ALU.add))
                for _ in range(3):
                    st.done(v.tensor_tensor(t1, y, y, ALU.mult))
                    st.done(v.tensor_tensor(t2, t1, a, ALU.mult))
                    st.done(v.tensor_scalar(t1, t2, -0.5, 1.5, ALU.mult, ALU.add))
                    st.done(v.tensor_tensor(y, y, t1, ALU.mult))

            def layer_norm(out, src):
                st.done(v.bn_stats(stats[:, :], src))
                st.done(v.bn_aggr(mv[:, :], stats[:, :]))
                st.done(v.tensor_scalar(nw[:, 0:1], mv[:, 1:2], LN_EPS, None, ALU.add))
                rsqrt(nw[:, 1:2], nw[:, 0:1], nw[:, 2:3], nw[:, 3:4])
                return v.tensor_scalar(out, src, mv[:, 0:1], nw[:, 1:2], ALU.subtract, ALU.mult)

            def norm(n):
                if n:
                    v.wait_ge(x_ready, n)
                layer_norm(xn[:, :], x[:, :]).then_inc(xn_ready, 1)

            def context_attention(layer):
                K = CA if layer < 2 else DC
                g0 = NG * layer
                if layer < 2:
                    v.wait_ge(q_in_psum, layer + 1)
                    st.done(v.tensor_scalar(qT[:, :], banks[6][:, 0:T], w(f"bq{layer}"), DH ** -0.5, ALU.add, ALU.mult))
                    v.tensor_tensor(big_a[:, :].rearrange("p (b h q) -> p b h q", b=B, h=H),
                                    qT[:, :].rearrange("p (b q) -> p b q", b=B).unsqueeze(2).to_broadcast([128, B, H, S]),
                                    w("head16").unsqueeze(1).unsqueeze(3).to_broadcast([128, B, H, S]),
                                    ALU.mult).then_inc(qbd_ready, 1)
                    if layer == 0:
                        v.wait_ge(mean_in_psum, 1)
                        v.tensor_copy(mean_cT[:, :], banks[5][0:CA, 0:B]).then_inc(mean_ready, 1)
                        v.wait_ge(mean_in_psum, 2)
                        st.done(v.tensor_copy(mean_vT[:, :], banks[5][:, 8:8 + B]))
                else:
                    v.wait_ge(q_in_psum, 3)
                    v.wait_ge(pool_set, SET_Q)
                    for half in range(2):
                        p = slice(64 * half, 64 * half + 64)
                        ins = v.tensor_scalar(q2bd[p, 4:8, half, :], banks[1][p, :].rearrange("p (a t) -> p a t", a=4),
                                              D2 ** -0.5, None, ALU.mult)
                    ins.then_inc(qw_dve, 1)
                    v.wait_ge(qw_in_psum, 8 + 4)
                for i in (1, 3):
                    v.wait_ge(qw_in_psum, 4 * layer + i + 1)
                    if layer < 2:
                        v.tensor_copy(big_b[0:K, i * 512:i * 512 + 512], banks[i][0:K, :]).then_inc(qw_dve, 1)
                    else:
                        out = big_b[0:K, :].rearrange("p (b g h q) -> p g h b q", b=B, g=HG, h=4)[:, i]
                        v.tensor_copy(out, banks[2 + i][0:K, :].rearrange("p (h b q) -> p h b q", h=4, b=B)).then_inc(qw_dve, 1)
                if layer == 0:
                    v.wait_ge(load["rows"], 16)
                st.done(v.tensor_tensor(xb[:, :], x[:, :], row(f"bo{layer}"), ALU.add))
                for i in range(NG + 2):
                    if i < NG:
                        g = g0 + i
                        v.wait_ge(scores_in_psum, g + 1)
                        if layer == 0:
                            if i >= 2:
                                v.wait_ge(probs_ready, g - 1)
                            v.tensor_scalar(clipped[:, i % 2, :], banks[i % 2][:, :], -1e4, 1e4, ALU.max, ALU.min).then_inc(clip_ready, 1)
                            v.wait_ge(clip_ready, i + 1)
                            v.tensor_reduce(negmax[:, i:i + 1], clipped[:, i % 2, :], AX.X, ALU.max, negate=True).then_inc(negmax_ready, 1)
                        else:
                            v.tensor_reduce(negmax[:, i:i + 1], banks[i % 2][:, :], AX.X, ALU.max, negate=True).then_inc(negmax_ready, 1)
                    if layer > 0 and 1 <= i <= NG:
                        j = i - 1
                        v.wait_ge(probsT_in_psum, g0 + j + 1)
                        if j >= 2:
                            v.wait_ge(pc_in_psum, g0 + j - 1)
                        v.tensor_copy(probsT[:, j % 2, :], banks[2 + j % 2][:, :]).then_inc(probsT_ready, 1)
                    if i >= 2:
                        j = i - 2
                        v.wait_ge(pc_in_psum, g0 + j + 1)
                        pc = banks[4 + j % 2]
                        st.done(v.reciprocal(rden[:, j:j + 1], pc[:, DC:CA]))
                        if j >= 2:
                            v.wait_ge(pcnT_in_psum, g0 + j - 1)
                        v.tensor_scalar(pcn[:, j % 2, :], pc[:, 0:CA], rden[:, j:j + 1], None, ALU.mult).then_inc(pcn_ready, 1)
                if layer == 0:
                    v.wait_ge(guard_read, NG)
                    v.tensor_tensor(nan_hit[:, :], nan_sum[:, :], nan_sum[:, :], ALU.not_equal).then_inc(nan_ready, 1)
                    v.wait_ge(nan_in_psum, 1)
                    st.done(v.tensor_reduce(nan_any[:, :], banks[5][:, 0:NG], AX.X, ALU.max))
                if layer < 2:
                    v.wait_ge(o_in_psum, layer + 1)
                    v.tensor_tensor(om[:, :, :].rearrange("p g (h d) -> p g h d", h=4),
                                    banks[0][:, :].rearrange("p (g h d) -> p g h d", g=NG, h=4),
                                    w("head4").unsqueeze(1).unsqueeze(3).to_broadcast([128, NG, 4, DH]),
                                    ALU.mult).then_inc(om_ready, 1)
                    v.wait_ge(oT_in_psum, layer + 1)
                    if layer == 0:
                        st.done(v.tensor_copy(oT[:, :], banks[1][:, 0:T]))
                        v.copy_predicated(oT[:, :].rearrange("p (b q) -> p b q", b=B),
                                          nan_any[:, :].bitcast(U32).unsqueeze(2).to_broadcast([128, B, S]),
                                          mean_vT[:, :].unsqueeze(2).to_broadcast([128, B, S])).then_inc(oT_ready, 1)
                    else:
                        v.tensor_copy(oT[:, :], banks[1][:, 0:T]).then_inc(oT_ready, 1)
                else:
                    v.wait_ge(o_in_psum, 3)
                    v.tensor_copy(o2T[:, 4:8, :], banks[1][:, :].rearrange("p (a t) -> p a t", a=4)).then_inc(qw_dve, 1)
                v.wait_ge(y_full, layer + 1)
                v.tensor_tensor(x[:, :], banks[2][:, 0:D], xb[:, :], ALU.add).then_inc(x_ready, 1)

            def softmax8(k, src):
                if src is not None:
                    st.done(src)
                v.tensor_reduce(rt[:, 0:1], lg[:, :], AX.X, ALU.max, negate=True).then_inc(lneg_ready, 1)
                v.wait_ge(lexp_ready, k + 1)
                st.done(v.reciprocal(rt[:, 2:3], rt[:, 1:2]))
                st.done(v.tensor_scalar(sc8[:, :], sc8[:, :], rt[:, 2:3], None, ALU.mult))

            def top2(values):
                st.done(v.max(top8[:, :], values))
                st.done(v.max_index(idx8[:, :], top8[:, :], values))
                st.done(v.tensor_copy(idxf[:, :], idx8[:, :]))

            def onehot(k, scale):
                return v.tensor_scalar(oh[:, k, :], w("iota"), idxf[:, k:k + 1], scale, ALU.is_equal, ALU.mult)

            def route(layer):
                v.wait_ge(logits_in_psum, layer + 1)
                logits = banks[7][:, 256:264]
                if layer == 0:
                    softmax8(0, v.tensor_tensor(lg[:, :], logits, row("f0_br"), ALU.add))
                    top2(sc8[:, :])
                    v.tensor_scalar(oh[:, 0, :], w("iota"), idxf[:, 0:1], top8[:, 0:1], ALU.is_equal, ALU.mult)
                    st.done(v.tensor_scalar(oh[:, 1, :], w("iota"), idxf[:, 1:2], top8[:, 1:2], ALU.is_equal, ALU.mult))
                    v.tensor_tensor(cw[:, :], oh[:, 0, :], oh[:, 1, :], ALU.add).then_inc(cw_ready, 1)
                    v.wait_ge(cw_ready, 1)
                    return
                if layer == 2:
                    st.done(v.tensor_copy(lg[:, :], logits))
                    top2(lg[:, :])
                    st.done(v.tensor_scalar(cw[:, :], w("iota"), idxf[:, 0:1], 0.5, ALU.is_equal, ALU.mult))
                    return
                softmax8(1 if layer == 1 else 2, v.tensor_copy(lg[:, :], logits))
                if layer == 1:
                    st.done(v.tensor_reduce(grp8[:, 0:4], sc8[:, :].rearrange("p (g e) -> p g e", g=4), AX.X, ALU.max))
                    top2(grp8[:, :])
                    onehot(0, 1.0)
                    st.done(onehot(1, 1.0))
                    st.done(v.tensor_tensor(oh[:, 0, 0:4], oh[:, 0, 0:4], oh[:, 1, 0:4], ALU.add))
                    st.done(v.tensor_tensor(sc8[:, :].rearrange("p (g e) -> p g e", g=4), sc8[:, :].rearrange("p (g e) -> p g e", g=4),
                                            oh[:, 0, 0:4].unsqueeze(2).to_broadcast([128, 4, 2]), ALU.mult))
                top2(sc8[:, :])
                st.done(v.tensor_tensor(rt[:, 3:4], top8[:, 0:1], top8[:, 1:2], ALU.add))
                st.done(v.reciprocal(rt[:, 4:5], rt[:, 3:4]))
                st.done(v.tensor_scalar(rt[:, 5:7], top8[:, 0:2], rt[:, 4:5], 0.5, ALU.mult, ALU.mult))
                if layer == 3:
                    onehot(0, 1.0)
                    v.tensor_scalar(oh[:, 1, :], w("iota"), idxf[:, 1:2], 1.0, ALU.is_equal, ALU.mult).then_inc(cw_ready, 1)
                    v.wait_ge(cwT_in_psum, 3)
                    st.done(v.tensor_scalar(act_a[:, 0:16], banks[6][:, 0:16], float(CAP), None, ALU.is_le))
                    st.done(v.tensor_tensor(oh[:, :, :], oh[:, :, :], act_a[:, 0:16].rearrange("p (k e) -> p k e", k=2), ALU.mult))
                    v.tensor_scalar(oh[:, 0, :], oh[:, 0, :], rt[:, 5:6], None, ALU.mult)
                    st.done(v.tensor_scalar(oh[:, 1, :], oh[:, 1, :], rt[:, 6:7], None, ALU.mult))
                else:
                    for k in range(2):
                        ins = v.tensor_scalar(oh[:, k, :], w("iota"), idxf[:, k:k + 1], rt[:, 5 + k:6 + k], ALU.is_equal, ALU.mult)
                    st.done(ins)
                st.done(v.tensor_tensor(cw[:, :], oh[:, 0, :], oh[:, 1, :], ALU.add))

            def feed_forward(layer):
                e0 = E * layer
                C = FFN_CHUNKS[layer] * 128

                def hidden(e):
                    n = e0 + e
                    if layer == 0:
                        v.wait_ge(up_in_psum, n + 1)
                        if e >= 2:
                            v.wait_ge(y_in_psum, n - 1)
                        v.tensor_scalar(hid[:, e % 2, T:2 * T], banks[2 + e % 2][:, 0:T], w("f0_b1", 128, 2 * e + 1, 2 * e + 2), 0.0,
                                        ALU.add, ALU.max).then_inc(hid_ready, 1)
                        return
                    v.wait_ge(tanh_ready, n + 1 - E)
                    if e:
                        v.wait_ge(hid_ready, n)
                    st.done(v.scalar_tensor_tensor(out=act_a[:, 0:C], in0=tg[:, e % 2, 0:C], scalar=1.0, in1=banks[e % 2][:, 0:C],
                                                   op0=ALU.add, op1=ALU.mult))
                    v.wait_ge(up_in_psum, n + 1)
                    if e >= 2:
                        v.wait_ge(y_in_psum, n - 1)
                    v.tensor_tensor(hid[:, e % 2, 0:C], act_a[:, 0:C], banks[2 + e % 2][:, 0:C], ALU.mult).then_inc(hid_ready, 1)

                def add(e):
                    n = e0 + e
                    v.wait_ge(y_in_psum, n + 1)
                    if e:
                        v.wait_ge(y_added, n)
                    v.scalar_tensor_tensor(out=x[:, :], in0=banks[4 + e % 2][:, 0:D], scalar=cw[:, e:e + 1], in1=x[:, :],
                                           op0=ALU.mult, op1=ALU.add).then_inc(y_added, 1)

                hidden(0)
                route(layer)
                for e in range(1, E + 1):
                    if e < E:
                        hidden(e)
                    add(e - 1)
                v.wait_ge(y_added, e0 + E)
                if layer == 0:
                    v.wait_ge(cwT_in_psum, 1)
                    v.tensor_copy(cwT[:, :], banks[6][0:8, 0:T]).then_inc(cwT_ready, 1)
                    v.wait_ge(cwT_in_psum, 2)
                    v.tensor_tensor(x[:, :], banks[6][:, 256:256 + D], x[:, :], ALU.add).then_inc(x_ready, 1)
                else:
                    v.tensor_copy(lg[:, :], cw[:, :]).then_inc(x_ready, 1)

            def linear_attention():
                v.wait_ge(mix_pe, 1)
                st.done(v.tensor_scalar(qT[:, :], banks[0][:, 0:T], 0.0, 1e-6, ALU.max, ALU.add))
                st.done(v.tensor_scalar(ktA[:, :], banks[1][:, 0:T], 0.0, 1e-6, ALU.max, ALU.add))
                v.tensor_tensor(big_a[:, :].rearrange("p (h t) -> p h t", h=H), qT[:, :].unsqueeze(1).to_broadcast([128, H, T]),
                                w("head16").unsqueeze(2).to_broadcast([128, H, T]), ALU.mult).then_inc(mix_dve, 1)
                for i in range(4):
                    v.wait_ge(mix_pe, 2 + i)
                    v.tensor_tensor(big_b[:, i * 512:i * 512 + 512].rearrange("p (h t) -> p h t", h=4),
                                    banks[3 + i][:, :].rearrange("p (h t) -> p h t", h=4),
                                    w("causal_ts").unsqueeze(1).to_broadcast([128, 4, T]), ALU.mult).then_inc(mix_dve, 1)
                v.wait_ge(mix_pe, 6)
                o9 = banks[0][:, 0:H * 9].rearrange("p (h d) -> p h d", h=H)
                st.done(v.tensor_scalar(den16[:, :].unsqueeze(2), o9[:, :, 8:9], 1e-6, None, ALU.add))
                st.done(v.reciprocal(den16[:, :], den16[:, :]))
                v.tensor_tensor(o_tok[:, :].rearrange("p (h d) -> p h d", h=H), o9[:, :, 0:8],
                                den16[:, :].unsqueeze(2).to_broadcast([128, H, DH]), ALU.mult).then_inc(mix_dve, 1)
                v.wait_ge(mix_pe, 7)
                v.tensor_copy(oT[:, :], banks[1][:, 0:T]).then_inc(mix_dve, 1)
                v.wait_ge(mix_pe, 8)
                v.tensor_tensor(x[:, :], banks[2][:, 0:D], x[:, :], ALU.add).then_inc(x_ready, 1)
                v.wait_ge(x_ready, 2)
                v.tensor_copy(lg[:, 0:1], x[:, 0:1]).then_inc(mix_dve, 1)

            def causal_attention():
                v.wait_ge(mix_pe, 8 + 1)
                for i in range(2):
                    v.tensor_tensor(qk_[:, 2 * i, :], banks[2 * i][:, 0:T], w("rope_cos"), ALU.mult)
                    st.done(v.tensor_tensor(qk_[:, 2 * i + 1, :], banks[2 * i + 1][:, 0:T], w("rope_sin"), ALU.mult))
                st.done(v.tensor_tensor(ktA[:, :], qk_[:, 2, :], qk_[:, 3, :], ALU.add))
                st.done(v.tensor_tensor(z2[:, :], qk_[:, 0, :], qk_[:, 1, :], ALU.add))
                st.done(v.tensor_scalar(qT[:, :], z2[:, :], DH ** -0.5, None, ALU.mult))
                v.tensor_tensor(big_a[:, :].rearrange("p (b h t) -> p b h t", b=B, h=H),
                                ktA[:, :].rearrange("p (b t) -> p b t", b=B).unsqueeze(2).to_broadcast([128, B, H, S]),
                                w("head16").unsqueeze(1).unsqueeze(3).to_broadcast([128, B, H, S]), ALU.mult).then_inc(mix_dve, 1)
                v.wait_ge(mix_pe, 8 + 2)
                st.done(v.tensor_tensor(s_sb[:, :, :], banks[5][:, :].rearrange("p (h t) -> p h t", h=H),
                                        w("causal_add").unsqueeze(1).to_broadcast([128, H, S]), ALU.add))
                v.tensor_reduce(den16[:, :], s_sb[:, :, :], AX.X, ALU.max).then_inc(mix_dve, 1)
                v.wait_ge(mix_dve, 8 + 2)
                v.tensor_tensor(s_sb[:, :, :], s_sb[:, :, :], den16[:, :].unsqueeze(2).to_broadcast([128, H, S]),
                                ALU.subtract).then_inc(mix_dve, 1)
                v.wait_ge(mix_act, 1 + 2)
                v.transpose(pT_sb[:, :, :].rearrange("p h t -> p (h t)"), s_sb[:, :, :].rearrange("p h t -> p (h t)"))
                st.done(v.tensor_reduce(den16[:, :], s_sb[:, :, :], AX.X, ALU.add))
                st.done(v.reciprocal(den16[:, :], den16[:, :]))
                v.tensor_tensor(big_b[:, :].rearrange("p (h b q) -> p h b q", h=H, b=B),
                                pT_sb[:, :, :].unsqueeze(2).to_broadcast([128, H, B, S]),
                                w("fold4").unsqueeze(1).unsqueeze(3).to_broadcast([128, H, B, S]), ALU.mult).then_inc(mix_dve, 1)
                v.wait_ge(mix_pe, 8 + 3)
                v.tensor_tensor(z2[:, :].rearrange("p (h d) -> p h d", h=H), banks[0][:, 0:D].rearrange("p (h d) -> p h d", h=H),
                                den16[:, :].unsqueeze(2).to_broadcast([128, H, DH]), ALU.mult).then_inc(mix_dve, 1)
                v.wait_ge(mix_pe, 8 + 4)
                v.tensor_copy(oT[:, :], banks[1][:, 0:T]).then_inc(oT_ready, 1)
                v.wait_ge(mix_pe, 8 + 5)
                v.tensor_tensor(x[:, :], banks[2][:, 0:D], x[:, :], ALU.add).then_inc(x_ready, 1)

            def lstm():
                for t in range(B):
                    v.wait_ge(mix_act, 3 + 2 * t + 1)
                    v.scalar_tensor_tensor(out=cst[:, 1 if t else 2, :], in0=gates[:, 0, :], scalar=1.0, in1=gates[:, 3, :],
                                           op0=ALU.add, op1=ALU.mult).then_inc(dve_step if t else mix_dve, 1)
                    if t:
                        st.n += 1
                        st.done(v.scalar_tensor_tensor(out=cst[:, 0, :], in0=gates[:, 1, :], scalar=1.0, in1=cst[:, 4, :],
                                                       op0=ALU.add, op1=ALU.mult))
                        v.tensor_tensor(cst[:, 2, :], cst[:, 0, :], cst[:, 1, :], ALU.add).then_inc(mix_dve, 1)
                    v.wait_ge(mix_dve, 13 + 2 * t + 1)
                    st.done(v.tensor_scalar(cst[:, 4, :], cst[:, 2, :], 0.5, None, ALU.mult))
                    v.wait_ge(mix_act, 3 + 2 * t + 2)
                    v.scalar_tensor_tensor(out=h2T[:, t * S:(t + 1) * S], in0=gates[:, 2, :], scalar=1.0, in1=cst[:, 3, :],
                                           op0=ALU.add, op1=ALU.mult).then_inc(mix_dve, 1)
                v.wait_ge(mix_pe, 13 + B + 1)
                v.scalar_tensor_tensor(out=x[:, :], in0=banks[1][:, 0:D], scalar=0.5, in1=x[:, :],
                                       op0=ALU.mult, op1=ALU.add).then_inc(x_ready, 1)

            def context3():
                v.wait_ge(load["ctxk"], 16)
                for k in range(NC):
                    ins = v.bn_stats(st3[:, k, :], ctxk[:, k, 0:DC])
                st.done(ins)
                for k in range(NC):
                    ins = v.bn_aggr(mv3[:, k, :], st3[:, k, :])
                st.done(ins)
                st.done(v.tensor_scalar(n3[:, 0, 0:NC].unsqueeze(2), mv3[:, :, 1:2], LN_EPS, None, ALU.add))
                rsqrt(n3[:, 1, 0:NC], n3[:, 0, 0:NC], n3[:, 2, 0:NC], n3[:, 3, 0:NC])
                zc = big_a[:, 0:NC * DC].rearrange("p (k c) -> p k c", k=NC)
                for k in range(NC):
                    ins = v.tensor_scalar(zc[:, k, :], ctxk[:, k, 0:DC], mv3[:, k, 0:1], n3[:, 1, k:k + 1], ALU.subtract, ALU.mult)
                ins.then_inc(c3_dve, 1)
                v.wait_ge(c3_act, 12)
                sq = big_b[:, :].rearrange("p (k n) -> p k n", k=NC)
                st.done(v.tensor_tensor(sq, kv3[:, :, 0:128], kv3[:, :, 0:128], ALU.mult))
                st.done(v.tensor_reduce(n3[:, 0, :], big_b[:, :].rearrange("p (k d) -> p k d", d=D3), AX.X, ALU.add))
                st.done(v.tensor_scalar(n3[:, 0, :], n3[:, 0, :], 1.0 / D3, 1e-16, ALU.mult, ALU.max))
                rsqrt(n3[:, 1, :], n3[:, 0, :], n3[:, 2, :], n3[:, 3, :])
                for h in range(H3):
                    ins = v.tensor_tensor(kv3[:, :, 64 * h:64 * h + 64], kv3[:, :, 64 * h:64 * h + 64],
                                          n3[:, 1, :].rearrange("p (k h) -> p k h", h=H3)[:, :, h:h + 1].to_broadcast([128, NC, D3]),
                                          ALU.mult)
                ins.then_inc(c3_dve, 1)

            def cross3():
                v.wait_ge(x_ready, 9)
                v.wait_ge(pool_set, SET_L3)
                st.done(v.tensor_tensor(xb[:, :], x[:, :], row("bo3"), ALU.add))
                st.done(layer_norm(xn[:, :], x[:, :]))
                layer_norm(z2[:, :], xn[:, :]).then_inc(c3_dve, 1)
                v.wait_ge(q_in_psum, 4)
                v.tensor_scalar(xnT[:, :], banks[7][:, 0:T], w("l3_g"), w("l3_b"), ALU.mult, ALU.add).then_inc(c3_dve, 1)
                v.wait_ge(c3_act, 17)
                st.done(v.tensor_tensor(big_a[:, 0:256], qkv3[:, 0:256], qkv3[:, 0:256], ALU.mult))
                st.done(v.tensor_reduce(d3[:, 4:8], big_a[:, 0:256].rearrange("p (k d) -> p k d", d=D3), AX.X, ALU.add))
                st.done(v.tensor_scalar(n3[:, 0, 0:4], d3[:, 4:8], 1.0 / D3, 1e-16, ALU.mult, ALU.max))
                rsqrt(n3[:, 1, 0:4], n3[:, 0, 0:4], n3[:, 2, 0:4], n3[:, 3, 0:4])
                v.tensor_tensor(xn[:, :].rearrange("p (h d) -> p h d", h=2), qkv3[:, 0:128].rearrange("p (h d) -> p h d", h=2),
                                n3[:, 1, 0:2].unsqueeze(2).to_broadcast([128, 2, D3]), ALU.mult)
                v.tensor_tensor(z2[:, :].rearrange("p (h d) -> p h d", h=2), qkv3[:, 128:256].rearrange("p (h d) -> p h d", h=2),
                                n3[:, 1, 2:4].unsqueeze(2).to_broadcast([128, 2, D3]), ALU.mult).then_inc(c3_dve, 1)
                v.wait_ge(c3_pe, 18)
                st.done(v.tensor_scalar(qT[:, :], banks[1][:, 0:T], w("qn_g"), w("kn_g"), ALU.mult, ALU.mult))
                v.tensor_copy(kl3T, banks[2][:, 0:T])
                for h in range(H3):
                    p = slice(64 * h, 64 * h + 64)
                    ins = v.tensor_scalar(q3bd[p, h, :], qT[p, :], D3 ** -0.5, None, ALU.mult)
                ins.then_inc(c3_dve, 1)
                v.wait_ge(c3_pe, 19)
                for h in range(H3):
                    v.tensor_tensor(big_a[:, h * 640:h * 640 + 512], banks[3 + h][:, :], mask_add, ALU.add).then_inc(c3_dve, 1)
                v.tensor_tensor(big_a[:, 0:1280].rearrange("p (h k) -> p h k", h=2)[:, :, 512:640],
                                banks[5][:, 0:256].rearrange("p (h k) -> p h k", h=2),
                                w("batch_add").unsqueeze(1).to_broadcast([128, 2, T]), ALU.add).then_inc(c3_dve, 1)
                v.wait_ge(c3_dve, 9)
                v.tensor_reduce(d3[:, 0:2], big_a[:, 0:1280].rearrange("p (h k) -> p h k", h=2), AX.X, ALU.max,
                                negate=True).then_inc(c3_dve, 1)
                for h in range(H3):
                    v.wait_ge(c3_act, 18 + h)
                    st.done(v.reciprocal(d3[:, 4 + h:5 + h], d3[:, 2 + h:3 + h]))
                    v.tensor_scalar(big_a[:, h * 640:h * 640 + 640], big_a[:, h * 640:h * 640 + 640], d3[:, 4 + h:5 + h], None,
                                    ALU.mult).then_inc(c3_dve, 1)
                v.wait_ge(c3_pe, 21)
                v.tensor_copy(big_b[:, 512:1024], banks[1][:, :]).then_inc(c3_dve, 1)
                v.wait_ge(c3_pe, 23)
                v.tensor_copy(oT[:, :], banks[6][:, 0:T]).then_inc(c3_dve, 1)
                v.wait_ge(y_full, 4)
                v.tensor_tensor(x[:, :], banks[0][:, 0:D], xb[:, :], ALU.add).then_inc(x_ready, 1)

            def state_space():
                m, d, a = 13 + B + 1, 13 + 2 * B, 3 + 2 * B
                v.wait_ge(mix_pe, m + 1)
                v.tensor_tensor(dts[:, 0, :].rearrange("p (d h) -> p d h", d=2),
                                banks[7][:, 256:264].rearrange("p (d h) -> p d h", d=2),
                                row("dtb").unsqueeze(1).to_broadcast([128, 2, NH]), ALU.add).then_inc(mix_dve, 1)
                v.tensor_copy(convp[:, :, :, PAD:PAD + S], banks[0][:, :].rearrange("p (j b l) -> p j b l", j=4, b=B)).then_inc(mix_dve, 1)
                v.tensor_scalar(big_c[:, 512:544], late[:, late_at["m_cw"][0]:late_at["m_cw"][0] + 32], 0.5, None, ALU.mult).then_inc(dve_step, 1)
                st.n += 1
                v.wait_ge(dve_step, st.n)
                v.wait_ge(mix_dve, d + 2)
                for k in range(TAPS):
                    for j in range(4):
                        out = big_b[:, j * T:(j + 1) * T].rearrange("p (b l) -> p b l", b=B)
                        src = convp[:, j, :, k:k + S]
                        tap = big_c[:, 512 + 7 * j + k:513 + 7 * j + k]
                        if k == 0:
                            ins = v.tensor_scalar(out, src, tap, big_c[:, 540 + j:541 + j], ALU.mult, ALU.add)
                        else:
                            ins = v.scalar_tensor_tensor(out=out, in0=src, scalar=tap, in1=out, op0=ALU.mult, op1=ALU.add)
                    if k == TAPS - 1:
                        ins.then_inc(mix_dve, 1)
                    else:
                        st.done(ins)
                v.wait_ge(mix_act, a + 3)
                st.done(v.tensor_scalar(dts[:, 3, :], dts[:, 0, :], 0.0, None, ALU.max))
                st.done(v.tensor_tensor(dts[:, 3, :], dts[:, 3, :], dts[:, 2, :], ALU.add))
                st.done(v.tensor_tensor(dts[:, 4, :].rearrange("p (d h) -> p d h", d=2), dts[:, 3, :].rearrange("p (d h) -> p d h", d=2),
                                        dts[:, 5, 0:4].unsqueeze(1).to_broadcast([128, 2, NH]), ALU.mult))
                for i, name in enumerate(("m_fw", "m_bw")):
                    ins = v.tensor_tensor(big_a[:, i * 512:i * 512 + 512].rearrange("p (h t) -> p h t", h=NH),
                                          w(name).unsqueeze(1).to_broadcast([128, NH, T]),
                                          dts[:, 4, 4 * i:4 * i + 4].unsqueeze(2).to_broadcast([128, NH, T]), ALU.mult)
                ins.then_inc(mix_dve, 1)
                v.wait_ge(mix_act, a + 5)
                v.scalar_tensor_tensor(out=big_b[:, 1024:1536], in0=big_b[:, 512:1024], scalar=1.0, in1=big_b[:, 0:512],
                                       op0=ALU.add, op1=ALU.mult).then_inc(mix_dve, 1)
                v.wait_ge(mix_dve, d + 5)
                v.tensor_copy(cbd[0:64, 0, 1:T], big_b[0:64, 1408:1535])
                v.tensor_copy(cbd[64:128, 1, 0:T - 1], big_b[64:128, 1409:1536]).then_inc(mix_dve, 1)
                v.wait_ge(mix_pe, m + 5)
                gm = big_c[:, 768:1024]
                st.done(v.tensor_tensor(gm.rearrange("p (d t) -> p d t", d=2), banks[5][:, 0:256].rearrange("p (d t) -> p d t", d=2),
                                        late[:, late_at["m_fw"][0]:late_at["m_fw"][0] + 256].rearrange("p (d t) -> p d t", d=2), ALU.mult))
                v.tensor_copy(big_c[:, 256:512], banks[4][:, 0:256])
                st.done(v.tensor_tensor(dts[:, 5, 4:8], banks[6][:, 0:4], row("dp"), ALU.add))
                v.wait_ge(mix_act, a + 7)
                for i in range(2):
                    dec = big_a[:, 1024 + 512 * i:1536 + 512 * i].rearrange("p (h t) -> p h t", h=NH)
                    ins = v.tensor_tensor(dec, dec, gm[:, i * T:(i + 1) * T].unsqueeze(1).to_broadcast([128, NH, T]), ALU.mult)
                ins.then_inc(mix_dve, 1)
                st.done(v.tensor_tensor(big_c[:, 1536:1792].rearrange("p (h n) -> p h n", h=NH),
                                        big_c[:, 256:512].rearrange("p (h n) -> p h n", h=NH),
                                        dts[:, 5, 4:8].unsqueeze(2).to_broadcast([128, NH, 64]), ALU.mult))
                st.done(v.scalar_tensor_tensor(out=big_c[:, 1792:2048], in0=big_c[:, 0:256], scalar=1.0, in1=banks[1][:, 0:256],
                                               op0=ALU.add, op1=ALU.mult))
                v.wait_ge(mix_pe, m + 6)
                y = big_c[:, 1024:1280]
                st.done(v.tensor_tensor(y, banks[0][:, 0:256], big_c[:, 1536:1792], ALU.add))
                st.done(v.tensor_tensor(big_c[:, 1536:1792], y, y, ALU.mult))
                st.done(v.tensor_reduce(nw[:, 0:1], big_c[:, 1536:1792], AX.X, ALU.add))
                st.done(v.tensor_scalar(nw[:, 0:1], nw[:, 0:1], 1.0 / DI, 1e-5, ALU.mult, ALU.add))
                rsqrt(nw[:, 1:2], nw[:, 0:1], nw[:, 2:3], nw[:, 3:4])
                v.scalar_tensor_tensor(out=y, in0=y, scalar=nw[:, 1:2], in1=big_c[:, 1792:2048],
                                       op0=ALU.mult, op1=ALU.mult).then_inc(mix_dve, 1)
                v.wait_ge(mix_pe, m + 7)
                for j in range(2):
                    ins = v.tensor_scalar(big_c[:, 1280 + j * 128:1280 + (j + 1) * 128], banks[1][:, j * 128:(j + 1) * 128],
                                          w("m_nw", 128, j, j + 1), 0.5, ALU.mult, ALU.mult)
                ins.then_inc(mix_dve, 1)
                v.wait_ge(mix_pe, m + 8)
                v.tensor_tensor(x[:, :], banks[2][:, 0:D], x[:, :], ALU.add).then_inc(x_ready, 1)

            v.wait_ge(load["x"], 16)
            v.wait_ge(load["early"], 16)
            norm(0)
            context_attention(0)
            if STAGES >= 2:
                norm(1); linear_attention()
            if STAGES >= 3:
                v.wait_ge(load["late"], 16)
                norm(2); feed_forward(0)
            if STAGES >= 4:
                norm(3); context_attention(1)
            if STAGES >= 5:
                norm(4); causal_attention()
            if STAGES >= 6:
                norm(5); feed_forward(1)
            if STAGES >= 7:
                norm(6); context_attention(2)
            if STAGES >= 8:
                norm(7); lstm()
            if STAGES >= 9:
                norm(8); feed_forward(2)
            if STAGES >= 10:
                context3()
                cross3()
            if STAGES >= 11:
                norm(10); state_space()
            if STAGES >= 12:
                norm(11); feed_forward(3)


def constants():
    p = np.arange(128)
    one = np.float32
    batch, t = p // S, p % S
    same = batch[:, None] == batch[None, :]
    c = {
        "ident": np.eye(128), "head16": p[:, None] // DH == np.arange(H)[None, :],
        "head4": p[:, None] // S == np.arange(4)[None, :], "fold": p[:, None] % S == np.arange(S)[None, :],
        "ones": np.ones((128, 128)), "causal_ts": same & (p[:, None] <= p[None, :]),
        "causal_add": np.where(np.arange(S)[None, :] <= t[:, None], 0.0, -BIG),
        "cum": p[:, None] <= p[None, :],
        "m_fw": same & (p[:, None] < p[None, :]), "m_bw": same & (p[:, None] > p[None, :]),
        "l_fw": same & (p[:, None] > p[None, :]), "l_bw": same & (p[:, None] < p[None, :]),
        "batch_add": np.where(same, 0.0, -BIG), "iota": np.tile(np.arange(8), (128, 1)),
    }
    d = p % DH
    freq = (np.float32(10000.0) ** (-(np.arange(0, DH, 2, dtype=np.float32)) / np.float32(DH)))[d // 2]
    ang = t[None, :].astype(np.float32) * freq[:, None].astype(np.float32)
    c["rope_cos"] = np.cos(ang)
    c["rope_sin"] = np.sin(ang) * np.where(d % 2 == 0, -1.0, 1.0)[:, None]
    return {k: np.asarray(v, one) for k, v in c.items()}


def kernel(**inputs):
    import concourse.bacc as bacc
    from concourse.bass_utils import run_bass_kernel_spmd

    i = {k: np.asarray(v) for k, v in inputs.items()}
    r = lambda a: np.ascontiguousarray(a)
    col = lambda a: a.reshape(-1, 1)
    small = constants()
    for k, pre in ((0, "L0_xattn_"), (1, "L1_xattn_")):
        if k == 0:
            wk, wv, bk, bv, wq, wo = (i[pre + n] for n in ("Wk", "Wv", "bk", "bv", "Wq", "Wo"))
        else:
            kv = i[pre + "Wkv"].reshape(H, 2, DH, DC)
            bkv = i[pre + "bkv"].reshape(H, 2, DH)
            wk, wv = (kv[:, j].reshape(D, DC).T for j in range(2))
            bk, bv = (bkv[:, j].reshape(D) for j in range(2))
            wq, wo = i[pre + "Wq"].T, i[pre + "Wo"].T
        small[f"wq{k}"], small[f"wo{k}"], small[f"bq{k}"] = wq, wo, col(i[pre + "bq"])
        small[f"wkT{k}"] = np.concatenate([wk.T, col(bk)], axis=1)
        small[f"wv{k}"] = np.concatenate([wv, bv[None, :]], axis=0)
    for n in ("q", "k", "v", "o"):
        small["a_w" + n] = i["L0_attn_W" + n].T
        small["r_w" + n] = i[f"L1_attn_{n}_proj"].T
    swap = np.arange(D) ^ 1
    for n in ("r_wq", "r_wk"):
        small[n] = np.concatenate([small[n], small[n][:, swap]], axis=1)
    small["f0_wr"], small["f1_wr"] = i["L0_ffn_Wr"], i["L1_ffn_gate_w"].T
    small["f2_wr"], small["f3_wr"] = i["L2_ffn_router_w"].T, i["L3_ffn_gate_w"].T
    small["f0_b1"] = i["L0_ffn_b1"].reshape(E * 2, 128).T
    small["f0_b2"] = i["L0_ffn_b2"]
    small["lstm_w"], small["lstm_u"] = i["L2_attn_w"], i["L2_attn_u"]
    small["x3_g"], small["x3_b"] = col(i["L3_xattn_ln_x_g"]), col(i["L3_xattn_ln_x_b"])
    small["l3_g"], small["l3_b"] = col(i["L3_xattn_ln_l_g"]), col(i["L3_xattn_ln_l_b"])
    small["qn_g"], small["kn_g"] = (col(np.tile(i[f"L3_xattn_{n}_g"], 2)) for n in ("qn", "kn"))
    small["x3_wqkv"] = np.concatenate([i["L3_xattn_Wq"].T, i["L3_xattn_Wlkv"].T], axis=1)
    small["x3_wkv"], small["x3_wo"] = i["L3_xattn_Wkv"].T, i["L3_xattn_Wo"].T
    ch = np.concatenate([np.arange(256), np.arange(256, 320), np.arange(384, 448), np.arange(320, 384), np.arange(448, 512)])
    order = np.concatenate([np.arange(DI), DI + ch, np.arange(768, 776)])
    small["m_in"] = i["L3_attn_W_in"][order].T
    small["m_cw"] = i["L3_attn_conv_w"][ch, 0].reshape(4, 128, TAPS).transpose(1, 0, 2).reshape(128, 28)
    small["m_cb"] = i["L3_attn_conv_b"][ch].reshape(4, 128).T
    small["m_fc"] = i["L3_attn_fc_D_w"].reshape(NH, 2, 128).transpose(2, 1, 0).reshape(128, 8)
    small["m_nw"] = i["L3_attn_norm_w"].reshape(2, 128).T
    small["m_out"] = i["L3_attn_W_out"].T.reshape(2, 128, 128).transpose(1, 0, 2).reshape(128, 256)
    small["fold4"] = small["head4"]

    def pack(table):
        out = np.zeros((128, columns(table)[1]), np.float32)
        for name, (at, n) in columns(table)[0].items():
            out[:small[name].shape[0], at:at + n] = small[name]
        return out

    def pad(a):
        return np.concatenate([a, np.zeros((E, 384 - a.shape[1], 128), a.dtype)], axis=1)

    def chunked(a):
        return r(a.reshape(E, -1, 128, 128).transpose(2, 0, 1, 3).reshape(128, E, -1))

    ctx = i["ctx_768"].reshape(B * SK, DC)
    up = lambda a: r(a.transpose(2, 0, 1))
    arrays = {
        "early": pack(EARLY), "late": pack(LATE), "x": r(i["x"].reshape(T, D)),
        "rows": r(np.concatenate([i["L0_xattn_bo"], i["L1_xattn_bo"], i["L2_xattn_b_out"], i["L3_xattn_bo"], i["L0_ffn_br"],
                                  i["L3_attn_dt_bias"], i["L3_attn_A_log"], i["L3_attn_Dp"], i["L2_attn_bias"]])[None, :]),
        "ctxT": r(ctx.T), "ctxk": r(ctx.reshape(NC, 128, DC).transpose(1, 0, 2)),
        "mask": r(i["mask_BxS2_bk0"]),
        "f0_w1": r(i["L0_ffn_W1"].transpose(1, 0, 2)), "f0_w2": chunked(i["L0_ffn_W2"]),
        "f1_w13": up(i["L1_ffn_w13_weight"]), "f1_w2": chunked(i["L1_ffn_w2_weight"].transpose(0, 2, 1)),
        "f2_wg": up(pad(i["L2_ffn_gate_w"])), "f2_wu": up(pad(i["L2_ffn_up_w"])),
        "f2_wd": chunked(pad(i["L2_ffn_down_w"].transpose(0, 2, 1))),
        "f3_wg": up(i["L3_ffn_wi_gate"]), "f3_wu": up(i["L3_ffn_wi_up"]), "f3_wd": chunked(i["L3_ffn_wo"].transpose(0, 2, 1)),
        "x2_wq": r(i["L2_xattn_w_q"]), "x2_wkT": r(i["L2_xattn_w_k"].T.reshape(8, 128, DC).transpose(1, 0, 2)),
        "x2_wv": r(i["L2_xattn_w_v"]), "x2_wo": r(i["L2_xattn_w_out"].reshape(8, 128, 128).transpose(1, 0, 2)),
    }
    nc = bacc.Bacc("TRN2", target_bir_lowering=False, num_devices=1)
    feeds = {f"in_{n}": a for n, a in arrays.items()}
    dram = {n: nc.dram_tensor(f"in_{n}", a.shape, mybir.dt.from_np(a.dtype), kind="ExternalInput").ap()
            for n, a in arrays.items()}
    dram["out"] = nc.dram_tensor("out_x", (T, D), F32, kind="ExternalOutput").ap()
    build(nc, dram)
    got = run_bass_kernel_spmd(nc, [feeds], core_ids=[0]).results[0]["out_x"]
    return got.reshape(B, S, D)
```

```python
from contextlib import ExitStack

import numpy as np

import concourse.bass as bass
from concourse import mybir

F32 = mybir.dt.float32
U32 = mybir.dt.uint32
I32 = mybir.dt.int32
U8 = mybir.dt.uint8
ALU = mybir.AluOpType
ACT = mybir.ActivationFunctionType
AX = mybir.AxisListType

STAGES = 12

B, S, D = 4, 32, 128
T = B * S
H = 16
DH = D // H
SK, DC = 512, 96
CK = SK // 128
NC = B * CK
CA = DC + 1
E = 8
HG = H // 4
NG = B * HG
LN_EPS = 1e-5
BIG = 3.0e38
CAP = int(T / E * 1.25)
RSQRT_MAGIC = float(0x5F3759DF - (3 << 23) - (1 << 31))
H2, D2 = 16, 64
H3, D3 = 2, 64
DI, NS_, NH = 256, 64, 4
TAPS = 7
PAD = TAPS // 2
SP = S + 2 * PAD
FFN_CHUNKS = {0: 2, 1: 2, 2: 3, 3: 4}

EARLY = [("ident", 128), ("head16", 16), ("head32", 32), ("fold", 32), ("ones", 128), ("causal_ts", 128),
         ("wq0", 128), ("bq0", 1), ("wkT0", CA), ("wv0", 128), ("wo0", 128)]
LATE = [("causal_add", 32), ("fold4", 4), ("rope_cos", 128), ("rope_sin", 128), ("cum", 128),
        ("m_fw", 128), ("m_bw", 128), ("l_fw", 128), ("l_bw", 128), ("batch_add", 128), ("iota", 8),
        ("a_wq", 128), ("a_wk", 128), ("a_wv", 128), ("a_wo", 128),
        ("f0_wr", 8), ("f0_b1", 16), ("f0_b2", 128),
        ("wq1", 128), ("bq1", 1), ("wkT1", CA), ("wv1", 128), ("wo1", 128),
        ("r_wq", 256), ("r_wk", 256), ("r_wv", 128), ("r_wo", 128), ("f1_wr", 8),
        ("lstm_w", 512), ("lstm_u", 512), ("f2_wr", 8),
        ("x3_g", 1), ("x3_b", 1), ("l3_g", 1), ("l3_b", 1), ("qn_g", 1), ("kn_g", 1),
        ("x3_wqkv", 384), ("x3_wkv", 256), ("x3_wo", 128),
        ("m_in", 776), ("m_cw", 28), ("m_cb", 4), ("m_fc", 8), ("m_nw", 2), ("m_out", 256), ("f3_wr", 8)]
ROWS = [("bo0", 128), ("bo1", 128), ("bo2", 128), ("bo3", 128), ("f0_br", 8), ("dtb", 4), ("alog", 4), ("dp", 4),
        ("lstm_b", 512)]


def columns(table):
    at, out = 0, {}
    for name, n in table:
        out[name] = (at, n)
        at += n
    return out, at


def build(nc, dram):
    with ExitStack() as ctx:
        def sb(name, shape, dt=F32):
            return ctx.enter_context(nc.sbuf_tensor(name, shape, dt))

        def sem(name):
            return ctx.enter_context(nc.semaphore(name))

        early_at, n_early = columns(EARLY)
        late_at, n_late = columns(LATE)
        row_at, n_rows = columns(ROWS)
        early = sb("early", [128, n_early])
        late = sb("late", [128, n_late])
        rows = sb("rows", [128, n_rows])

        def w(name, rows_=128, a=0, b=None):
            tile, at = (early, early_at) if name in early_at else (late, late_at)
            start, n = at[name]
            return tile[0:rows_, start + a:start + (n if b is None else b)]

        def row(name, a=0, b=None, p=128):
            start, n = row_at[name]
            return rows[0:p, start + a:start + (n if b is None else b)]

        ident = w("ident")
        ctxT = sb("ctxT", [CA, B * SK])
        ctxk = sb("ctxk", [128, NC, CA])
        f0_w1 = sb("f0_w1", [128, E, 256])
        f0_w2 = sb("f0_w2", [128, E, 256])
        f1_w13 = sb("f1_w13", [128, E, 512])
        f1_w2 = sb("f1_w2", [128, E, 256])
        f2_wg = sb("f2_wg", [128, E, 384])
        f2_wu = sb("f2_wu", [128, E, 384])
        f2_wd = sb("f2_wd", [128, E, 384])
        x2_wqo = sb("x2_wqo", [128, 2, 1024])
        x2_wq = x2_wqo[:, 0, :]
        x2_wkT = sb("x2_wkT", [128, 8, DC])
        x2_v = sb("x2_v", [128, H2 * D2])
        x2_wv = x2_v[0:DC, :]
        x2_wo = x2_wqo[:, 1, :].rearrange("p (a n) -> p a n", a=8)

        f3_wg = f1_w13
        f3_wd = [f0_w1[:, :, :].rearrange("p (e a) f -> p e (a f)", a=2), f0_w2[:, :, :].rearrange("p (e a) f -> p e (a f)", a=2)]
        f3_wu = [f1_w2[:, :, :].rearrange("p (e a) f -> p e (a f)", a=2), x2_wqo[:, :, :].rearrange("p a (e f) -> p (a e) f", e=2)]

        x = sb("x", [128, D])
        xb = sb("xb", [128, D])
        xn = sb("xn", [128, D])
        xnT = sb("xnT", [128, T])
        stats = sb("stats", [128, 6])
        mv = sb("mv", [128, 2])
        nw = sb("nw", [128, 8])
        z2 = sb("z2", [128, D])

        big_a = sb("big_a", [128, 2048])
        big_b = sb("big_b", [128, 2048])
        big_c = sb("big_c", [128, 2048])
        kv3 = sb("kv3", [128, NC, 256])
        zc = kv3[:, :, :].rearrange("p a n -> p (a n)")[:, 0:NC * DC].rearrange("p (k c) -> p k c", k=NC)
        q2bd = f0_w1[:, :, :].rearrange("p a (h t) -> p a h t", h=2)
        o2T = f0_w2[:, 0:4, :].rearrange("p a (h t) -> p (a h) t", h=2)
        k3T = sb("k3T", [128, B * SK])
        clipped = k3T[:, 0:1024].rearrange("p (a k) -> p a k", a=2)
        guard_out = k3T[:, 1024:1536]
        s_sb = k3T[:, 1024:1536].rearrange("p (h t) -> p h t", h=H)
        pT_sb = k3T[:, 1536:2048].rearrange("p (h t) -> p h t", h=H)
        probs = sb("probs", [128, 2, SK])
        probsT = sb("probsT", [128, 2, SK])
        qT = sb("qT", [128, T])
        negmax = sb("negmax", [128, NG])
        nan_sum = sb("nan_sum", [128, NG])
        nan_hit = sb("nan_hit", [128, NG])
        nan_any = sb("nan_any", [128, 1])
        mean_col = sb("mean_col", [128, 1])
        mean_cT = sb("mean_cT", [CA, B])
        mean_vT = sb("mean_vT", [128, B])
        den = sb("den", [128, NG])
        rden = sb("rden", [128, NG])
        pcn = sb("pcn", [128, 2, CA])
        om = sb("om", [128, NG, 32])
        oT = sb("oT", [128, T])

        hid, tg = probs, probsT
        act_a = om[:, :, :].rearrange("p g n -> p (g n)")
        lg = sb("lg", [128, 8])
        sc8 = sb("sc8", [128, 8])
        top8 = sb("top8", [128, 8])
        idx8 = sb("idx8", [128, 8], U32)
        idxf = sb("idxf", [128, 8])
        oh = sb("oh", [128, 2, 8])
        cw = sb("cw", [128, 8])
        cwT = sb("cwT", [8, T])
        rt = sb("rt", [128, 8])
        grp8 = sb("grp8", [128, 8])
        place = sb("place", [128, 16])

        vaug = sb("vaug", [128, H, DH + 1])
        qk_ = sb("qk_", [128, 4, T])
        ktA = sb("ktA", [128, T])
        den16 = sb("den16", [128, H])
        o_tok = sb("o_tok", [128, D])

        u_half = sb("u_half", [128, 512])
        h2T = ktA
        gates = qk_[:, 0, :].rearrange("p (g b) -> p g b", g=4)
        cst = qk_[:, 1:3, :].rearrange("p a (g b) -> p (a g) b", g=4)

        mask_u8 = sb("mask_u8", [128, SK], U8)
        mask_add = x2_v[:, 0:SK]
        st3 = sb("st3", [128, NC, 6])
        mv3 = sb("mv3", [128, NC, 2])
        n3 = sb("n3", [128, 5, 2 * NC])
        qkv3 = qk_[:, 0:3, :].rearrange("p a t -> p (a t)")
        kl3T = qk_[:, 3, :]
        q3bd = x2_v[:, SK + 2 * T:SK + 4 * T].rearrange("p (h t) -> p h t", h=2)
        d3 = sb("d3", [128, 8])

        convp = x2_wkT[:, :, :].rearrange("p a c -> p (a c)")[:, 0:4 * B * SP].rearrange("p (j b l) -> p j b l", j=4, b=B)
        cbd = x2_v[:, SK:SK + 2 * T].rearrange("p (d t) -> p d t", d=2)
        dts = sb("dts", [128, 6, 8])

        banks = [ctx.enter_context(nc.psum_tensor(f"bank{i}", [128, 512], F32)) for i in range(8)]

        load = {n: sem("load_" + n) for n in
                ("early", "rows", "x", "ctxT", "ctxk", "late", "f0", "f1", "f2", "x2", "f3up", "f3gate", "f3down", "mask")}
        pool_set = sem("pool_set")
        pool_step = sem("pool_step")
        dve_step = sem("dve_step")
        act_step = sem("act_step")
        out_stored = sem("out_stored")

        xn_ready = sem("xn_ready")
        xnT_in_psum = sem("xnT_in_psum")
        xnT_ready = sem("xnT_ready")
        x_ready = sem("x_ready")
        y_full = sem("y_full")

        q_in_psum = sem("q_in_psum")
        qbd_ready = sem("qbd_ready")
        qw_in_psum = sem("qw_in_psum")
        qw_act = sem("qw_act")
        qw_dve = sem("qw_dve")
        scores_in_psum = sem("scores_in_psum")
        negmax_ready = sem("negmax_ready")
        clip_ready = sem("clip_ready")
        guard_read = sem("guard_read")
        probs_ready = sem("probs_ready")
        probsT_in_psum = sem("probsT_in_psum")
        probsT_ready = sem("probsT_ready")
        pc_in_psum = sem("pc_in_psum")
        pcn_ready = sem("pcn_ready")
        pcnT_in_psum = sem("pcnT_in_psum")
        pcnT_ready = sem("pcnT_ready")
        o_in_psum = sem("o_in_psum")
        o2_ready = sem("o2_ready")
        v_in_psum = sem("v_in_psum")
        v_ready = sem("v_ready")
        om_ready = sem("om_ready")
        oT_in_psum = sem("oT_in_psum")
        oT_ready = sem("oT_ready")
        nan_ready = sem("nan_ready")
        nan_in_psum = sem("nan_in_psum")
        mean_in_psum = sem("mean_in_psum")
        mean_ready = sem("mean_ready")

        logits_in_psum = sem("logits_in_psum")
        lneg_ready = sem("lneg_ready")
        lexp_ready = sem("lexp_ready")
        gate_in_psum = sem("gate_in_psum")
        up_in_psum = sem("up_in_psum")
        tanh_ready = sem("tanh_ready")
        hid_ready = sem("hid_ready")
        hid_act = sem("hid_act")
        y_in_psum = sem("y_in_psum")
        y_added = sem("y_added")
        cw_ready = sem("cw_ready")
        cwT_in_psum = sem("cwT_in_psum")
        cwT_ready = sem("cwT_ready")
        mix_pe = sem("mix_pe")
        mix_dve = sem("mix_dve")
        mix_act = sem("mix_act")
        c3_pe = sem("c3_pe")
        c3_dve = sem("c3_dve")
        c3_act = sem("c3_act")
        c3_pool = sem("c3_pool")

        LIN_PE, LIN_DVE = 8, 7
        CAU_PE, CAU_DVE = LIN_PE + 5, LIN_DVE + 5
        Y_BASE = {0: 0, 1: 8, 2: 15, 3: 22}
        QW_BANK = (6, 7, 4, 5)

        block = ctx.enter_context(nc.Block())

        class Steps:

            def __init__(self, engine, semaphore):
                self.engine, self.semaphore, self.n = engine, semaphore, 0

            def done(self, ins):
                ins.then_inc(self.semaphore, 1)
                self.n += 1
                self.engine.wait_ge(self.semaphore, self.n)

        class Count:

            def __init__(self):
                self.n = 0

        @block.sync
        def _(sp):
            sp.dma_start(early[:, :], dram["early"]).then_inc(load["early"], 16)
            sp.dma_start(x[:, :], dram["x"]).then_inc(load["x"], 16)
            sp.dma_start(ctxT[0:DC, :], dram["ctxT"]).then_inc(load["ctxT"], 16)
            sp.dma_start(ctxk[:, :, 0:DC], dram["ctxk"]).then_inc(load["ctxk"], 16)
            sp.dma_start(rows[:, :], dram["rows"].partition_broadcast(128)).then_inc(load["rows"], 16)
            sp.dma_start(late[:, :], dram["late"]).then_inc(load["late"], 16)
            sp.dma_start(f0_w1[:, :, :], dram["f0_w1"]).then_inc(load["f0"], 16)
            sp.dma_start(f0_w2[:, :, :], dram["f0_w2"]).then_inc(load["f0"], 16)
            sp.dma_start(f1_w13[:, :, :], dram["f1_w13"]).then_inc(load["f1"], 16)
            sp.dma_start(f1_w2[:, :, :], dram["f1_w2"]).then_inc(load["f1"], 16)
            for tile, name in ((x2_wq, "x2_wq"), (x2_wkT[:, :, :], "x2_wkT"), (x2_wv, "x2_wv"), (x2_wo, "x2_wo")):
                sp.dma_start(tile, dram[name]).then_inc(load["x2"], 16)
            for tile, name in ((f2_wg, "f2_wg"), (f2_wu, "f2_wu"), (f2_wd, "f2_wd")):
                sp.dma_start(tile[:, :, :], dram[name]).then_inc(load["f2"], 16)
            for b in range(B):
                sp.dma_start(mask_u8[b * S:(b + 1) * S, :],
                             dram["mask"][b:b + 1, :].partition_broadcast(S)).then_inc(load["mask"], 16)
            if STAGES >= 6:
                sp.wait_ge(y_in_psum, 2 * E)
                sp.dma_start(f3_wg[:, :, :], dram["f3_wg"]).then_inc(load["f3gate"], 16)
                sp.dma_start(f3_wu[0], dram["f3_wu"][:, 0:4, :]).then_inc(load["f3up"], 16)
            if STAGES >= 7:
                sp.wait_ge(y_full, 3)
                sp.dma_start(f3_wu[1], dram["f3_wu"][:, 4:8, :]).then_inc(load["f3up"], 16)
                for i in range(2):
                    sp.dma_start(f3_wd[i], dram["f3_wd"][:, 4 * i:4 * i + 4, :]).then_inc(load["f3down"], 16)
            sp.wait_ge(x_ready, STAGES)
            sp.dma_start(dram["out"], x[:, :]).then_inc(out_stored, 16)
            sp.wait_ge(out_stored, 16)

        @block.gpsimd
        def _(pool):
            n = Steps(pool, pool_set)
            n.done(pool.memset(ctxT[DC:CA, :], 1.0))
            n.done(pool.memset(mean_col[:, :], 1.0 / SK))
            n.done(pool.memset(ctxk[:, :, DC:CA], 1.0))
            n.done(pool.memset(vaug[:, :, DH:DH + 1], 1.0))
            n.done(pool.memset(grp8[:, :], -1.0))
            pool.wait_ge(load["late"], 16)
            n.done(pool.tensor_scalar(u_half[:, :], w("lstm_u"), 0.5, None, ALU.mult))
            if STAGES >= 3:
                pool.wait_ge(y_in_psum, E)
                n.done(pool.memset(q2bd, 0.0))
            if STAGES >= 4:
                st = Steps(pool, pool_step)
                pool.wait_ge(c3_dve, 1)
                st.done(pool.tensor_tensor(zc, ctxk[:, :, 0:DC], mv3[:, :, 0:1].to_broadcast([128, NC, DC]), ALU.subtract))
                pool.tensor_tensor(zc, zc, n3[:, 1, 0:NC].unsqueeze(2).to_broadcast([128, NC, DC]), ALU.mult).then_inc(c3_pool, 1)
            if STAGES >= 7:
                pool.wait_ge(c3_act, 12)
                pool.tensor_tensor(k3T[:, :].rearrange("p (k n) -> p k n", k=NC), kv3[:, :, 0:128], kv3[:, :, 0:128],
                                   ALU.mult).then_inc(c3_pool, 1)
                pool.wait_ge(c3_dve, 2)
                pool.wait_ge(c3_pool, 2)
                for h in range(H3):
                    pool.tensor_tensor(kv3[:, :, 64 * h:64 * h + 64], kv3[:, :, 64 * h:64 * h + 64],
                                       n3[:, 1, :].rearrange("p (k h) -> p k h", h=H3)[:, :, h:h + 1].to_broadcast([128, NC, D3]),
                                       ALU.mult).then_inc(c3_pool, 1)
                    pool.wait_ge(c3_pool, 3 + h)
                pool.wait_ge(load["mask"], 64)
                pool.wait_ge(y_full, 3)
                n.done(pool.tensor_scalar(mask_add, mask_u8[:, :], 1.0, BIG, ALU.subtract, ALU.mult))
                n.done(pool.memset(convp, 0.0))
                n.done(pool.memset(cbd, 0.0))
                n.done(pool.memset(q3bd, 0.0))

        SET_T, SET_C, SET_Q, SET_U, SET_Z, SET_L3 = 1, 3, 5, 6, 7, 11

        @block.scalar
        def _(act):
            st = Steps(act, act_step)

            def turn_norm(n):
                act.wait_ge(xnT_in_psum, n + 1)
                act.copy(xnT[:, :], banks[7][:, 0:T]).then_inc(xnT_ready, 1)

            def context_values(layer):
                for i in range(4):
                    act.wait_ge(v_in_psum, 4 * layer + i + 1)
                    act.copy(big_c[:, i * 512:i * 512 + 512], banks[3 + i][:, :]).then_inc(v_ready, 1)

            def context_attention(layer):
                K = CA if layer < 2 else DC
                if layer == 2:
                    act.wait_ge(q_in_psum, 3)
                    act.wait_ge(pool_set, SET_Z)
                    for half in range(2):
                        p = slice(64 * half, 64 * half + 64)
                        ins = act.activation(q2bd[p, 0:4, half, :], banks[0][p, :].rearrange("p (a t) -> p a t", a=4),
                                             ACT.Copy, scale=D2 ** -0.5)
                    ins.then_inc(qw_act, 1)
                for i in (0, 2):
                    act.wait_ge(qw_in_psum, 4 * layer + i + 1)
                    if layer < 2:
                        act.copy(big_b[0:K, i * 512:i * 512 + 512], banks[QW_BANK[i]][0:K, :]).then_inc(qw_act, 1)
                    else:
                        out = big_b[0:K, :].rearrange("p (b g h q) -> p g h b q", b=B, g=HG, h=4)[:, i]
                        act.copy(out, banks[QW_BANK[i]][0:K, :].rearrange("p (h b q) -> p h b q", h=4, b=B)).then_inc(qw_act, 1)
                g0 = NG * layer
                for i in range(NG + 6):
                    if i < NG:
                        g = g0 + i
                        if layer == 0:
                            act.wait_ge(clip_ready, g + 1)
                            if g >= 1:
                                act.wait_ge(guard_read, g)
                            act.activation(guard_out[:, :], banks[i % 2][:, :], ACT.Tanh,
                                           accum_out=nan_sum[:, i:i + 1]).then_inc(guard_read, 1)
                        act.wait_ge(negmax_ready, g + 1)
                        if g >= 2:
                            act.wait_ge(probsT_in_psum, g - 1)
                        src = clipped[:, i % 2, :] if layer == 0 else banks[i % 2][:, :]
                        act.activation(probs[:, i % 2, :], src, ACT.Exp, bias=negmax[:, i:i + 1],
                                       accum_out=den[:, i:i + 1]).then_inc(probs_ready, 1)
                    if layer == 0 and 1 <= i <= NG:
                        j = i - 1
                        act.wait_ge(probsT_in_psum, g0 + j + 1)
                        if j >= 2:
                            act.wait_ge(pc_in_psum, g0 + j - 1)
                        act.copy(probsT[:, j % 2, :], banks[2 + j % 2][:, :]).then_inc(probsT_ready, 1)
                    if layer == 2:
                        j = i - 4
                        if j >= 0 and j % 4 == 3 and j < NG:
                            hg = j // 4
                            act.wait_ge(pcnT_in_psum, j + 1)
                            act.copy(big_c[0:DC, hg * 512:hg * 512 + 512], banks[6][0:DC, :]).then_inc(pcnT_ready, 1)
                        j = i - 6
                        if j >= 0 and j % 4 == 3:
                            hg = j // 4
                            act.wait_ge(o_in_psum, hg + 1)
                            act.copy(o2T[:, 2 * hg:2 * hg + 2, :],
                                     banks[7][:, 0:256].rearrange("p (a t) -> p a t", a=2)).then_inc(o2_ready, 1)

            def feed_forward(layer):
                e0 = E * layer
                C = FFN_CHUNKS[layer] * 128
                k = {0: 0, 1: 1, 3: 2}.get(layer)
                for e in range(E):
                    n = e0 + e
                    if e == (1 if layer else 0) and k is not None:
                        act.wait_ge(lneg_ready, k + 1)
                        act.activation(sc8[:, :], lg[:, :], ACT.Exp, bias=rt[:, 0:1],
                                       accum_out=rt[:, 1:2]).then_inc(lexp_ready, 1)
                    if layer == 0:
                        act.wait_ge(gate_in_psum, n + 1)
                        if e >= 2:
                            act.wait_ge(y_in_psum, n - 1)
                        act.activation(hid[:, e % 2, 0:T], banks[e % 2][:, 0:T], ACT.Relu,
                                       bias=w("f0_b1", 128, 2 * e, 2 * e + 1)).then_inc(hid_act, 1)
                    else:
                        act.wait_ge(gate_in_psum, n + 1)
                        if e >= 2:
                            act.wait_ge(hid_ready, n - 1)
                        act.activation(tg[:, e % 2, 0:C], banks[e % 2][:, 0:C], ACT.Tanh, scale=0.5).then_inc(tanh_ready, 1)

            def linear_attention():
                act.wait_ge(mix_pe, 1)
                act.copy(vaug[:, :, 0:DH], banks[2][:, 0:D].rearrange("p (h d) -> p h d", h=H)).then_inc(mix_act, 1)

            def causal_attention():
                act.wait_ge(mix_pe, LIN_PE + 1)
                act.copy(o_tok[:, :], banks[4][:, 0:D]).then_inc(mix_act, 1)
                act.wait_ge(mix_dve, LIN_DVE + 3)
                act.activation(s_sb[:, :, :], s_sb[:, :, :], ACT.Exp).then_inc(mix_act, 1)

            def lstm():
                for t in range(B):
                    act.wait_ge(mix_pe, CAU_PE + 1 + t)
                    g = banks[0][:, t * 128:(t + 1) * 128]
                    act.activation(gates[:, 0:3, :], g[:, 0:96].rearrange("p (g b) -> p g b", g=3), ACT.Tanh, scale=0.5)
                    act.activation(gates[:, 3, :], g[:, 96:128], ACT.Tanh).then_inc(mix_act, 1)
                    act.wait_ge(mix_dve, CAU_DVE + 2 * t + 1)
                    act.activation(cst[:, 3, :], cst[:, 2, :], ACT.Tanh, scale=0.5).then_inc(mix_act, 1)

            def context3_turned():
                act.wait_ge(load["late"], 16)
                for i in range(4):
                    act.wait_ge(c3_pe, i + 1)
                    act.activation(big_c[0:DC, i * 512:i * 512 + 512], banks[3 + i][0:DC, :], ACT.Identity,
                                   bias=w("x3_b", DC), scale=w("x3_g", DC)).then_inc(c3_act, 1)

            def context3_kv(first, last):
                for i in range(first, last):
                    act.wait_ge(c3_pe, 4 + i + 1)
                    act.copy(kv3[:, 2 * i:2 * i + 2, :],
                             banks[3 + i % 4][:, :].rearrange("p (a n) -> p a n", a=2)).then_inc(c3_act, 1)

            def context3_keys():
                for i in range(4):
                    act.wait_ge(c3_pe, 12 + i + 1)
                    act.copy(k3T[:, i * 512:i * 512 + 512], banks[3 + i][:, :]).then_inc(c3_act, 1)

            def cross3():
                act.wait_ge(c3_pe, 16 + 1)
                act.copy(qkv3, banks[0][:, 0:384]).then_inc(c3_act, 1)
                act.wait_ge(c3_dve, 5 + 5)
                for h in range(H3):
                    act.activation(big_a[:, h * 640:h * 640 + 640], big_a[:, h * 640:h * 640 + 640], ACT.Exp,
                                   bias=d3[:, h:h + 1], accum_out=d3[:, 2 + h:3 + h]).then_inc(c3_act, 1)
                act.wait_ge(c3_pe, 16 + 4)
                act.copy(big_b[:, 0:512], banks[0][:, :]).then_inc(c3_act, 1)
                act.wait_ge(c3_pe, 16 + 6)
                act.copy(big_b[:, 1024:1280], banks[2][:, 0:256]).then_inc(c3_act, 1)

            def state_space():
                a0 = ACT0
                act.wait_ge(mix_dve, DV0 + 1)
                st.done(act.activation(dts[:, 1, :], dts[:, 0, :], ACT.Abs))
                act.activation(dts[:, 1, :], dts[:, 1, :], ACT.Exp, scale=-1.0).then_inc(mix_act, 1)
                act.activation(dts[:, 5, 0:4], row("alog"), ACT.Exp).then_inc(mix_act, 1)
                act.wait_ge(mix_act, a0 + 1)
                act.activation(dts[:, 2, :], dts[:, 1, :], ACT.Ln, bias=1.0).then_inc(mix_act, 1)
                act.wait_ge(mix_pe, PE0 + 2)
                act.activation(big_c[:, 0:256], banks[1][:, 0:256], ACT.Tanh, scale=0.5).then_inc(mix_act, 1)
                act.wait_ge(mix_dve, DV0 + 3)
                act.activation(big_b[:, 512:1024], big_b[:, 0:512], ACT.Tanh).then_inc(mix_act, 1)
                for i in range(2):
                    act.wait_ge(mix_pe, PE0 + 3 + i)
                    act.activation(big_a[:, 1024 + 512 * i:1536 + 512 * i], banks[2 + i][:, :], ACT.Exp,
                                   scale=-1.0).then_inc(mix_act, 1)

            ACT0, DV0, PE0 = 3 + 2 * B, CAU_DVE + 2 * B, CAU_PE + B + 1

            act.wait_ge(load["early"], 16)
            context_values(0)
            turn_norm(0)
            context_attention(0)
            if STAGES >= 2:
                turn_norm(1); linear_attention()
            if STAGES >= 3:
                context_values(1)
                turn_norm(2); feed_forward(0)
            if STAGES >= 4:
                turn_norm(3); context_attention(1)
            if STAGES >= 5:
                context3_turned()
                turn_norm(4); causal_attention()
            if STAGES >= 6:
                context3_kv(0, 4)
                turn_norm(5); feed_forward(1)
            if STAGES >= 7:
                context3_kv(4, 8)
                turn_norm(6); context_attention(2)
            if STAGES >= 8:
                turn_norm(7); lstm()
            if STAGES >= 9:
                context3_keys()
                turn_norm(8); feed_forward(2)
            if STAGES >= 10:
                cross3()
            if STAGES >= 11:
                turn_norm(9); state_space()
            if STAGES >= 12:
                turn_norm(10); feed_forward(3)

        @block.tensor
        def _(pe):
            def turn_norm(n):
                pe.wait_ge(xn_ready, n + 1)
                pe.transpose(banks[7][:, 0:T], xn[:, :], ident).then_inc(xnT_in_psum, 1)
                pe.wait_ge(xnT_ready, n + 1)

            def context_values(layer):
                for i in range(4):
                    for c in range(4):
                        k = 4 * i + c
                        ins = pe.matmul(banks[3 + i][:, c * 128:(c + 1) * 128], ctxT[:, k * 128:(k + 1) * 128], w(f"wv{layer}", CA),
                                        start=True, stop=True)
                    ins.then_inc(v_in_psum, 1)

            def context_attention(layer):
                K = CA if layer < 2 else DC
                g0 = NG * layer
                if layer < 2:
                    wq, wkT, wo = (w(f"{n}{layer}") for n in ("wq", "wkT", "wo"))
                    pe.matmul(banks[2][:, 0:T], wq, xnT[:, :], start=True, stop=True).then_inc(q_in_psum, 1)
                    if layer == 0:
                        pe.wait_ge(load["ctxk"], 16)
                        pe.wait_ge(pool_set, SET_C)
                        pe.wait_ge(v_ready, 4)
                        for b in range(B):
                            for c in range(CK):
                                ins = pe.matmul(banks[3][0:CA, b:b + 1], ctxk[:, b * CK + c, :], mean_col[:, :],
                                                start=c == 0, stop=c == CK - 1)
                        ins.then_inc(mean_in_psum, 1)
                    for b in range(B):
                        pe.wait_ge(qbd_ready, B * layer + b + 1)
                        pe.matmul(banks[QW_BANK[b]][0:CA, :], wkT, big_a[:, b * 512:b * 512 + 512],
                                  start=True, stop=True).then_inc(qw_in_psum, 1)
                    if layer == 0:
                        pe.wait_ge(mean_ready, 1)
                        pe.matmul(banks[3][:, 8:8 + B], w("wv0", CA), mean_cT[:, :], start=True, stop=True).then_inc(mean_in_psum, 1)
                else:
                    pe.wait_ge(load["x2"], 64)
                    for p in range(8):
                        ins = pe.matmul(banks[p // 4][:, (p % 4) * 128:(p % 4) * 128 + 128], x2_wq[:, p * 128:(p + 1) * 128],
                                        xnT[:, :], start=True, stop=True)
                        if p % 4 == 3:
                            ins.then_inc(q_in_psum, 1)
                    for p in range(8):
                        if p == 0:
                            pe.wait_ge(qw_act, 4 + 1)
                        if p == 4:
                            pe.wait_ge(qw_dve, 4 + 1)
                        ins = pe.matmul(banks[QW_BANK[p // 2]][0:DC, (p % 2) * 256:(p % 2) * 256 + 256], x2_wkT[:, p, :],
                                        q2bd[:, p, :, :], start=True, stop=True)
                        if p % 2:
                            ins.then_inc(qw_in_psum, 1)

                def group(i):
                    return (i // HG, i % HG) if layer < 2 else (i % B, i // B)

                def scores(i):
                    b, hg = group(i)
                    if i % 4 == 0:
                        k = i // 4
                        if k % 2 == 0:
                            pe.wait_ge(qw_act, 2 * layer + layer // 2 + k // 2 + 1)
                        else:
                            pe.wait_ge(qw_dve, 2 * layer + layer // 2 + k // 2 + 1)
                    if i >= 2:
                        if layer == 0:
                            pe.wait_ge(guard_read, g0 + i - 1)
                        else:
                            pe.wait_ge(probs_ready, g0 + i - 1)
                    k = b * HG + hg
                    pe.matmul(banks[i % 2][:, :], big_b[0:K, k * 128:(k + 1) * 128], ctxT[0:K, b * SK:(b + 1) * SK],
                              start=True, stop=True).then_inc(scores_in_psum, 1)

                def turn_probs(i):
                    pe.wait_ge(probs_ready, g0 + i + 1)
                    if i >= 2:
                        pe.wait_ge(probsT_ready, g0 + i - 1)
                    for c in range(CK):
                        ins = pe.transpose(banks[2 + i % 2][:, c * 128:(c + 1) * 128], probs[:, i % 2, c * 128:(c + 1) * 128], ident)
                    ins.then_inc(probsT_in_psum, 1)

                def weighted(i):
                    b, hg = group(i)
                    pe.wait_ge(probsT_ready, g0 + i + 1)
                    if i == 0:
                        pe.wait_ge(qw_act, 2 * layer + layer // 2 + 2)
                        pe.wait_ge(qw_dve, 2 * layer + layer // 2 + 2)
                        if layer < 2:
                            pe.wait_ge(v_ready, 4 * layer + 4)
                    if i >= 2:
                        if layer < 2:
                            pe.wait_ge(om_ready, g0 + i - 1)
                        else:
                            pe.wait_ge(pcn_ready, i - 1)
                    for c in range(CK):
                        k = b * CK + c
                        rhs = ctxk[:, k, 0:DC] if layer == 2 else big_c[:, k * D + 32 * hg:k * D + 32 * hg + 32]
                        ins = pe.matmul(banks[4 + i % 2][:, 0:DC if layer == 2 else 32], probsT[:, i % 2, c * 128:(c + 1) * 128],
                                        rhs, start=c == 0, stop=c == CK - 1)
                    ins.then_inc(pc_in_psum, 1)

                def fold(b):
                    pe.wait_ge(om_ready, g0 + HG * (b + 1))
                    ins = pe.matmul(banks[6][:, b * S:(b + 1) * S], om[:, b * HG:(b + 1) * HG, :], w("fold"), start=True, stop=True)
                    if b == B - 1:
                        ins.then_inc(oT_in_psum, 1)

                def turn_weighted(i):
                    b, hg = group(i)
                    pe.wait_ge(pcn_ready, i + 1)
                    if b == 0 and hg >= 1:
                        pe.wait_ge(pcnT_ready, hg)
                    pe.transpose(banks[6][0:DC, b * 128:b * 128 + 128], pcn[:, i % 2, 0:DC], ident).then_inc(pcnT_in_psum, 1)

                def values(hg):
                    pc = big_c[0:DC, hg * 512:(hg + 1) * 512].rearrange("p (b h q) -> p h b q", b=B, h=4)
                    pe.wait_ge(pcnT_ready, hg + 1)
                    if hg:
                        pe.wait_ge(o2_ready, hg)
                    for k in range(4):
                        h = 4 * hg + k
                        ins = pe.matmul(banks[7][64 * (k % 2):64 * (k % 2) + 64, (k // 2) * 128:(k // 2) * 128 + 128],
                                        x2_wv[:, h * D2:(h + 1) * D2], pc[:, k], start=True, stop=True)
                    ins.then_inc(o_in_psum, 1)

                for i in range(NG + 3 if layer < 2 else NG + 5):
                    if i < NG:
                        scores(i)
                    if 1 <= i <= NG:
                        turn_probs(i - 1)
                    if 2 <= i <= NG + 1:
                        weighted(i - 2)
                    if layer == 0 and i == NG + 1:
                        pe.wait_ge(nan_ready, 1)
                        pe.matmul(banks[7][:, 0:NG], w("ones"), nan_hit[:, :], start=True, stop=True).then_inc(nan_in_psum, 1)
                    if layer < 2 and i >= 3 and (i - 3) % 4 == 3:
                        fold((i - 3) // 4)
                    if layer == 2 and 3 <= i <= NG + 2:
                        turn_weighted(i - 3)
                    if layer == 2 and i >= 5 and (i - 5) % 4 == 3:
                        values((i - 5) // 4)
                if layer < 2:
                    pe.wait_ge(oT_ready, layer + 1)
                    pe.matmul(banks[2][:, 0:D], oT[:, :], wo, start=True, stop=True).then_inc(y_full, 1)
                else:
                    for p in range(8):
                        if p % 2 == 0:
                            pe.wait_ge(o2_ready, p // 2 + 1)
                        ins = pe.matmul(banks[2][:, 0:D], o2T[:, p, :], x2_wo[:, p, :], start=p == 0, stop=p == 7)
                    ins.then_inc(y_full, 1)

            def feed_forward(layer):
                e0 = E * layer
                C = FFN_CHUNKS[layer]
                pe.wait_ge(load["late"], 16)
                pe.matmul(banks[7][:, 256:264], xnT[:, :], w(f"f{layer}_wr"), start=True, stop=True).then_inc(logits_in_psum, 1)
                if layer == 0:
                    pe.wait_ge(load["f0"], 32)
                elif layer == 1:
                    pe.wait_ge(load["f1"], 32)
                elif layer == 2:
                    pe.wait_ge(load["f2"], 48)
                else:
                    pe.wait_ge(load["f3up"], 32)
                    pe.wait_ge(load["f3gate"], 16)
                    pe.wait_ge(load["f3down"], 32)

                def gate_w(e, c):
                    if layer == 1:
                        return f1_w13[:, e, c * 128:(c + 1) * 128]
                    return (f2_wg if layer == 2 else f3_wg)[:, e, c * 128:(c + 1) * 128]

                def up_w(e, c):
                    if layer == 1:
                        return f1_w13[:, e, 256 + c * 128:256 + (c + 1) * 128]
                    return (f2_wu[:, e, :] if layer == 2 else f3_wu[e // 4][:, e % 4, :])[:, c * 128:(c + 1) * 128]

                def down_w(e, c):
                    if layer == 3:
                        return f3_wd[e // 4][:, e % 4, c * 128:(c + 1) * 128]
                    return {0: f0_w2, 1: f1_w2, 2: f2_wd}[layer][:, e, c * 128:(c + 1) * 128]

                def up(e):
                    n = e0 + e
                    if e >= 2:
                        pe.wait_ge(hid_ready, n - 1)
                        if layer == 0:
                            pe.wait_ge(hid_act, n - 1)
                    if layer == 0:
                        pe.matmul(banks[e % 2][:, 0:T], f0_w1[:, e, 0:128], xnT[:, :], start=True, stop=True).then_inc(gate_in_psum, 1)
                        pe.matmul(banks[2 + e % 2][:, 0:T], f0_w1[:, e, 128:256], xnT[:, :], start=True, stop=True).then_inc(up_in_psum, 1)
                        return
                    for wt, bank, s in ((gate_w, banks[e % 2], gate_in_psum), (up_w, banks[2 + e % 2], up_in_psum)):
                        for c in range(C):
                            ins = pe.matmul(bank[:, c * T:(c + 1) * T], wt(e, c), xnT[:, :], start=True, stop=True)
                        ins.then_inc(s, 1)

                def down(e):
                    n = e0 + e
                    pe.wait_ge(hid_ready, n + 1)
                    if layer == 0:
                        pe.wait_ge(hid_act, n + 1)
                    if e >= 3:
                        pe.wait_ge(y_added, Y_BASE[layer] + e - 2)
                    for c in range(C):
                        ins = pe.matmul(banks[4 + e % 3][:, 0:D], hid[:, e % 2, c * T:(c + 1) * T], down_w(e, c),
                                        start=c == 0, stop=c == C - 1)
                    ins.then_inc(y_in_psum, 1)

                for e in range(E + 1):
                    if e < E:
                        up(e)
                    if e >= 1:
                        down(e - 1)
                    if layer == 3 and e == 2:
                        pe.wait_ge(cw_ready, 2)
                        pe.matmul(banks[7][:, 0:16], w("cum"), oh[:, :, :], start=True, stop=True).then_inc(cwT_in_psum, 1)
                if layer == 0:
                    pe.wait_ge(cw_ready, 1)
                    pe.transpose(banks[7][0:8, 0:T], cw[:, :], ident).then_inc(cwT_in_psum, 1)
                    pe.wait_ge(cwT_ready, 1)
                    pe.matmul(banks[7][:, 256:256 + D], cwT[:, :], w("f0_b2", 8), start=True, stop=True).then_inc(cwT_in_psum, 1)

            def linear_attention():
                pe.wait_ge(load["late"], 16)
                pe.matmul(banks[0][:, 0:T], w("a_wq"), xnT[:, :], start=True, stop=True)
                pe.matmul(banks[1][:, 0:T], w("a_wk"), xnT[:, :], start=True, stop=True)
                pe.matmul(banks[2][:, 0:D], xnT[:, :], w("a_wv"), start=True, stop=True).then_inc(mix_pe, 1)
                pe.wait_ge(mix_dve, 1)
                for i in range(4):
                    pe.matmul(banks[3 + i][:, :], ktA[:, :], big_a[:, i * 512:i * 512 + 512],
                              start=True, stop=True).then_inc(mix_pe, 1)
                pe.wait_ge(mix_act, 1)
                pe.wait_ge(pool_set, SET_Q)
                for i in range(4):
                    pe.wait_ge(mix_dve, 2 + i)
                    for h in range(4 * i, 4 * i + 4):
                        ins = pe.matmul(banks[0][:, h * 9:h * 9 + 9], big_b[:, h * T:(h + 1) * T], vaug[:, h, :],
                                        start=True, stop=True)
                ins.then_inc(mix_pe, 1)
                pe.wait_ge(mix_dve, 6)
                pe.transpose(banks[1][:, 0:T], o_tok[:, :], ident).then_inc(mix_pe, 1)
                pe.wait_ge(mix_dve, 7)
                pe.matmul(banks[2][:, 0:D], oT[:, :], w("a_wo"), start=True, stop=True).then_inc(mix_pe, 1)

            def causal_attention():
                for i, (name, a) in enumerate((("r_wq", 0), ("r_wq", 128), ("r_wk", 0), ("r_wk", 128))):
                    pe.matmul(banks[i][:, 0:T], w(name, 128, a, a + 128), xnT[:, :], start=True, stop=True)
                pe.matmul(banks[4][:, 0:D], xnT[:, :], w("r_wv"), start=True, stop=True).then_inc(mix_pe, 1)
                pe.wait_ge(mix_dve, LIN_DVE + 1)
                for b in range(B):
                    ins = pe.matmul(banks[5][b * S:(b + 1) * S, :], qT[:, b * S:(b + 1) * S],
                                    big_a[:, b * 512:(b + 1) * 512], start=True, stop=True)
                ins.then_inc(mix_pe, 1)
                pe.wait_ge(mix_dve, LIN_DVE + 4)
                pe.wait_ge(mix_act, 2)
                for h in range(H):
                    ins = pe.matmul(banks[0][:, h * DH:(h + 1) * DH], big_b[:, h * T:(h + 1) * T],
                                    o_tok[:, h * DH:(h + 1) * DH], start=True, stop=True)
                ins.then_inc(mix_pe, 1)
                pe.wait_ge(mix_dve, LIN_DVE + 5)
                pe.transpose(banks[1][:, 0:T], z2[:, :], ident).then_inc(mix_pe, 1)
                pe.wait_ge(oT_ready, 3)
                pe.matmul(banks[2][:, 0:D], oT[:, :], w("r_wo"), start=True, stop=True).then_inc(mix_pe, 1)

            def lstm():
                pe.wait_ge(pool_set, SET_U)
                pe.wait_ge(load["rows"], 16)
                g = banks[0][:, :].rearrange("p (t g b) -> p g t b", t=B, g=4)
                for k in range(4):
                    pe.matmul(g[:, k], row("lstm_b", k * 128, k * 128 + 128, 1), w("ones", 1),
                              start=k == 0, stop=False, skip_group_check=True)
                for k in range(4):
                    ins = pe.matmul(g[:, k], w("lstm_w", 128, k * 128, k * 128 + 128), xnT[:, :],
                                    start=False, stop=k == 3, skip_group_check=True)
                ins.then_inc(mix_pe, 1)
                for t in range(1, B):
                    pe.wait_ge(mix_dve, CAU_DVE + 2 * t)
                    for k in range(4):
                        ins = pe.matmul(banks[0][:, t * 128 + k * S:t * 128 + (k + 1) * S], u_half[:, k * 128:(k + 1) * 128],
                                        h2T[:, (t - 1) * S:t * S], start=False, stop=True, skip_group_check=True)
                    ins.then_inc(mix_pe, 1)
                pe.wait_ge(mix_dve, CAU_DVE + 2 * B)
                pe.transpose(banks[1][:, 0:D], h2T[:, :], ident).then_inc(mix_pe, 1)

            def context3_turned():
                pe.wait_ge(c3_pool, 1)
                for i in range(4):
                    for c in range(4):
                        ins = pe.transpose(banks[3 + i][0:DC, c * 128:(c + 1) * 128], zc[:, 4 * i + c, :], ident)
                    ins.then_inc(c3_pe, 1)

            def context3_kv(first, last):
                for i in range(first, last):
                    pe.wait_ge(c3_act, 4 + max(i - 3, 0))
                    if i == 5:
                        pe.wait_ge(y_added, Y_BASE[2])
                    if i == 6:
                        pe.wait_ge(x_ready, 6)
                    for c in range(2):
                        k = 2 * i + c
                        ins = pe.matmul(banks[3 + i % 4][:, c * 256:(c + 1) * 256], big_c[0:DC, k * 128:(k + 1) * 128],
                                        w("x3_wkv", DC), start=True, stop=True)
                    ins.then_inc(c3_pe, 1)

            def context3_keys():
                pe.wait_ge(c3_pool, 4)
                for i in range(4):
                    for c in range(4):
                        ins = pe.transpose(banks[3 + i][:, c * 128:(c + 1) * 128], kv3[:, 4 * i + c, 0:128], ident)
                    ins.then_inc(c3_pe, 1)

            def cross3():
                pe.wait_ge(c3_dve, 3)
                pe.transpose(banks[7][:, 0:T], z2[:, :], ident).then_inc(q_in_psum, 1)
                pe.wait_ge(c3_dve, 4)
                pe.wait_ge(c3_act, 16)
                pe.matmul(banks[0][:, 0:384], xnT[:, :], w("x3_wqkv"), start=True, stop=True).then_inc(c3_pe, 1)
                pe.wait_ge(c3_dve, 5)
                pe.transpose(banks[1][:, 0:T], xn[:, :], ident)
                pe.transpose(banks[2][:, 0:T], z2[:, :], ident).then_inc(c3_pe, 1)
                pe.wait_ge(c3_dve, 6)
                for h in range(H3):
                    for b in range(B):
                        pe.matmul(banks[3 + h][b * S:(b + 1) * S, :], q3bd[:, h, b * S:(b + 1) * S],
                                  k3T[:, b * SK:(b + 1) * SK], start=True, stop=True)
                for h in range(H3):
                    ins = pe.matmul(banks[5][:, h * T:(h + 1) * T], q3bd[:, h, :], kl3T, start=True, stop=True)
                ins.then_inc(c3_pe, 1)
                for h in range(H3):
                    pe.wait_ge(c3_dve, 11 + h)
                    for c in range(4):
                        ins = pe.transpose(banks[h][:, c * 128:(c + 1) * 128],
                                           big_a[:, h * 640 + c * 128:h * 640 + (c + 1) * 128], ident)
                    ins.then_inc(c3_pe, 1)
                for h in range(H3):
                    ins = pe.transpose(banks[2][:, h * T:(h + 1) * T], big_a[:, h * 640 + 512:h * 640 + 640], ident)
                ins.then_inc(c3_pe, 1)
                pe.wait_ge(c3_act, 21)
                pe.wait_ge(c3_dve, 13)
                for h in range(H3):
                    p = slice(64 * h, 64 * h + 64)
                    pe.matmul(banks[6][p, 0:T], qkv3[:, 256 + 64 * h:320 + 64 * h], big_b[:, 1024 + h * T:1024 + (h + 1) * T],
                              start=True, stop=False, skip_group_check=True)
                    for b in range(B):
                        for c in range(CK):
                            ins = pe.matmul(banks[6][p, b * S:(b + 1) * S], kv3[:, b * CK + c, 128 + 64 * h:192 + 64 * h],
                                            big_b[:, h * 512 + c * 128 + b * S:h * 512 + c * 128 + (b + 1) * S],
                                            start=False, stop=c == CK - 1, skip_group_check=True)
                ins.then_inc(c3_pe, 1)
                pe.wait_ge(c3_dve, 14)
                pe.matmul(banks[0][:, 0:D], oT[:, :], w("x3_wo"), start=True, stop=True).then_inc(y_full, 1)

            def state_space():
                m = 13 + B + 1
                pe.matmul(banks[7][:, 256:264], xnT[:, :], w("m_in", 128, 768, 776), start=True, stop=True)
                for j in range(4):
                    ins = pe.matmul(banks[0][:, j * T:(j + 1) * T], w("m_in", 128, 256 + j * 128, 384 + j * 128), xnT[:, :],
                                    start=True, stop=True)
                ins.then_inc(mix_pe, 1)
                pe.matmul(banks[1][:, 0:256], xnT[:, :], w("m_in", 128, 0, 256), start=True, stop=True).then_inc(mix_pe, 1)
                pe.wait_ge(mix_dve, CAU_DVE + 2 * B + 4)
                for i, name in enumerate(("l_fw", "l_bw")):
                    pe.matmul(banks[2 + i][:, :], w(name), big_a[:, i * 512:i * 512 + 512], start=True, stop=True).then_inc(mix_pe, 1)
                pe.wait_ge(mix_dve, CAU_DVE + 2 * B + 5)
                for j in range(2):
                    pe.transpose(banks[4][:, j * 128:(j + 1) * 128], big_b[:, 1024 + j * 128:1024 + (j + 1) * 128], ident)
                for j in range(2):
                    pe.matmul(banks[6][:, 0:4], big_b[:, 1024 + j * 128:1024 + (j + 1) * 128], w("m_fc", 128, 4 * j, 4 * j + 4),
                              start=j == 0, stop=j == 1)
                pe.wait_ge(mix_dve, CAU_DVE + 2 * B + 6)
                pe.matmul(banks[5][:, 0:256], big_b[:, 1280:1408], cbd, start=True, stop=True).then_inc(mix_pe, 1)
                pe.wait_ge(mix_dve, CAU_DVE + 2 * B + 7)
                for h in range(NH):
                    for d in range(2):
                        ins = pe.matmul(banks[0][:, h * 64:(h + 1) * 64],
                                        big_a[:, 1024 + d * 512 + h * T:1024 + d * 512 + (h + 1) * T],
                                        big_c[:, 256 + h * 64:256 + (h + 1) * 64], start=d == 0, stop=d == 1)
                ins.then_inc(mix_pe, 1)
                pe.wait_ge(mix_dve, CAU_DVE + 2 * B + 8)
                for j in range(2):
                    ins = pe.transpose(banks[1][:, j * 128:(j + 1) * 128], big_c[:, 1024 + j * 128:1024 + (j + 1) * 128], ident)
                ins.then_inc(mix_pe, 1)
                pe.wait_ge(mix_dve, CAU_DVE + 2 * B + 9)
                for j in range(2):
                    ins = pe.matmul(banks[2][:, 0:D], big_c[:, 1280 + j * 128:1280 + (j + 1) * 128],
                                    w("m_out", 128, j * 128, (j + 1) * 128), start=j == 0, stop=j == 1)
                ins.then_inc(mix_pe, 1)

            pe.wait_ge(load["early"], 16)
            pe.wait_ge(load["ctxT"], 16)
            pe.wait_ge(pool_set, SET_T)
            context_values(0)
            turn_norm(0)
            context_attention(0)
            if STAGES >= 2:
                turn_norm(1); linear_attention()
            if STAGES >= 3:
                context_values(1)
                turn_norm(2); feed_forward(0)
            if STAGES >= 4:
                turn_norm(3); context_attention(1)
            if STAGES >= 5:
                context3_turned()
                turn_norm(4); causal_attention()
            if STAGES >= 6:
                context3_kv(0, 4)
                turn_norm(5); feed_forward(1)
            if STAGES >= 7:
                context3_kv(4, 8)
                turn_norm(6); context_attention(2)
            if STAGES >= 8:
                turn_norm(7); lstm()
            if STAGES >= 9:
                context3_keys()
                turn_norm(8); feed_forward(2)
            if STAGES >= 10:
                cross3()
            if STAGES >= 11:
                turn_norm(9); state_space()
            if STAGES >= 12:
                turn_norm(10); feed_forward(3)

        @block.vector
        def _(v):
            st = Steps(v, dve_step)

            NEWTON = (64.0, 16.0, 4.0)

            def rsqrt_step(k, y, a, t):
                if k == 0:
                    return v.tensor_single_scalar(t.bitcast(U32), a.bitcast(U32), 1, op=ALU.logical_shift_right)
                if k == 1:
                    return v.tensor_scalar(y.bitcast(I32), t.bitcast(I32), -1.0, RSQRT_MAGIC, ALU.mult, ALU.add)
                if k % 3 == 2:
                    return v.tensor_tensor(t, y, y, ALU.mult)
                if k % 3 == 0:
                    return v.scalar_tensor_tensor(out=t, in0=t, scalar=NEWTON[k // 3 - 1], in1=a, op0=ALU.mult, op1=ALU.mult)
                return v.scalar_tensor_tensor(out=y, in0=t, scalar=3.0, in1=y, op0=ALU.subtract, op1=ALU.mult)

            def rsqrt(y, a, t):
                for k in range(11):
                    st.done(rsqrt_step(k, y, a, t))

            def rsqrt_column():
                a, y, t = nw[:, 0:1], nw[:, 1:2], nw[:, 2:3]
                v.tensor_single_scalar(t.bitcast(U32), a.bitcast(U32), 1, op=ALU.logical_shift_right).then_inc(dve_step, 1)
                st.n += 1
                for k, c in enumerate(NEWTON):
                    ins = v.tensor_scalar(nw[:, 3 + k:4 + k], a, c, None, ALU.mult)
                v.wait_ge(dve_step, st.n)
                st.done(v.tensor_scalar(y.bitcast(I32), t.bitcast(I32), -1.0, RSQRT_MAGIC, ALU.mult, ALU.add))
                for k in range(3):
                    st.done(v.scalar_tensor_tensor(out=t, in0=y, scalar=y, in1=nw[:, 3 + k:4 + k], op0=ALU.mult, op1=ALU.mult))
                    st.done(v.scalar_tensor_tensor(out=y, in0=t, scalar=3.0, in1=y, op0=ALU.subtract, op1=ALU.mult))

            def layer_norm(out, src):
                st.done(v.bn_stats(stats[:, :], src))
                st.done(v.bn_aggr(mv[:, :], stats[:, :]))
                st.done(v.tensor_scalar(nw[:, 0:1], mv[:, 1:2], LN_EPS, None, ALU.add))
                rsqrt_column()
                return v.tensor_scalar(out, src, mv[:, 0:1], nw[:, 1:2], ALU.subtract, ALU.mult)

            def norm(n):
                if n:
                    v.wait_ge(x_ready, n)
                layer_norm(xn[:, :], x[:, :]).then_inc(xn_ready, 1)

            def context_attention(layer):
                K = CA if layer < 2 else DC
                g0 = NG * layer

                def bring(i):
                    v.wait_ge(qw_in_psum, 4 * layer + i + 1)
                    if layer < 2:
                        v.tensor_copy(big_b[0:K, i * 512:i * 512 + 512], banks[QW_BANK[i]][0:K, :]).then_inc(qw_dve, 1)
                    else:
                        out = big_b[0:K, :].rearrange("p (b g h q) -> p g h b q", b=B, g=HG, h=4)[:, i]
                        v.tensor_copy(out, banks[QW_BANK[i]][0:K, :].rearrange("p (h b q) -> p h b q", h=4, b=B)).then_inc(qw_dve, 1)

                if layer < 2:
                    v.wait_ge(q_in_psum, layer + 1)
                    st.done(v.tensor_scalar(qT[:, :], banks[2][:, 0:T], w(f"bq{layer}"), DH ** -0.5, ALU.add, ALU.mult))
                    for b in range(B):
                        v.tensor_tensor(big_a[:, b * 512:b * 512 + 512].rearrange("p (h q) -> p h q", h=H),
                                        qT[:, b * S:(b + 1) * S].unsqueeze(1).to_broadcast([128, H, S]),
                                        w("head16").unsqueeze(2).to_broadcast([128, H, S]), ALU.mult).then_inc(qbd_ready, 1)
                    if layer == 0:
                        v.wait_ge(mean_in_psum, 1)
                        v.tensor_copy(mean_cT[:, :], banks[3][0:CA, 0:B]).then_inc(mean_ready, 1)
                else:
                    v.wait_ge(q_in_psum, 4)
                    v.wait_ge(pool_set, SET_Z)
                    for half in range(2):
                        p = slice(64 * half, 64 * half + 64)
                        ins = v.tensor_scalar(q2bd[p, 4:8, half, :], banks[1][p, :].rearrange("p (a t) -> p a t", a=4),
                                              D2 ** -0.5, None, ALU.mult)
                    ins.then_inc(qw_dve, 1)
                bring(1)
                bring(3)
                if layer == 0:
                    v.wait_ge(mean_in_psum, 2)
                    st.done(v.tensor_copy(mean_vT[:, :], banks[3][:, 8:8 + B]))
                    v.wait_ge(load["rows"], 16)
                st.done(v.tensor_tensor(xb[:, :], x[:, :], row(f"bo{layer}"), ALU.add))

                def context3_share(i):
                    if layer == 0:
                        if i < NG:
                            st.done(v.bn_stats(st3[:, i, :], ctxk[:, i, 0:DC]))
                            v.bn_aggr(mv3[:, i, :], st3[:, i, :])
                    elif layer == 1:
                        if i == 0:
                            st.done(v.tensor_scalar(n3[:, 0, 0:NC].unsqueeze(2), mv3[:, :, 1:2], LN_EPS, None, ALU.add))
                        elif i <= 10:
                            st.done(rsqrt_step(i - 1, n3[:, 1, 0:NC], n3[:, 0, 0:NC], n3[:, 2, 0:NC]))
                        elif i == 11:
                            rsqrt_step(10, n3[:, 1, 0:NC], n3[:, 0, 0:NC], n3[:, 2, 0:NC]).then_inc(c3_dve, 1)
                    else:
                        if 3 <= i < 11:
                            j = i - 3
                            v.wait_ge(c3_pool, 2)
                            v.tensor_reduce(n3[:, 0, 4 * j:4 * j + 4], k3T[:, 256 * j:256 * j + 256].rearrange("p (k d) -> p k d", d=D3),
                                            AX.X, ALU.add).then_inc(dve_step, 1)
                            st.n += 1
                        elif i == 11:
                            v.wait_ge(dve_step, st.n)
                            st.done(v.tensor_scalar(n3[:, 0, :], n3[:, 0, :], 1.0 / D3, 1e-16, ALU.mult, ALU.max))
                        elif 12 <= i < 17:
                            for k in (2 * i - 24, 2 * i - 23):
                                st.done(rsqrt_step(k, n3[:, 1, :], n3[:, 0, :], n3[:, 2, :]))
                        elif i == 17:
                            rsqrt_step(10, n3[:, 1, :], n3[:, 0, :], n3[:, 2, :]).then_inc(c3_dve, 1)

                for i in range(NG + 2):
                    if i < NG:
                        g = g0 + i
                        v.wait_ge(scores_in_psum, g + 1)
                        if layer == 0:
                            if i >= 2:
                                v.wait_ge(probs_ready, g - 1)
                            v.tensor_scalar(clipped[:, i % 2, :], banks[i % 2][:, :], -1e4, 1e4, ALU.max, ALU.min).then_inc(clip_ready, 1)
                            v.wait_ge(clip_ready, i + 1)
                            v.tensor_reduce(negmax[:, i:i + 1], clipped[:, i % 2, :], AX.X, ALU.max, negate=True).then_inc(negmax_ready, 1)
                        else:
                            v.tensor_reduce(negmax[:, i:i + 1], banks[i % 2][:, :], AX.X, ALU.max, negate=True).then_inc(negmax_ready, 1)
                    if layer > 0 and 1 <= i <= NG:
                        j = i - 1
                        v.wait_ge(probsT_in_psum, g0 + j + 1)
                        if j >= 2:
                            v.wait_ge(pc_in_psum, g0 + j - 1)
                        v.tensor_copy(probsT[:, j % 2, :], banks[2 + j % 2][:, :]).then_inc(probsT_ready, 1)
                    if layer == 0 and i == NG:
                        v.wait_ge(guard_read, NG)
                        v.tensor_tensor(nan_hit[:, :], nan_sum[:, :], nan_sum[:, :], ALU.not_equal).then_inc(nan_ready, 1)
                    if i >= 2:
                        j = i - 2
                        v.wait_ge(probs_ready, g0 + j + 1)
                        st.done(v.reciprocal(rden[:, j:j + 1], den[:, j:j + 1]))
                        v.wait_ge(pc_in_psum, g0 + j + 1)
                        pc = banks[4 + j % 2]
                        if layer < 2:
                            v.scalar_tensor_tensor(out=om[:, j, :], in0=pc[:, 0:32], scalar=rden[:, j:j + 1], in1=w("head32"),
                                                   op0=ALU.mult, op1=ALU.mult).then_inc(om_ready, 1)
                        else:
                            if j >= 2:
                                v.wait_ge(pcnT_in_psum, j - 1)
                            v.tensor_scalar(pcn[:, j % 2, 0:DC], pc[:, 0:DC], rden[:, j:j + 1], None, ALU.mult).then_inc(pcn_ready, 1)
                    context3_share(i)
                if layer < 2:
                    if layer == 0:
                        v.wait_ge(nan_in_psum, 1)
                        st.done(v.tensor_reduce(nan_any[:, :], banks[7][:, 0:NG], AX.X, ALU.max))
                    v.wait_ge(oT_in_psum, layer + 1)
                    if layer == 0:
                        st.done(v.tensor_copy(oT[:, :], banks[6][:, 0:T]))
                        v.copy_predicated(oT[:, :].rearrange("p (b q) -> p b q", b=B),
                                          nan_any[:, :].bitcast(U32).unsqueeze(2).to_broadcast([128, B, S]),
                                          mean_vT[:, :].unsqueeze(2).to_broadcast([128, B, S])).then_inc(oT_ready, 1)
                    else:
                        v.tensor_copy(oT[:, :], banks[6][:, 0:T]).then_inc(oT_ready, 1)
                v.wait_ge(y_full, layer + 1)
                v.tensor_tensor(x[:, :], banks[2][:, 0:D], xb[:, :], ALU.add).then_inc(x_ready, 1)

            def top2(values):
                st.done(v.max(top8[:, :], values))
                st.done(v.max_index(idx8[:, :], top8[:, :], values))
                st.done(v.tensor_copy(idxf[:, :], idx8[:, :]))

            def onehot(k, scale):
                return v.tensor_scalar(oh[:, k, :], w("iota"), idxf[:, k:k + 1], scale, ALU.is_equal, ALU.mult)

            def route_logits(layer):
                v.wait_ge(logits_in_psum, layer + 1)
                logits = banks[7][:, 256:264]
                if layer == 0:
                    st.done(v.tensor_tensor(lg[:, :], logits, row("f0_br"), ALU.add))
                else:
                    st.done(v.tensor_copy(lg[:, :], logits))
                if layer != 2:
                    v.tensor_reduce(rt[:, 0:1], lg[:, :], AX.X, ALU.max, negate=True).then_inc(lneg_ready, 1)

            def route_choice(layer):
                if layer == 2:
                    top2(lg[:, :])
                    return
                v.wait_ge(lexp_ready, {0: 1, 1: 2, 3: 3}[layer])
                st.done(v.reciprocal(rt[:, 2:3], rt[:, 1:2]))
                st.done(v.tensor_scalar(sc8[:, :], sc8[:, :], rt[:, 2:3], None, ALU.mult))
                if layer == 1:
                    groups = sc8[:, :].rearrange("p (g e) -> p g e", g=4)
                    st.done(v.tensor_reduce(grp8[:, 0:4], groups, AX.X, ALU.max))
                    top2(grp8[:, :])
                    onehot(0, 1.0)
                    st.done(onehot(1, 1.0))
                    st.done(v.tensor_tensor(oh[:, 0, 0:4], oh[:, 0, 0:4], oh[:, 1, 0:4], ALU.add))
                    st.done(v.tensor_tensor(groups, groups, oh[:, 0, 0:4].unsqueeze(2).to_broadcast([128, 4, 2]), ALU.mult))
                    return
                top2(sc8[:, :])
                if layer == 3:
                    onehot(0, 1.0)
                    onehot(1, 1.0).then_inc(cw_ready, 1)

            def route_weights(layer):
                if layer == 2:
                    st.done(v.tensor_scalar(cw[:, :], w("iota"), idxf[:, 0:1], 0.5, ALU.is_equal, ALU.mult))
                    return
                if layer == 0:
                    for k in range(2):
                        ins = onehot(k, top8[:, k:k + 1])
                    st.done(ins)
                    v.tensor_tensor(cw[:, :], oh[:, 0, :], oh[:, 1, :], ALU.add).then_inc(cw_ready, 1)
                    v.wait_ge(cw_ready, 1)
                    return
                if layer == 1:
                    top2(sc8[:, :])
                st.done(v.tensor_tensor(rt[:, 3:4], top8[:, 0:1], top8[:, 1:2], ALU.add))
                st.done(v.reciprocal(rt[:, 4:5], rt[:, 3:4]))
                st.done(v.tensor_scalar(rt[:, 5:7], top8[:, 0:2], rt[:, 4:5], 0.5, ALU.mult, ALU.mult))
                if layer == 3:
                    v.wait_ge(cwT_in_psum, 3)
                    st.done(v.tensor_scalar(place[:, :], banks[7][:, 0:16], float(CAP), None, ALU.is_le))
                    for k in range(2):
                        ins = v.scalar_tensor_tensor(out=oh[:, k, :], in0=oh[:, k, :], scalar=rt[:, 5 + k:6 + k],
                                                     in1=place[:, 8 * k:8 * k + 8], op0=ALU.mult, op1=ALU.mult)
                else:
                    for k in range(2):
                        ins = onehot(k, rt[:, 5 + k:6 + k])
                st.done(ins)
                st.done(v.tensor_tensor(cw[:, :], oh[:, 0, :], oh[:, 1, :], ALU.add))

            def feed_forward(layer):
                e0 = E * layer
                C = FFN_CHUNKS[layer] * 128

                def hidden(e):
                    n = e0 + e
                    if layer == 0:
                        v.wait_ge(up_in_psum, n + 1)
                        if e >= 2:
                            v.wait_ge(y_in_psum, n - 1)
                        v.tensor_scalar(hid[:, e % 2, T:2 * T], banks[2 + e % 2][:, 0:T], w("f0_b1", 128, 2 * e + 1, 2 * e + 2), 0.0,
                                        ALU.add, ALU.max).then_inc(hid_ready, 1)
                        return
                    v.wait_ge(tanh_ready, n + 1 - E)
                    if e:
                        v.wait_ge(hid_ready, n)
                    st.done(v.scalar_tensor_tensor(out=act_a[:, 0:C], in0=tg[:, e % 2, 0:C], scalar=1.0, in1=banks[e % 2][:, 0:C],
                                                   op0=ALU.add, op1=ALU.mult))
                    v.wait_ge(up_in_psum, n + 1)
                    if e >= 2:
                        v.wait_ge(y_in_psum, n - 1)
                    v.tensor_tensor(hid[:, e % 2, 0:C], act_a[:, 0:C], banks[2 + e % 2][:, 0:C], ALU.mult).then_inc(hid_ready, 1)

                def add(e):
                    n = e0 + e
                    v.wait_ge(y_in_psum, n + 1)
                    if e:
                        v.wait_ge(y_added, Y_BASE[layer] + e)
                    last = layer > 0 and e == E - 1
                    v.scalar_tensor_tensor(out=x[:, :], in0=banks[4 + e % 3][:, 0:D], scalar=cw[:, e:e + 1], in1=x[:, :],
                                           op0=ALU.mult, op1=ALU.add).then_inc(x_ready if last else y_added, 1)

                hidden(0)
                route_logits(layer)
                hidden(1)
                route_choice(layer)
                hidden(2)
                route_weights(layer)
                add(0)
                for e in range(3, E):
                    hidden(e)
                    add(e - 2)
                add(E - 2)
                add(E - 1)
                if layer == 0:
                    v.wait_ge(cwT_in_psum, 1)
                    v.tensor_copy(cwT[:, :], banks[7][0:8, 0:T]).then_inc(cwT_ready, 1)
                    v.wait_ge(cwT_in_psum, 2)
                    v.wait_ge(y_added, E)
                    v.tensor_tensor(x[:, :], banks[7][:, 256:256 + D], x[:, :], ALU.add).then_inc(x_ready, 1)

            def linear_attention():
                v.wait_ge(mix_pe, 1)
                st.done(v.tensor_scalar(qT[:, :], banks[0][:, 0:T], 0.0, 1e-6, ALU.max, ALU.add))
                st.done(v.tensor_scalar(ktA[:, :], banks[1][:, 0:T], 0.0, 1e-6, ALU.max, ALU.add))
                v.tensor_tensor(big_a[:, :].rearrange("p (h t) -> p h t", h=H), qT[:, :].unsqueeze(1).to_broadcast([128, H, T]),
                                w("head16").unsqueeze(2).to_broadcast([128, H, T]), ALU.mult).then_inc(mix_dve, 1)
                for i in range(4):
                    v.wait_ge(mix_pe, 2 + i)
                    v.tensor_tensor(big_b[:, i * 512:i * 512 + 512].rearrange("p (h t) -> p h t", h=4),
                                    banks[3 + i][:, :].rearrange("p (h t) -> p h t", h=4),
                                    w("causal_ts").unsqueeze(1).to_broadcast([128, 4, T]), ALU.mult).then_inc(mix_dve, 1)
                v.wait_ge(mix_pe, 6)
                o9 = banks[0][:, 0:H * 9].rearrange("p (h d) -> p h d", h=H)
                st.done(v.tensor_scalar(den16[:, :].unsqueeze(2), o9[:, :, 8:9], 1e-6, None, ALU.add))
                st.done(v.reciprocal(den16[:, :], den16[:, :]))
                v.tensor_tensor(o_tok[:, :].rearrange("p (h d) -> p h d", h=H), o9[:, :, 0:8],
                                den16[:, :].unsqueeze(2).to_broadcast([128, H, DH]), ALU.mult).then_inc(mix_dve, 1)
                v.wait_ge(mix_pe, 7)
                v.tensor_copy(oT[:, :], banks[1][:, 0:T]).then_inc(mix_dve, 1)
                v.wait_ge(mix_pe, 8)
                v.tensor_tensor(x[:, :], banks[2][:, 0:D], x[:, :], ALU.add).then_inc(x_ready, 1)

            def causal_attention():
                v.wait_ge(mix_pe, 8 + 1)
                for i in range(2):
                    v.tensor_tensor(qk_[:, 2 * i, :], banks[2 * i][:, 0:T], w("rope_cos"), ALU.mult)
                    st.done(v.tensor_tensor(qk_[:, 2 * i + 1, :], banks[2 * i + 1][:, 0:T], w("rope_sin"), ALU.mult))
                st.done(v.tensor_tensor(ktA[:, :], qk_[:, 2, :], qk_[:, 3, :], ALU.add))
                st.done(v.tensor_tensor(z2[:, :], qk_[:, 0, :], qk_[:, 1, :], ALU.add))
                st.done(v.tensor_scalar(qT[:, :], z2[:, :], DH ** -0.5, None, ALU.mult))
                v.tensor_tensor(big_a[:, :].rearrange("p (b h t) -> p b h t", b=B, h=H),
                                ktA[:, :].rearrange("p (b t) -> p b t", b=B).unsqueeze(2).to_broadcast([128, B, H, S]),
                                w("head16").unsqueeze(1).unsqueeze(3).to_broadcast([128, B, H, S]), ALU.mult).then_inc(mix_dve, 1)
                v.wait_ge(mix_pe, 8 + 2)
                st.done(v.tensor_tensor(s_sb[:, :, :], banks[5][:, :].rearrange("p (h t) -> p h t", h=H),
                                        w("causal_add").unsqueeze(1).to_broadcast([128, H, S]), ALU.add))
                v.tensor_reduce(den16[:, :], s_sb[:, :, :], AX.X, ALU.max).then_inc(mix_dve, 1)
                v.wait_ge(mix_dve, LIN_DVE + 2)
                v.tensor_tensor(s_sb[:, :, :], s_sb[:, :, :], den16[:, :].unsqueeze(2).to_broadcast([128, H, S]),
                                ALU.subtract).then_inc(mix_dve, 1)
                v.wait_ge(mix_act, 1 + 2)
                v.transpose(pT_sb[:, :, :].rearrange("p h t -> p (h t)"), s_sb[:, :, :].rearrange("p h t -> p (h t)"))
                st.done(v.tensor_reduce(den16[:, :], s_sb[:, :, :], AX.X, ALU.add))
                st.done(v.reciprocal(den16[:, :], den16[:, :]))
                v.tensor_tensor(big_b[:, :].rearrange("p (h b q) -> p h b q", h=H, b=B),
                                pT_sb[:, :, :].unsqueeze(2).to_broadcast([128, H, B, S]),
                                w("fold4").unsqueeze(1).unsqueeze(3).to_broadcast([128, H, B, S]), ALU.mult).then_inc(mix_dve, 1)
                v.wait_ge(mix_pe, 8 + 3)
                v.tensor_tensor(z2[:, :].rearrange("p (h d) -> p h d", h=H), banks[0][:, 0:D].rearrange("p (h d) -> p h d", h=H),
                                den16[:, :].unsqueeze(2).to_broadcast([128, H, DH]), ALU.mult).then_inc(mix_dve, 1)
                v.wait_ge(mix_pe, 8 + 4)
                v.tensor_copy(oT[:, :], banks[1][:, 0:T]).then_inc(oT_ready, 1)
                v.wait_ge(mix_pe, 8 + 5)
                v.tensor_tensor(x[:, :], banks[2][:, 0:D], x[:, :], ALU.add).then_inc(x_ready, 1)

            def lstm():
                for t in range(B):
                    v.wait_ge(mix_act, 3 + 2 * t + 1)
                    v.scalar_tensor_tensor(out=cst[:, 1 if t else 2, :], in0=gates[:, 0, :], scalar=1.0, in1=gates[:, 3, :],
                                           op0=ALU.add, op1=ALU.mult).then_inc(dve_step if t else mix_dve, 1)
                    if t:
                        st.n += 1
                        st.done(v.scalar_tensor_tensor(out=cst[:, 0, :], in0=gates[:, 1, :], scalar=1.0, in1=cst[:, 4, :],
                                                       op0=ALU.add, op1=ALU.mult))
                        v.tensor_tensor(cst[:, 2, :], cst[:, 0, :], cst[:, 1, :], ALU.add).then_inc(mix_dve, 1)
                    v.wait_ge(mix_dve, CAU_DVE + 2 * t + 1)
                    st.done(v.tensor_scalar(cst[:, 4, :], cst[:, 2, :], 0.5, None, ALU.mult))
                    v.wait_ge(mix_act, 3 + 2 * t + 2)
                    v.scalar_tensor_tensor(out=h2T[:, t * S:(t + 1) * S], in0=gates[:, 2, :], scalar=1.0, in1=cst[:, 3, :],
                                           op0=ALU.add, op1=ALU.mult).then_inc(mix_dve, 1)
                v.wait_ge(mix_pe, CAU_PE + B + 1)
                v.scalar_tensor_tensor(out=x[:, :], in0=banks[1][:, 0:D], scalar=0.5, in1=x[:, :],
                                       op0=ALU.mult, op1=ALU.add).then_inc(x_ready, 1)

            def cross3():
                v.wait_ge(x_ready, 9)
                v.wait_ge(pool_set, SET_L3)
                st.done(v.tensor_tensor(xb[:, :], x[:, :], row("bo3"), ALU.add))
                st.done(layer_norm(xn[:, :], x[:, :]))
                layer_norm(z2[:, :], xn[:, :]).then_inc(c3_dve, 1)
                v.wait_ge(q_in_psum, 5)
                v.tensor_scalar(xnT[:, :], banks[7][:, 0:T], w("l3_g"), w("l3_b"), ALU.mult, ALU.add).then_inc(c3_dve, 1)
                v.wait_ge(c3_act, 17)
                st.done(v.tensor_tensor(big_a[:, 0:256], qkv3[:, 0:256], qkv3[:, 0:256], ALU.mult))
                st.done(v.tensor_reduce(d3[:, 4:8], big_a[:, 0:256].rearrange("p (k d) -> p k d", d=D3), AX.X, ALU.add))
                st.done(v.tensor_scalar(n3[:, 0, 0:4], d3[:, 4:8], 1.0 / D3, 1e-16, ALU.mult, ALU.max))
                rsqrt(n3[:, 1, 0:4], n3[:, 0, 0:4], n3[:, 2, 0:4])
                v.tensor_tensor(xn[:, :].rearrange("p (h d) -> p h d", h=2), qkv3[:, 0:128].rearrange("p (h d) -> p h d", h=2),
                                n3[:, 1, 0:2].unsqueeze(2).to_broadcast([128, 2, D3]), ALU.mult)
                v.tensor_tensor(z2[:, :].rearrange("p (h d) -> p h d", h=2), qkv3[:, 128:256].rearrange("p (h d) -> p h d", h=2),
                                n3[:, 1, 2:4].unsqueeze(2).to_broadcast([128, 2, D3]), ALU.mult).then_inc(c3_dve, 1)
                v.wait_ge(c3_pe, 18)
                st.done(v.tensor_scalar(qT[:, :], banks[1][:, 0:T], w("qn_g"), w("kn_g"), ALU.mult, ALU.mult))
                v.tensor_copy(kl3T, banks[2][:, 0:T])
                for h in range(H3):
                    p = slice(64 * h, 64 * h + 64)
                    ins = v.tensor_scalar(q3bd[p, h, :], qT[p, :], D3 ** -0.5, None, ALU.mult)
                ins.then_inc(c3_dve, 1)
                v.wait_ge(c3_pe, 19)
                for h in range(H3):
                    v.tensor_tensor(big_a[:, h * 640:h * 640 + 512], banks[3 + h][:, :], mask_add, ALU.add).then_inc(c3_dve, 1)
                v.tensor_tensor(big_a[:, 0:1280].rearrange("p (h k) -> p h k", h=2)[:, :, 512:640],
                                banks[5][:, 0:256].rearrange("p (h k) -> p h k", h=2),
                                w("batch_add").unsqueeze(1).to_broadcast([128, 2, T]), ALU.add).then_inc(c3_dve, 1)
                v.wait_ge(c3_dve, 9)
                v.tensor_reduce(d3[:, 0:2], big_a[:, 0:1280].rearrange("p (h k) -> p h k", h=2), AX.X, ALU.max,
                                negate=True).then_inc(c3_dve, 1)
                for h in range(H3):
                    v.wait_ge(c3_act, 18 + h)
                    st.done(v.reciprocal(d3[:, 4 + h:5 + h], d3[:, 2 + h:3 + h]))
                    v.tensor_scalar(big_a[:, h * 640:h * 640 + 640], big_a[:, h * 640:h * 640 + 640], d3[:, 4 + h:5 + h], None,
                                    ALU.mult).then_inc(c3_dve, 1)
                v.wait_ge(c3_pe, 21)
                v.tensor_copy(big_b[:, 512:1024], banks[1][:, :]).then_inc(c3_dve, 1)
                v.wait_ge(c3_pe, 23)
                v.tensor_copy(oT[:, :], banks[6][:, 0:T]).then_inc(c3_dve, 1)
                v.wait_ge(y_full, 4)
                v.tensor_tensor(x[:, :], banks[0][:, 0:D], xb[:, :], ALU.add).then_inc(x_ready, 1)

            def state_space():
                m, d, a = CAU_PE + B + 1, CAU_DVE + 2 * B, 3 + 2 * B
                v.wait_ge(mix_pe, m + 1)
                v.tensor_tensor(dts[:, 0, :].rearrange("p (d h) -> p d h", d=2),
                                banks[7][:, 256:264].rearrange("p (d h) -> p d h", d=2),
                                row("dtb").unsqueeze(1).to_broadcast([128, 2, NH]), ALU.add).then_inc(mix_dve, 1)
                v.tensor_copy(convp[:, :, :, PAD:PAD + S], banks[0][:, :].rearrange("p (j b l) -> p j b l", j=4, b=B)).then_inc(mix_dve, 1)
                v.tensor_scalar(big_c[:, 512:544], late[:, late_at["m_cw"][0]:late_at["m_cw"][0] + 32], 0.5, None, ALU.mult).then_inc(dve_step, 1)
                st.n += 1
                v.wait_ge(dve_step, st.n)
                v.wait_ge(mix_dve, d + 2)
                for k in range(TAPS):
                    for j in range(4):
                        out = big_b[:, j * T:(j + 1) * T].rearrange("p (b l) -> p b l", b=B)
                        src = convp[:, j, :, k:k + S]
                        tap = big_c[:, 512 + 7 * j + k:513 + 7 * j + k]
                        if k == 0:
                            ins = v.tensor_scalar(out, src, tap, big_c[:, 540 + j:541 + j], ALU.mult, ALU.add)
                        else:
                            ins = v.scalar_tensor_tensor(out=out, in0=src, scalar=tap, in1=out, op0=ALU.mult, op1=ALU.add)
                    if k == TAPS - 1:
                        ins.then_inc(mix_dve, 1)
                    else:
                        st.done(ins)
                v.wait_ge(mix_act, a + 3)
                st.done(v.tensor_scalar(dts[:, 3, :], dts[:, 0, :], 0.0, None, ALU.max))
                st.done(v.tensor_tensor(dts[:, 3, :], dts[:, 3, :], dts[:, 2, :], ALU.add))
                st.done(v.tensor_tensor(dts[:, 4, :].rearrange("p (d h) -> p d h", d=2), dts[:, 3, :].rearrange("p (d h) -> p d h", d=2),
                                        dts[:, 5, 0:4].unsqueeze(1).to_broadcast([128, 2, NH]), ALU.mult))
                for i, name in enumerate(("m_fw", "m_bw")):
                    ins = v.tensor_tensor(big_a[:, i * 512:i * 512 + 512].rearrange("p (h t) -> p h t", h=NH),
                                          w(name).unsqueeze(1).to_broadcast([128, NH, T]),
                                          dts[:, 4, 4 * i:4 * i + 4].unsqueeze(2).to_broadcast([128, NH, T]), ALU.mult)
                ins.then_inc(mix_dve, 1)
                v.wait_ge(mix_act, a + 5)
                v.scalar_tensor_tensor(out=big_b[:, 1024:1536], in0=big_b[:, 512:1024], scalar=1.0, in1=big_b[:, 0:512],
                                       op0=ALU.add, op1=ALU.mult).then_inc(mix_dve, 1)
                v.wait_ge(mix_dve, d + 5)
                v.tensor_copy(cbd[0:64, 0, 1:T], big_b[0:64, 1408:1535])
                v.tensor_copy(cbd[64:128, 1, 0:T - 1], big_b[64:128, 1409:1536]).then_inc(mix_dve, 1)
                v.wait_ge(mix_pe, m + 5)
                gm = big_c[:, 768:1024]
                st.done(v.tensor_tensor(gm.rearrange("p (d t) -> p d t", d=2), banks[5][:, 0:256].rearrange("p (d t) -> p d t", d=2),
                                        late[:, late_at["m_fw"][0]:late_at["m_fw"][0] + 256].rearrange("p (d t) -> p d t", d=2), ALU.mult))
                v.tensor_copy(big_c[:, 256:512], banks[4][:, 0:256])
                st.done(v.tensor_tensor(dts[:, 5, 4:8], banks[6][:, 0:4], row("dp"), ALU.add))
                v.wait_ge(mix_act, a + 7)
                for i in range(2):
                    dec = big_a[:, 1024 + 512 * i:1536 + 512 * i].rearrange("p (h t) -> p h t", h=NH)
                    ins = v.tensor_tensor(dec, dec, gm[:, i * T:(i + 1) * T].unsqueeze(1).to_broadcast([128, NH, T]), ALU.mult)
                ins.then_inc(mix_dve, 1)
                st.done(v.tensor_tensor(big_c[:, 1536:1792].rearrange("p (h n) -> p h n", h=NH),
                                        big_c[:, 256:512].rearrange("p (h n) -> p h n", h=NH),
                                        dts[:, 5, 4:8].unsqueeze(2).to_broadcast([128, NH, 64]), ALU.mult))
                st.done(v.scalar_tensor_tensor(out=big_c[:, 1792:2048], in0=big_c[:, 0:256], scalar=1.0, in1=banks[1][:, 0:256],
                                               op0=ALU.add, op1=ALU.mult))
                v.wait_ge(mix_pe, m + 6)
                y = big_c[:, 1024:1280]
                st.done(v.tensor_tensor(y, banks[0][:, 0:256], big_c[:, 1536:1792], ALU.add))
                st.done(v.tensor_tensor(big_c[:, 1536:1792], y, y, ALU.mult))
                st.done(v.tensor_reduce(nw[:, 0:1], big_c[:, 1536:1792], AX.X, ALU.add))
                st.done(v.tensor_scalar(nw[:, 0:1], nw[:, 0:1], 1.0 / DI, 1e-5, ALU.mult, ALU.add))
                rsqrt_column()
                v.scalar_tensor_tensor(out=y, in0=y, scalar=nw[:, 1:2], in1=big_c[:, 1792:2048],
                                       op0=ALU.mult, op1=ALU.mult).then_inc(mix_dve, 1)
                v.wait_ge(mix_pe, m + 7)
                for j in range(2):
                    ins = v.tensor_scalar(big_c[:, 1280 + j * 128:1280 + (j + 1) * 128], banks[1][:, j * 128:(j + 1) * 128],
                                          w("m_nw", 128, j, j + 1), 0.5, ALU.mult, ALU.mult)
                ins.then_inc(mix_dve, 1)
                v.wait_ge(mix_pe, m + 8)
                v.tensor_tensor(x[:, :], banks[2][:, 0:D], x[:, :], ALU.add).then_inc(x_ready, 1)

            v.wait_ge(load["x"], 16)
            v.wait_ge(load["early"], 16)
            norm(0)
            context_attention(0)
            if STAGES >= 2:
                norm(1); linear_attention()
            if STAGES >= 3:
                v.wait_ge(load["late"], 16)
                norm(2); feed_forward(0)
            if STAGES >= 4:
                norm(3); context_attention(1)
            if STAGES >= 5:
                norm(4); causal_attention()
            if STAGES >= 6:
                norm(5); feed_forward(1)
            if STAGES >= 7:
                norm(6); context_attention(2)
            if STAGES >= 8:
                norm(7); lstm()
            if STAGES >= 9:
                norm(8); feed_forward(2)
            if STAGES >= 10:
                cross3()
            if STAGES >= 11:
                norm(10); state_space()
            if STAGES >= 12:
                norm(11); feed_forward(3)


def constants():
    p = np.arange(128)
    one = np.float32
    batch, t = p // S, p % S
    same = batch[:, None] == batch[None, :]
    c = {
        "ident": np.eye(128), "head16": p[:, None] // DH == np.arange(H)[None, :],
        "head32": p[:, None] // S == np.arange(32)[None, :] // DH, "fold4": p[:, None] // S == np.arange(4)[None, :], "fold": p[:, None] % S == np.arange(S)[None, :],
        "ones": np.ones((128, 128)), "causal_ts": same & (p[:, None] <= p[None, :]),
        "causal_add": np.where(np.arange(S)[None, :] <= t[:, None], 0.0, -BIG),
        "cum": p[:, None] <= p[None, :],
        "m_fw": same & (p[:, None] < p[None, :]), "m_bw": same & (p[:, None] > p[None, :]),
        "l_fw": same & (p[:, None] > p[None, :]), "l_bw": same & (p[:, None] < p[None, :]),
        "batch_add": np.where(same, 0.0, -BIG), "iota": np.tile(np.arange(8), (128, 1)),
    }
    d = p % DH
    freq = (np.float32(10000.0) ** (-(np.arange(0, DH, 2, dtype=np.float32)) / np.float32(DH)))[d // 2]
    ang = t[None, :].astype(np.float32) * freq[:, None].astype(np.float32)
    c["rope_cos"] = np.cos(ang)
    c["rope_sin"] = np.sin(ang) * np.where(d % 2 == 0, -1.0, 1.0)[:, None]
    return {k: np.asarray(v, one) for k, v in c.items()}


def kernel(**inputs):
    import concourse.bacc as bacc
    from concourse.bass_utils import run_bass_kernel_spmd

    i = {k: np.asarray(v) for k, v in inputs.items()}
    r = lambda a: np.ascontiguousarray(a)
    col = lambda a: a.reshape(-1, 1)
    small = constants()
    for k, pre in ((0, "L0_xattn_"), (1, "L1_xattn_")):
        if k == 0:
            wk, wv, bk, bv, wq, wo = (i[pre + n] for n in ("Wk", "Wv", "bk", "bv", "Wq", "Wo"))
        else:
            kv = i[pre + "Wkv"].reshape(H, 2, DH, DC)
            bkv = i[pre + "bkv"].reshape(H, 2, DH)
            wk, wv = (kv[:, j].reshape(D, DC).T for j in range(2))
            bk, bv = (bkv[:, j].reshape(D) for j in range(2))
            wq, wo = i[pre + "Wq"].T, i[pre + "Wo"].T
        small[f"wq{k}"], small[f"wo{k}"], small[f"bq{k}"] = wq, wo, col(i[pre + "bq"])
        small[f"wkT{k}"] = np.concatenate([wk.T, col(bk)], axis=1)
        small[f"wv{k}"] = np.concatenate([wv, bv[None, :]], axis=0)
    for n in ("q", "k", "v", "o"):
        small["a_w" + n] = i["L0_attn_W" + n].T
        small["r_w" + n] = i[f"L1_attn_{n}_proj"].T
    swap = np.arange(D) ^ 1
    for n in ("r_wq", "r_wk"):
        small[n] = np.concatenate([small[n], small[n][:, swap]], axis=1)
    small["f0_wr"], small["f1_wr"] = i["L0_ffn_Wr"], i["L1_ffn_gate_w"].T
    small["f2_wr"], small["f3_wr"] = i["L2_ffn_router_w"].T, i["L3_ffn_gate_w"].T
    small["f0_b1"] = i["L0_ffn_b1"].reshape(E * 2, 128).T
    small["f0_b2"] = i["L0_ffn_b2"]
    small["lstm_w"], small["lstm_u"] = i["L2_attn_w"], i["L2_attn_u"]
    small["x3_g"], small["x3_b"] = col(i["L3_xattn_ln_x_g"]), col(i["L3_xattn_ln_x_b"])
    small["l3_g"], small["l3_b"] = col(i["L3_xattn_ln_l_g"]), col(i["L3_xattn_ln_l_b"])
    small["qn_g"], small["kn_g"] = (col(np.tile(i[f"L3_xattn_{n}_g"], 2)) for n in ("qn", "kn"))
    small["x3_wqkv"] = np.concatenate([i["L3_xattn_Wq"].T, i["L3_xattn_Wlkv"].T], axis=1)
    small["x3_wkv"], small["x3_wo"] = i["L3_xattn_Wkv"].T, i["L3_xattn_Wo"].T
    ch = np.concatenate([np.arange(256), np.arange(256, 320), np.arange(384, 448), np.arange(320, 384), np.arange(448, 512)])
    order = np.concatenate([np.arange(DI), DI + ch, np.arange(768, 776)])
    small["m_in"] = i["L3_attn_W_in"][order].T
    small["m_cw"] = i["L3_attn_conv_w"][ch, 0].reshape(4, 128, TAPS).transpose(1, 0, 2).reshape(128, 28)
    small["m_cb"] = i["L3_attn_conv_b"][ch].reshape(4, 128).T
    small["m_fc"] = i["L3_attn_fc_D_w"].reshape(NH, 2, 128).transpose(2, 1, 0).reshape(128, 8)
    small["m_nw"] = i["L3_attn_norm_w"].reshape(2, 128).T
    small["m_out"] = i["L3_attn_W_out"].T.reshape(2, 128, 128).transpose(1, 0, 2).reshape(128, 256)

    def pack(table):
        out = np.zeros((128, columns(table)[1]), np.float32)
        for name, (at, n) in columns(table)[0].items():
            out[:small[name].shape[0], at:at + n] = small[name]
        return out

    def pad(a):
        return np.concatenate([a, np.zeros((E, 384 - a.shape[1], 128), a.dtype)], axis=1)

    def chunked(a):
        return r(a.reshape(E, -1, 128, 128).transpose(2, 0, 1, 3).reshape(128, E, -1))

    ctx = i["ctx_768"].reshape(B * SK, DC)
    up = lambda a: r(a.transpose(2, 0, 1))
    arrays = {
        "early": pack(EARLY), "late": pack(LATE), "x": r(i["x"].reshape(T, D)),
        "rows": r(np.concatenate([i["L0_xattn_bo"], i["L1_xattn_bo"], i["L2_xattn_b_out"], i["L3_xattn_bo"], i["L0_ffn_br"],
                                  i["L3_attn_dt_bias"], i["L3_attn_A_log"], i["L3_attn_Dp"], i["L2_attn_bias"]])[None, :]),
        "ctxT": r(ctx.T), "ctxk": r(ctx.reshape(NC, 128, DC).transpose(1, 0, 2)),
        "mask": r(i["mask_BxS2_bk0"]),
        "f0_w1": r(i["L0_ffn_W1"].transpose(1, 0, 2)), "f0_w2": chunked(i["L0_ffn_W2"]),
        "f1_w13": up(i["L1_ffn_w13_weight"]), "f1_w2": chunked(i["L1_ffn_w2_weight"].transpose(0, 2, 1)),
        "f2_wg": up(pad(i["L2_ffn_gate_w"])), "f2_wu": up(pad(i["L2_ffn_up_w"])),
        "f2_wd": chunked(pad(i["L2_ffn_down_w"].transpose(0, 2, 1))),
        "f3_wg": up(i["L3_ffn_wi_gate"]), "f3_wu": up(i["L3_ffn_wi_up"]), "f3_wd": chunked(i["L3_ffn_wo"].transpose(0, 2, 1)),
        "x2_wq": r(i["L2_xattn_w_q"]), "x2_wkT": r(i["L2_xattn_w_k"].T.reshape(8, 128, DC).transpose(1, 0, 2)),
        "x2_wv": r(i["L2_xattn_w_v"]), "x2_wo": r(i["L2_xattn_w_out"].reshape(8, 128, 128).transpose(1, 0, 2)),
    }
    nc = bacc.Bacc("TRN2", target_bir_lowering=False, num_devices=1)
    feeds = {f"in_{n}": a for n, a in arrays.items()}
    dram = {n: nc.dram_tensor(f"in_{n}", a.shape, mybir.dt.from_np(a.dtype), kind="ExternalInput").ap()
            for n, a in arrays.items()}
    dram["out"] = nc.dram_tensor("out_x", (T, D), F32, kind="ExternalOutput").ap()
    build(nc, dram)
    got = run_bass_kernel_spmd(nc, [feeds], core_ids=[0]).results[0]["out_x"]
    return got.reshape(B, S, D)
```

```python
from contextlib import ExitStack

import numpy as np

import concourse.bass as bass
from concourse import mybir

F32 = mybir.dt.float32
U32 = mybir.dt.uint32
I32 = mybir.dt.int32
U8 = mybir.dt.uint8
ALU = mybir.AluOpType
ACT = mybir.ActivationFunctionType
AX = mybir.AxisListType

B, S, D = 4, 32, 128
T = B * S
H = 16
DH = D // H
SK, DC = 512, 96
CK = SK // 128
NC = B * CK
CA = DC + 1
E = 8
HG = H // 4
NG = B * HG
LN_EPS = 1e-5
SUBLAYERS = 12
KEEP_WARM = 12
BIG = 3.0e38
CAP = int(T / E * 1.25)
RSQRT_MAGIC = float(0x5F3759DF - (1 << 31))
KAPPA = (3 / 16) ** 0.5
H2, D2 = 16, 64
H3, D3 = 2, 64
DI, NH = 256, 4
TAPS = 7
PAD = TAPS // 2
SP = S + 2 * PAD
FFN_CHUNKS = {0: 2, 1: 2, 2: 3, 3: 4}

EARLY = [("ident", 128), ("head16", 16), ("head32", 32), ("ones", 128),
         ("wq0", 128), ("bq0", 1), ("wk0", 128), ("wv0", 128), ("wo0", 128)]
LATE = [("causal_add", 32), ("causal_mul", 32), ("own4", 4), ("rope_cos", 128), ("rope_sin", 128), ("cum", 128),
        ("m_fw", 128), ("m_bw", 128), ("l_fw", 128), ("l_bw", 128), ("batch_add", 128), ("iota", 8),
        ("a_wq", 128), ("a_wk", 128), ("a_wv", 128), ("a_wo", 128),
        ("f0_wr", 8), ("f0_b1", 16), ("f0_b2", 128),
        ("wq1", 128), ("bq1", 1), ("wk1", 128), ("wv1", 128), ("wo1", 128),
        ("r_wq", 256), ("r_wk", 256), ("r_wv", 128), ("r_wo", 128), ("f1_wr", 8),
        ("lstm_w", 512), ("lstm_u", 512), ("f2_wr", 8),
        ("x3_g", 1), ("x3_b", 1), ("l3_g", 1), ("l3_b", 1), ("qn_g", 1), ("kn_g", 1),
        ("x3_wqkv", 384), ("x3_wkv", 256), ("x3_wo", 128),
        ("m_in", 776), ("m_cw", 28), ("m_cb", 4), ("m_fc", 8), ("m_nw", 2), ("m_out", 256), ("f3_wr", 8)]
ROWS = [("bo0", 128), ("bo1", 128), ("bo2", 128), ("bo3", 128), ("f0_br", 8), ("dtb", 4), ("alog", 4), ("dp", 4),
        ("lstm_b", 512)]


def columns(table):
    at, out = 0, {}
    for name, n in table:
        out[name] = (at, n)
        at += n
    return out, at


def build(nc, dram):
    with ExitStack() as ctx:
        def sb(name, shape, dt=F32):
            return ctx.enter_context(nc.sbuf_tensor(name, shape, dt))

        def sem(name):
            return ctx.enter_context(nc.semaphore(name))

        early_at, n_early = columns(EARLY)
        late_at, n_late = columns(LATE)
        row_at, n_rows = columns(ROWS)
        early = sb("early", [128, n_early])
        late = sb("late", [128, n_late])
        rows = sb("rows", [128, n_rows])

        def probs_turned(layer, i):
            flat = kv3[:, :, :].rearrange("p a n -> p (a n)")
            place = (i % 8) * 512
            if layer == 0:
                return flat[:, place:place + 512]
            if i % 8 < 4:
                return k3T[:, place:place + 512]
            return flat[:, place - 512:place]

        def w(name, rows_=128, a=0, b=None):
            tile, at = (early, early_at) if name in early_at else (late, late_at)
            start, n = at[name]
            return tile[0:rows_, start + a:start + (n if b is None else b)]

        def row(name, a=0, b=None, p=128):
            start, n = row_at[name]
            return rows[0:p, start + a:start + (n if b is None else b)]

        ident = w("ident")
        ctxT = sb("ctxT", [CA, B * SK])
        ctxk = sb("ctxk", [128, NC, DC])
        f0_w1 = sb("f0_w1", [128, E, 256])
        f0_w2 = sb("f0_w2", [128, E, 256])
        f1_w13 = sb("f1_w13", [128, E, 512])
        f1_w2 = sb("f1_w2", [128, E, 256])
        f2_wg = sb("f2_wg", [128, E, 384])
        f2_wu = sb("f2_wu", [128, E, 384])
        f2_wd = sb("f2_wd", [128, E, 384])
        x2_wqo = sb("x2_wqo", [128, 2, 1024])
        x2_wq = x2_wqo[:, 0, :]
        x2_wkT = sb("x2_wkT", [128, 8, DC])
        x2_v = sb("x2_v", [128, H2 * D2])
        x2_wv = x2_v[0:DC, :]
        x2_wo = x2_wqo[:, 1, :].rearrange("p (a n) -> p a n", a=8)

        f3_wg = f1_w13
        f3_wd = [f0_w1[:, :, :].rearrange("p (e a) f -> p e (a f)", a=2), f0_w2[:, :, :].rearrange("p (e a) f -> p e (a f)", a=2)]
        f3_wu = [f1_w2[:, :, :].rearrange("p (e a) f -> p e (a f)", a=2), x2_wqo[:, :, :].rearrange("p a (e f) -> p (a e) f", e=2)]

        x = sb("x", [128, D])
        xb = sb("xb", [128, D])
        xn = sb("xn", [128, D])
        xnT = sb("xnT", [128, T])
        stats = sb("stats", [128, 6])
        mv = sb("mv", [128, 2])
        nw = sb("nw", [128, 8])
        z2 = sb("z2", [128, D])

        big_a = sb("big_a", [128, 2048])
        big_b = sb("big_b", [128, 2048])
        big_c = sb("big_c", [128, 2048])
        kv3 = sb("kv3", [128, NC, 256])
        zc = kv3[:, :, :].rearrange("p a n -> p (a n)")[:, 0:NC * DC].rearrange("p (k c) -> p k c", k=NC)
        q2bd = f0_w1[:, :, :].rearrange("p a (h t) -> p a h t", h=2)
        o2T = f0_w2[:, 0:4, :].rearrange("p a (h t) -> p (a h) t", h=2)
        k3T = sb("k3T", [128, B * SK])
        clipped = k3T[:, 0:1024].rearrange("p (a k) -> p a k", a=2)
        guard_out = k3T[:, 1024:1536]
        s_sb = k3T[:, 1024:1536].rearrange("p (h t) -> p h t", h=H)
        pT_sb = k3T[:, 1536:2048].rearrange("p (h t) -> p h t", h=H)
        probs = sb("probs", [128, 2, SK])
        probsT = sb("probsT", [128, 2, SK])
        qT = sb("qT", [128, T])
        negmax = sb("negmax", [128, NG])
        nan_sum = sb("nan_sum", [128, NG])
        nan_hit = sb("nan_hit", [128, NG])
        nan_any = sb("nan_any", [128, 1])
        uniform = sb("uniform", [128, S])
        den = sb("den", [128, NG])
        rden = sb("rden", [128, NG])
        pcn = big_a[:, 0:4 * DC].rearrange("p (k n) -> p k n", k=4)
        inverse = sb("inverse", [128, HG, 32])
        turned_inverse = xn
        own = z2
        oT = sb("oT", [128, T])

        hid, tg = big_a[:, 0:1536].rearrange("p (k n) -> p k n", k=3), probsT
        act_a = sb("act_a", [128, 512])
        mean_tok = act_a[:, 0:D]
        lg = sb("lg", [128, 8])
        sc8 = sb("sc8", [128, 8])
        top8 = sb("top8", [128, 8])
        idx8 = sb("idx8", [128, 8], U32)
        idxf = sb("idxf", [128, 8])
        oh = sb("oh", [128, 2, 8])
        cw = sb("cw", [128, 8])
        cwT = sb("cwT", [8, T])
        rt = sb("rt", [128, 8])
        grp8 = sb("grp8", [128, 8])
        place = sb("place", [128, 16])

        qk_ = sb("qk_", [128, 4, T])
        ktA = sb("ktA", [128, T])
        k_own = big_a[:, 0:512].rearrange("p (b h t) -> p b h t", b=B, h=4)
        den16 = sb("den16", [128, H])
        o_tok = sb("o_tok", [128, D])

        u_half = sb("u_half", [128, 512])
        h2T = ktA
        gates = qk_[:, 0, :].rearrange("p (g b) -> p g b", g=4)
        cst = qk_[:, 1:3, :].rearrange("p a (g b) -> p (a g) b", g=4)

        mask_u8 = sb("mask_u8", [128, SK], U8)
        mask_add = x2_v[:, 0:SK]
        st3 = sb("st3", [128, NC, 6])
        mv3 = sb("mv3", [128, NC, 2])
        n3 = sb("n3", [128, 5, 2 * NC])
        qkv3 = qk_[:, 0:3, :].rearrange("p a t -> p (a t)")
        kl3T = qk_[:, 3, :]
        q3bd = x2_v[:, SK + 2 * T:SK + 4 * T].rearrange("p (h t) -> p h t", h=2)
        d3 = sb("d3", [128, 8])

        padded = x2_wkT[:, :, :].rearrange("p a c -> p (a c)")[:, 0:3 * B * SP].rearrange("p (j b l) -> p j b l", j=3, b=B)
        convp = padded[:, 0:2]
        xpad = padded[:, 2]
        taps = f2_wu[:, :, :].rearrange("p e f -> p (e f)")[:, 0:TAPS * 256].rearrange("p (k n) -> p k n", k=TAPS)
        tapped = f2_wg[:, :, :].rearrange("p e f -> p (e f)")[:, 0:TAPS * 256].rearrange("p (k n) -> p k n", k=TAPS)
        cbd = x2_v[:, SK:SK + 2 * T].rearrange("p (d t) -> p d t", d=2)
        dts = sb("dts", [128, 6, 8])
        half_taps = big_c[:, 512:544]

        banks = [ctx.enter_context(nc.psum_tensor(f"bank{i}", [128, 512], F32)) for i in range(8)]

        load = {n: sem("load_" + n) for n in
                ("early", "rows", "x", "ctxT", "ctxk", "late", "f0", "f1", "f2", "x2", "f3up", "f3gate", "f3down", "mask", "taps")}
        pool_set = sem("pool_set")
        pool_step = sem("pool_step")
        dve_step = sem("dve_step")
        act_step = sem("act_step")
        out_stored = sem("out_stored")

        xn_ready = sem("xn_ready")
        xnT_in_psum = sem("xnT_in_psum")
        xnT_ready = sem("xnT_ready")
        x_ready = sem("x_ready")
        y_full = sem("y_full")

        q_in_psum = sem("q_in_psum")
        qbd_ready = sem("qbd_ready")
        qw_in_psum = sem("qw_in_psum")
        qw_act = sem("qw_act")
        qw_dve = sem("qw_dve")
        scores_in_psum = sem("scores_in_psum")
        negmax_ready = sem("negmax_ready")
        clip_ready = sem("clip_ready")
        guard_read = sem("guard_read")
        probs_ready = sem("probs_ready")
        probsT_in_psum = sem("probsT_in_psum")
        probsT_ready = sem("probsT_ready")
        probsT_act = sem("probsT_act")
        pc_in_psum = sem("pc_in_psum")
        pcn_ready = sem("pcn_ready")
        pcnT_in_psum = sem("pcnT_in_psum")
        pcnT_ready = sem("pcnT_ready")
        o_in_psum = sem("o_in_psum")
        o2_ready = sem("o2_ready")
        mean_in_psum = sem("mean_in_psum")
        mean_ready = sem("mean_ready")
        keys_in_psum = sem("keys_in_psum")
        keys_ready = sem("keys_ready")
        v_in_psum = sem("v_in_psum")
        v_ready = sem("v_ready")
        inverse_ready = sem("inverse_ready")
        inverse_in_psum = sem("inverse_in_psum")
        inverse_out = sem("inverse_out")
        own_ready = sem("own_ready")
        oT_ready = sem("oT_ready")
        nan_ready = sem("nan_ready")
        nan_in_psum = sem("nan_in_psum")

        logits_in_psum = sem("logits_in_psum")
        lneg_ready = sem("lneg_ready")
        lexp_ready = sem("lexp_ready")
        gate_in_psum = sem("gate_in_psum")
        up_in_psum = sem("up_in_psum")
        tanh_ready = sem("tanh_ready")
        hid_ready = sem("hid_ready")
        hid_act = sem("hid_act")
        y_in_psum = sem("y_in_psum")
        y_added = sem("y_added")
        cw_ready = sem("cw_ready")
        cwT_in_psum = sem("cwT_in_psum")
        cwT_ready = sem("cwT_ready")
        mix_pe = sem("mix_pe")
        mix_dve = sem("mix_dve")
        mix_act = sem("mix_act")
        c3_pe = sem("c3_pe")
        c3_dve = sem("c3_dve")
        c3_act = sem("c3_act")
        c3_pool = sem("c3_pool")
        tapped_ready = sem("tapped_ready")

        LIN_PE, LIN_DVE = 12, 4
        CAU_PE, CAU_DVE, CAU_ACT = LIN_PE + 12, LIN_DVE + 8, 6
        VALUE_BANK = (0, 1, 3, 4)
        Y_BASE = {0: 0, 1: 8, 2: 15, 3: 22}
        QW_BANK = (6, 7, 4, 5)
        L0_KEYS = {-1: (0, 4), 0: (1, 5), 1: (2, 6), 3: (3, 6)}
        L0_VALUES = {2: (0, 7), 4: (1, 7), 5: (2, 6), 6: (3, 7)}

        block = ctx.enter_context(nc.Block())

        class Steps:

            def __init__(self, engine, semaphore):
                self.engine, self.semaphore, self.n = engine, semaphore, 0

            def count(self, ins):
                ins.then_inc(self.semaphore, 1)
                self.n += 1
                return self.n

            def after(self, n):
                self.engine.wait_ge(self.semaphore, n)

            def done(self, ins):
                ins.then_inc(self.semaphore, 1)
                self.n += 1
                self.engine.wait_ge(self.semaphore, self.n)

        @block.sync
        def _(sp):
            sp.dma_start(early[:, :], dram["early"]).then_inc(load["early"], 16)
            sp.dma_start(x[:, :], dram["x"]).then_inc(load["x"], 16)
            sp.dma_start(ctxT[0:DC, :], dram["ctxT"]).then_inc(load["ctxT"], 16)
            sp.dma_start(ctxk[:, :, :], dram["ctxk"]).then_inc(load["ctxk"], 16)
            sp.dma_start(rows[:, :], dram["rows"].partition_broadcast(128)).then_inc(load["rows"], 16)
            sp.dma_start(late[:, :], dram["late"]).then_inc(load["late"], 16)
            sp.dma_start(f0_w1[:, :, :], dram["f0_w1"]).then_inc(load["f0"], 16)
            sp.dma_start(f0_w2[:, :, :], dram["f0_w2"]).then_inc(load["f0"], 16)
            sp.dma_start(f1_w13[:, :, :], dram["f1_w13"]).then_inc(load["f1"], 16)
            sp.dma_start(f1_w2[:, :, :], dram["f1_w2"]).then_inc(load["f1"], 16)
            for tile, name in ((x2_wq, "x2_wq"), (x2_wkT[:, :, :], "x2_wkT"), (x2_wv, "x2_wv"), (x2_wo, "x2_wo")):
                sp.dma_start(tile, dram[name]).then_inc(load["x2"], 16)
            for tile, name in ((f2_wg, "f2_wg"), (f2_wu, "f2_wu"), (f2_wd, "f2_wd")):
                sp.dma_start(tile[:, :, :], dram[name]).then_inc(load["f2"], 16)
            for b in range(B):
                sp.dma_start(mask_u8[b * S:(b + 1) * S, :],
                             dram["mask"][b:b + 1, :].partition_broadcast(S)).then_inc(load["mask"], 16)
            sp.wait_ge(y_in_psum, 2 * E)
            sp.dma_start(f3_wg[:, :, :], dram["f3_wg"]).then_inc(load["f3gate"], 16)
            sp.dma_start(f3_wu[0], dram["f3_wu"][:, 0:4, :]).then_inc(load["f3up"], 16)
            sp.wait_ge(y_full, 3)
            sp.dma_start(f3_wu[1], dram["f3_wu"][:, 4:8, :]).then_inc(load["f3up"], 16)
            for i in range(2):
                sp.dma_start(f3_wd[i], dram["f3_wd"][:, 4 * i:4 * i + 4, :]).then_inc(load["f3down"], 16)
            sp.wait_ge(y_in_psum, 3 * E)
            sp.dma_start(taps, dram["taps"].partition_broadcast(128)).then_inc(load["taps"], 16)
            sp.wait_ge(x_ready, SUBLAYERS)
            sp.dma_start(dram["out"], x[:, :]).then_inc(out_stored, 16)
            sp.wait_ge(out_stored, 16)

        @block.gpsimd
        def _(pool):
            n = Steps(pool, pool_set)
            n.done(pool.memset(ctxT[DC:CA, :], 1.0))
            n.done(pool.memset(uniform[:, :], 1.0 / SK))
            n.done(pool.memset(grp8[:, :], -1.0))
            pool.wait_ge(load["late"], 16)
            n.done(pool.tensor_scalar(u_half[:, :], w("lstm_u"), 0.5, None, ALU.mult))
            pool.wait_ge(y_in_psum, E)
            n.done(pool.memset(q2bd, 0.0))
            st = Steps(pool, pool_step)
            pool.wait_ge(c3_dve, 1)
            st.done(pool.tensor_tensor(zc, ctxk[:, :, :], mv3[:, :, 0:1].to_broadcast([128, NC, DC]), ALU.subtract))
            pool.tensor_tensor(zc, zc, n3[:, 1, 0:NC].unsqueeze(2).to_broadcast([128, NC, DC]), ALU.mult).then_inc(c3_pool, 1)
            pool.wait_ge(c3_act, 12)
            pool.tensor_tensor(k3T[:, :].rearrange("p (k n) -> p k n", k=NC), kv3[:, :, 0:128], kv3[:, :, 0:128],
                               ALU.mult).then_inc(c3_pool, 1)
            pool.wait_ge(c3_dve, 2)
            pool.wait_ge(c3_pool, 2)
            for h in range(H3):
                pool.tensor_tensor(kv3[:, :, 64 * h:64 * h + 64], kv3[:, :, 64 * h:64 * h + 64],
                                   n3[:, 1, :].rearrange("p (k h) -> p k h", h=H3)[:, :, h:h + 1].to_broadcast([128, NC, D3]),
                                   ALU.mult).then_inc(c3_pool, 1)
                pool.wait_ge(c3_pool, 3 + h)
            pool.wait_ge(load["mask"], 64)
            pool.wait_ge(y_full, 3)
            n.done(pool.tensor_scalar(mask_add, mask_u8[:, :], 1.0, BIG, ALU.subtract, ALU.mult))
            n.done(pool.memset(padded, 0.0))
            n.done(pool.memset(cbd, 0.0))
            n.done(pool.memset(q3bd, 0.0))
            pool.wait_ge(load["taps"], 16)
            pool.tensor_tensor(tapped, taps, w("m_in", 128, 512, 768).unsqueeze(1).to_broadcast([128, TAPS, 256]),
                               ALU.mult).then_inc(tapped_ready, 1)

        SET_T, SET_C, SET_G, SET_U, SET_Z, SET_L3 = 1, 2, 3, 4, 5, 9

        @block.scalar
        def _(act):
            st = Steps(act, act_step)

            def turn_norm(n):
                act.wait_ge(xnT_in_psum, n + 1)
                act.copy(xnT[:, :], banks[7][:, 0:T]).then_inc(xnT_ready, 1)

            def context_keys(layer, b, bank):
                act.wait_ge(keys_in_psum, B * layer + b + 1)
                act.copy(big_b[:, b * SK:(b + 1) * SK], banks[bank][:, :]).then_inc(keys_ready, 1)

            def context_values(b, bank):
                act.wait_ge(v_in_psum, B + b + 1)
                act.copy(big_c[:, b * SK:(b + 1) * SK], banks[bank][:, :]).then_inc(v_ready, 1)

            def context_attention(layer):
                def bring(i):
                    act.wait_ge(qw_in_psum, i + 1)
                    out = big_b[0:DC, :].rearrange("p (b g h q) -> p g h b q", b=B, g=HG, h=4)[:, i]
                    act.copy(out, banks[QW_BANK[i]][0:DC, :].rearrange("p (h b q) -> p h b q", h=4, b=B)).then_inc(qw_act, 1)

                if layer == 2:
                    act.wait_ge(q_in_psum, 3)
                    act.wait_ge(pool_set, SET_Z)
                    for half in range(2):
                        p = slice(64 * half, 64 * half + 64)
                        ins = act.activation(q2bd[p, 0:4, half, :], banks[0][p, :].rearrange("p (a t) -> p a t", a=4),
                                             ACT.Copy, scale=D2 ** -0.5)
                    ins.then_inc(qw_act, 1)
                    bring(0)
                g0 = NG * layer
                for i in range(NG + 8):
                    if layer == 2:
                        j = i - 6
                        if j >= 0 and j % 4 == 3 and j < NG:
                            hg = j // 4
                            act.wait_ge(pcnT_in_psum, j + 1)
                            act.copy(big_c[0:DC, hg * 512:hg * 512 + 512], banks[6][0:DC, :]).then_inc(pcnT_ready, 1)
                        j = i - 8
                        if j >= 0 and j % 4 == 3:
                            hg = j // 4
                            act.wait_ge(o_in_psum, hg + 1)
                            act.copy(o2T[:, 2 * hg:2 * hg + 2, :],
                                     banks[7][:, 0:256].rearrange("p (a t) -> p a t", a=2)).then_inc(o2_ready, 1)
                    if i < NG:
                        g = g0 + i
                        if layer == 0:
                            act.wait_ge(clip_ready, g + 1)
                            if g >= 1:
                                act.wait_ge(guard_read, g)
                            act.activation(guard_out[:, :], banks[i % 2][:, :], ACT.Tanh,
                                           accum_out=nan_sum[:, i:i + 1]).then_inc(guard_read, 1)
                        act.wait_ge(negmax_ready, g + 1)
                        if g >= 2:
                            act.wait_ge(probsT_in_psum, g - 1)
                        src = clipped[:, i % 2, :] if layer == 0 else banks[i % 2][:, :]
                        act.activation(probs[:, i % 2, :], src, ACT.Exp, bias=negmax[:, i:i + 1],
                                       accum_out=den[:, i:i + 1]).then_inc(probs_ready, 1)
                    if layer == 0 and i in (0, 1, 3):
                        context_keys(0, *L0_KEYS[i])
                    if layer == 0 and 2 <= i <= NG + 1:
                        j = i - 2
                        act.wait_ge(probsT_in_psum, g0 + j + 1)
                        if j % HG == 0 and j >= 2 * HG:
                            act.wait_ge(pc_in_psum, B * layer + j // HG - 1)
                        act.copy(probs_turned(0, j), banks[2 + j % 2][:, :]).then_inc(probsT_ready, 1)
                    if layer == 2:
                        if i == 0:
                            bring(2)
                        j = i - 2
                        if j % 2 == 1 and 0 <= j < NG:
                            act.wait_ge(probsT_in_psum, g0 + j + 1)
                            if j >= 2:
                                act.wait_ge(pc_in_psum, 2 * B + j - 1)
                            act.copy(probsT[:, j % 2, :], banks[2 + j % 2][:, :]).then_inc(probsT_act, 1)

            def feed_forward(layer):
                e0 = E * layer
                C = FFN_CHUNKS[layer] * 128
                k = {0: 0, 1: 1, 3: 2}.get(layer)
                for e in range(E):
                    n = e0 + e
                    if e == (1 if layer else 0) and k is not None:
                        act.wait_ge(lneg_ready, k + 1)
                        act.activation(sc8[:, :], lg[:, :], ACT.Exp, bias=rt[:, 0:1],
                                       accum_out=rt[:, 1:2]).then_inc(lexp_ready, 1)
                    if layer == 0:
                        act.wait_ge(gate_in_psum, n + 1)
                        if e >= 3:
                            act.wait_ge(y_in_psum, n - 2)
                        act.activation(hid[:, e % 3, 0:T], banks[e % 2][:, 0:T], ACT.Relu,
                                       bias=w("f0_b1", 128, 2 * e, 2 * e + 1)).then_inc(hid_act, 1)
                        if e in (2, 3):
                            context_values(e, 7)
                        elif e >= 4:
                            context_keys(1, e - 4, 7)
                    else:
                        act.wait_ge(gate_in_psum, n + 1)
                        if e >= 2:
                            act.wait_ge(hid_ready, n - 1)
                        act.activation(tg[:, e % 2, 0:C], banks[e % 2][:, 0:C], ACT.Tanh, scale=0.5).then_inc(tanh_ready, 1)

            def linear_attention():
                act.wait_ge(mix_pe, 2)
                act.copy(o_tok[:, :], banks[2][:, 0:D]).then_inc(mix_act, 1)

            def causal_attention():
                act.wait_ge(mix_pe, LIN_PE + 2)
                act.copy(o_tok[:, :], banks[2][:, 0:D]).then_inc(mix_act, 1)
                for hg in range(HG):
                    act.wait_ge(mix_dve, LIN_DVE + 2 + hg)
                    part = s_sb[:, 4 * hg:4 * hg + 4, :]
                    act.activation(part, part, ACT.Exp, scale=DH ** -0.5).then_inc(mix_act, 1)

            def lstm():
                for t in range(B):
                    act.wait_ge(mix_pe, CAU_PE + 1 + t)
                    g = banks[0][:, t * 128:(t + 1) * 128]
                    act.activation(gates[:, 0:3, :], g[:, 0:96].rearrange("p (g b) -> p g b", g=3), ACT.Tanh, scale=0.5)
                    act.activation(gates[:, 3, :], g[:, 96:128], ACT.Tanh).then_inc(mix_act, 1)
                    act.wait_ge(mix_dve, CAU_DVE + 2 * t + 1)
                    act.activation(cst[:, 3, :], cst[:, 2, :], ACT.Tanh, scale=0.5).then_inc(mix_act, 1)
                    context3_keys(t)

            def context3_turned():
                act.wait_ge(load["late"], 16)
                for i in range(4):
                    act.wait_ge(c3_pe, i + 1)
                    act.activation(big_c[0:DC, i * 512:i * 512 + 512], banks[3 + i][0:DC, :], ACT.Identity,
                                   bias=w("x3_b", DC), scale=w("x3_g", DC)).then_inc(c3_act, 1)

            def context3_kv(first, last):
                for i in range(first, last):
                    act.wait_ge(c3_pe, 4 + i + 1)
                    act.copy(kv3[:, 2 * i:2 * i + 2, :],
                             banks[3 + i % 4][:, :].rearrange("p (a n) -> p a n", a=2)).then_inc(c3_act, 1)

            def context3_keys(i):
                act.wait_ge(c3_pe, 12 + i + 1)
                act.copy(k3T[:, i * 512:i * 512 + 512], banks[3 + i][:, :]).then_inc(c3_act, 1)

            def cross3():
                act.wait_ge(c3_pe, 16 + 1)
                act.copy(qkv3, banks[0][:, 0:384]).then_inc(c3_act, 1)
                for h in range(H3):
                    act.wait_ge(c3_dve, 7 + h)
                    act.activation(big_a[:, h * 640:h * 640 + 640], big_a[:, h * 640:h * 640 + 640], ACT.Exp,
                                   bias=d3[:, h:h + 1], accum_out=d3[:, 2 + h:3 + h]).then_inc(c3_act, 1)
                act.wait_ge(c3_pe, 21)
                act.copy(big_b[:, 0:512], banks[0][:, :])
                act.copy(big_b[:, 1024:1024 + T], banks[2][:, 0:T]).then_inc(c3_act, 1)

            def state_space():
                a0 = ACT0
                act.wait_ge(pool_set, SET_L3)
                act.copy(xpad[:, :, PAD:PAD + S], banks[7][:, 0:T].rearrange("p (b s) -> p b s", b=B)).then_inc(mix_act, 1)
                act.wait_ge(mix_dve, DV0 + 1)
                st.done(act.activation(dts[:, 1, :], dts[:, 0, :], ACT.Abs))
                act.activation(dts[:, 1, :], dts[:, 1, :], ACT.Exp, scale=-1.0).then_inc(mix_act, 1)
                act.activation(dts[:, 5, 0:4], row("alog"), ACT.Exp).then_inc(mix_act, 1)
                act.wait_ge(mix_act, a0 + 2)
                act.activation(dts[:, 2, :], dts[:, 1, :], ACT.Ln, bias=1.0).then_inc(mix_act, 1)
                act.wait_ge(mix_pe, PE0 + 2)
                for j in (2, 3):
                    conv = banks[4][:, (j - 2) * T:(j - 1) * T]
                    act.activation(big_b[:, j * T:(j + 1) * T], conv, ACT.Identity, bias=half_taps[:, 28 + j:29 + j], scale=0.5)
                    ins = act.activation(big_b[:, 512 + j * T:512 + (j + 1) * T], conv, ACT.Tanh, bias=half_taps[:, 28 + j:29 + j], scale=0.5)
                ins.then_inc(mix_act, 1)
                act.wait_ge(mix_pe, PE0 + 3)
                act.activation(big_c[:, 0:256], banks[1][:, 0:256], ACT.Tanh, scale=0.5).then_inc(mix_act, 1)
                for i in range(2):
                    act.wait_ge(mix_pe, PE0 + 4 + i)
                    act.activation(big_a[:, 1024 + 512 * i:1536 + 512 * i], banks[2 + i][:, :], ACT.Exp,
                                   scale=-1.0).then_inc(mix_act, 1)
                act.wait_ge(mix_dve, DV0 + 3)
                act.activation(big_b[:, 512:768], big_b[:, 0:256], ACT.Tanh).then_inc(mix_act, 1)
                act.wait_ge(mix_dve, DV0 + 8)
                act.activation(big_c[:, 1536:1792], big_c[:, 1024:1280], ACT.Square,
                               accum_out=nw[:, 0:1]).then_inc(mix_act, 1)

            ACT0, DV0, PE0 = CAU_ACT + 2 * B, CAU_DVE + 2 * B, CAU_PE + B + 1

            context_keys(0, *L0_KEYS[-1])
            turn_norm(0)
            context_attention(0)
            turn_norm(1); linear_attention()
            context_values(0, 3)
            context_values(1, 4)
            turn_norm(2); feed_forward(0)
            turn_norm(3); context_attention(1)
            context3_turned()
            turn_norm(4); causal_attention()
            context3_kv(0, 4)
            turn_norm(5); feed_forward(1)
            context3_kv(4, 8)
            turn_norm(6); context_attention(2)
            turn_norm(7); lstm()
            turn_norm(8); feed_forward(2)
            cross3()
            turn_norm(9); state_space()
            turn_norm(10); feed_forward(3)

        @block.tensor
        def _(pe):
            def keep_warm(n):
                pe.wait_ge(x_ready, n)
                for _ in range(KEEP_WARM):
                    pe.transpose(banks[7][:, 0:T], ident, ident)

            def turn_norm(n):
                pe.wait_ge(xn_ready, n + 1)
                pe.transpose(banks[7][:, 0:T], xn[:, :], ident).then_inc(xnT_in_psum, 1)
                pe.wait_ge(xnT_ready, n + 1)

            def context_keys(layer, b, bank):
                pe.matmul(banks[bank][:, :], w(f"wk{layer}", CA), ctxT[:, b * SK:(b + 1) * SK], start=True, stop=True).then_inc(keys_in_psum, 1)

            def context_values(layer, b, bank):
                for c in range(CK):
                    k = b * CK + c
                    ins = pe.matmul(banks[bank][:, c * 128:(c + 1) * 128], ctxT[:, k * 128:(k + 1) * 128], w(f"wv{layer}", CA),
                                    start=True, stop=True)
                ins.then_inc(v_in_psum, 1)

            def context_attention(layer):
                g0 = NG * layer

                def quarter(k):
                    pe.wait_ge((qw_act, qw_dve)[k // 2], 1)
                    for p in (2 * k, 2 * k + 1):
                        ins = pe.matmul(banks[QW_BANK[k]][0:DC, (p % 2) * 256:(p % 2) * 256 + 256], x2_wkT[:, p, :],
                                        q2bd[:, p, :, :], start=True, stop=True)
                    ins.then_inc(qw_in_psum, 1)

                if layer < 2:
                    wq, wo = (w(f"{n}{layer}") for n in ("wq", "wo"))
                    pe.matmul(banks[2][:, 0:T], wq, xnT[:, :], start=True, stop=True).then_inc(q_in_psum, 1)
                else:
                    pe.wait_ge(load["x2"], 64)
                    for p in range(8):
                        ins = pe.matmul(banks[p // 4][:, (p % 4) * 128:(p % 4) * 128 + 128], x2_wq[:, p * 128:(p + 1) * 128],
                                        xnT[:, :], start=True, stop=True)
                        if p % 4 == 3:
                            ins.then_inc(q_in_psum, 1)
                    quarter(0)
                    quarter(1)

                def group(i):
                    return (i // HG, i % HG) if layer < 2 else (i % B, i // B)

                def scores(i):
                    b, hg = group(i)
                    if i % 4 == 0:
                        k = i // 4
                        if layer < 2:
                            pe.wait_ge(qbd_ready, B * layer + k + 1)
                            pe.wait_ge(keys_ready, B * layer + k + 1)
                        else:
                            pe.wait_ge((qw_act, qw_dve)[k % 2], k // 2 + 2)
                    if i >= 2:
                        if layer == 0:
                            pe.wait_ge(guard_read, g0 + i - 1)
                        else:
                            pe.wait_ge(probs_ready, g0 + i - 1)
                    k = b * HG + hg
                    if layer < 2:
                        q, keys = big_a[:, k * 128:(k + 1) * 128], big_b[:, b * SK:(b + 1) * SK]
                    else:
                        q, keys = big_b[0:DC, k * 128:(k + 1) * 128], ctxT[0:DC, b * SK:(b + 1) * SK]
                    pe.matmul(banks[i % 2][:, :], q, keys, start=True, stop=True).then_inc(scores_in_psum, 1)

                def turned(i):
                    if layer < 2:
                        pe.wait_ge(probsT_ready, g0 + i + 1)
                    elif i % 2 == 0:
                        pe.wait_ge(probsT_ready, g0 + i // 2 + 1)
                    else:
                        pe.wait_ge(probsT_act, i // 2 + 1)

                def turn_probs(i):
                    pe.wait_ge(probs_ready, g0 + i + 1)
                    if i >= 2:
                        turned(i - 2)
                    for c in range(CK):
                        ins = pe.transpose(banks[2 + i % 2][:, c * 128:(c + 1) * 128], probs[:, i % 2, c * 128:(c + 1) * 128], ident)
                    ins.then_inc(probsT_in_psum, 1)

                def weighted(b, c):
                    if c == 0:
                        pe.wait_ge(probsT_ready, g0 + HG * (b + 1))
                        pe.wait_ge(v_ready, B * layer + b + 1)
                        if b >= 2:
                            pe.wait_ge(own_ready, B * layer + b - 1)
                    for hg in range(HG):
                        k = b * CK + c
                        ins = pe.matmul(banks[4 + b % 2][32 * hg:32 * hg + 32, 0:128], big_c[:, k * D + 32 * hg:k * D + 32 * hg + 32],
                                        probs_turned(layer, b * HG + hg)[:, c * 128:(c + 1) * 128],
                                        start=c == 0, stop=c == CK - 1, skip_group_check=True)
                    if c == CK - 1:
                        ins.then_inc(pc_in_psum, 1)

                def uniform_values(c):
                    if c == 0:
                        pe.wait_ge(v_ready, 4)
                        pe.wait_ge(pool_set, SET_C)
                    for b in range(B):
                        k = b * CK + c
                        ins = pe.matmul(banks[7][b * S:(b + 1) * S, 0:D], uniform[:, :], big_c[:, k * D:(k + 1) * D],
                                        start=c == 0, stop=c == CK - 1, skip_group_check=True)
                    if c == CK - 1:
                        ins.then_inc(mean_in_psum, 1)

                def turn_inverse(b):
                    pe.wait_ge(inverse_ready, B * layer + b + 1)
                    if b:
                        pe.wait_ge(inverse_out, B * layer + b)
                    elif layer == 0:
                        pe.wait_ge(v_ready, 3)
                    pe.transpose(banks[6][:, 0:128], inverse[:, :, :].rearrange("p g n -> p (g n)"), ident).then_inc(inverse_in_psum, 1)

                def weighted_context(i):
                    b, hg = group(i)
                    turned(i)
                    if i == 0:
                        pe.wait_ge(qw_act, 3)
                        pe.wait_ge(qw_dve, 3)
                    if i >= 2:
                        pe.wait_ge(pcn_ready, i - 1)
                    for c in range(CK):
                        ins = pe.matmul(banks[4 + i % 2][:, 0:DC], probsT[:, i % 2, c * 128:(c + 1) * 128],
                                        ctxk[:, b * CK + c, :], start=c == 0, stop=c == CK - 1)
                    ins.then_inc(pc_in_psum, 1)

                def turn_weighted(i):
                    b, hg = group(i)
                    pe.wait_ge(pcn_ready, i + 1)
                    if b == 0 and hg >= 1:
                        pe.wait_ge(pcnT_ready, hg)
                    pe.transpose(banks[6][0:DC, b * 128:b * 128 + 128], pcn[:, i % 4, :], ident).then_inc(pcnT_in_psum, 1)

                def project(first, last):
                    for p in range(first, last):
                        if p % 2 == 0:
                            pe.wait_ge(o2_ready, p // 2 + 1)
                        ins = pe.matmul(banks[2][:, 0:D], o2T[:, p, :], x2_wo[:, p, :], start=p == 0, stop=p == 7)
                    if last == 8:
                        ins.then_inc(y_full, 1)

                def values(hg):
                    pc = big_c[0:DC, hg * 512:(hg + 1) * 512].rearrange("p (b h q) -> p h b q", b=B, h=4)
                    pe.wait_ge(pcnT_ready, hg + 1)
                    if hg:
                        pe.wait_ge(o2_ready, hg)
                    for k in range(4):
                        h = 4 * hg + k
                        ins = pe.matmul(banks[7][64 * (k % 2):64 * (k % 2) + 64, (k // 2) * 128:(k // 2) * 128 + 128],
                                        x2_wv[:, h * D2:(h + 1) * D2], pc[:, k], start=True, stop=True)
                    ins.then_inc(o_in_psum, 1)

                for i in range(NG + 7):
                    if i < NG:
                        scores(i)
                    if layer == 2 and i < 2:
                        quarter(2 + i)
                    if 2 <= i <= NG + 1:
                        turn_probs(i - 2)
                    if layer == 0 and i in L0_KEYS:
                        b, bank = L0_KEYS[i]
                        if b == 3:
                            pe.wait_ge(keys_ready, 3)
                        context_keys(0, b, bank)
                    if layer == 0 and i in L0_VALUES:
                        b, bank = L0_VALUES[i]
                        if b == 2:
                            pe.wait_ge(keys_ready, 4)
                        elif b:
                            pe.wait_ge(v_ready, b // 2 + 1)
                        context_values(0, b, bank)
                    if layer == 0 and 9 <= i < 9 + CK:
                        uniform_values(i - 9)
                    if layer == 0 and i == 14:
                        pe.wait_ge(mean_ready, 1)
                        pe.transpose(banks[7][:, 128:256], mean_tok, ident)
                    if layer < 2:
                        if 6 <= i < NG + 6:
                            weighted((i - 6) // CK, (i - 6) % CK)
                        if 6 <= i < NG + 6 and (i - 6) % CK == 1:
                            turn_inverse((i - 6) // CK)
                    else:
                        if 3 <= i <= NG + 2:
                            weighted_context(i - 3)
                        if 5 <= i <= NG + 4:
                            turn_weighted(i - 5)
                        if i == NG + 6:
                            project(0, 6)
                        if i >= 10 and (i - 10) % 4 == 0:
                            values((i - 10) // 4)
                    if layer == 0 and i == NG + 1:
                        pe.wait_ge(nan_ready, 1)
                        pe.matmul(banks[7][:, 256:256 + NG], w("ones"), nan_hit[:, :], start=True, stop=True).then_inc(nan_in_psum, 1)
                if layer < 2:
                    pe.wait_ge(oT_ready, layer + 1)
                    pe.matmul(banks[2][:, 0:D], oT[:, :], wo, start=True, stop=True).then_inc(y_full, 1)
                else:
                    project(6, 8)

            def feed_forward(layer):
                e0 = E * layer
                C = FFN_CHUNKS[layer]
                pe.wait_ge(load["late"], 16)
                pe.matmul(banks[7][:, 256:264], xnT[:, :], w(f"f{layer}_wr"), start=True, stop=True).then_inc(logits_in_psum, 1)
                if layer == 0:
                    pe.wait_ge(load["f0"], 32)
                elif layer == 1:
                    pe.wait_ge(load["f1"], 32)
                elif layer == 2:
                    pe.wait_ge(load["f2"], 48)
                else:
                    pe.wait_ge(load["f3up"], 32)
                    pe.wait_ge(load["f3gate"], 16)
                    pe.wait_ge(load["f3down"], 32)

                def gate_w(e, c):
                    if layer == 1:
                        return f1_w13[:, e, c * 128:(c + 1) * 128]
                    return (f2_wg if layer == 2 else f3_wg)[:, e, c * 128:(c + 1) * 128]

                def up_w(e, c):
                    if layer == 1:
                        return f1_w13[:, e, 256 + c * 128:256 + (c + 1) * 128]
                    return (f2_wu[:, e, :] if layer == 2 else f3_wu[e // 4][:, e % 4, :])[:, c * 128:(c + 1) * 128]

                def down_w(e, c):
                    if layer == 3:
                        return f3_wd[e // 4][:, e % 4, c * 128:(c + 1) * 128]
                    return {0: f0_w2, 1: f1_w2, 2: f2_wd}[layer][:, e, c * 128:(c + 1) * 128]

                def up(e):
                    n = e0 + e
                    if e >= 2:
                        pe.wait_ge(hid_ready, n - 1)
                        if layer == 0:
                            pe.wait_ge(hid_act, n - 1)
                    if layer == 0:
                        pe.matmul(banks[e % 2][:, 0:T], f0_w1[:, e, 0:128], xnT[:, :], start=True, stop=True).then_inc(gate_in_psum, 1)
                        pe.matmul(banks[2 + e % 2][:, 0:T], f0_w1[:, e, 128:256], xnT[:, :], start=True, stop=True).then_inc(up_in_psum, 1)
                        return
                    for wt, bank, s in ((gate_w, banks[e % 2], gate_in_psum), (up_w, banks[2 + e % 2], up_in_psum)):
                        for c in range(C):
                            ins = pe.matmul(bank[:, c * T:(c + 1) * T], wt(e, c), xnT[:, :], start=True, stop=True)
                        ins.then_inc(s, 1)

                def down(e):
                    n = e0 + e
                    pe.wait_ge(hid_ready, n + 1)
                    if layer == 0:
                        pe.wait_ge(hid_act, n + 1)
                    if e >= 3:
                        pe.wait_ge(y_added, Y_BASE[layer] + e - 2)
                    for c in range(C):
                        ins = pe.matmul(banks[4 + e % 3][:, 0:D], hid[:, e % 3, c * T:(c + 1) * T], down_w(e, c),
                                        start=c == 0, stop=c == C - 1)
                    ins.then_inc(y_in_psum, 1)

                for e in range(E + 2):
                    if e < E:
                        up(e)
                    if layer == 3 and e == 3:
                        pe.wait_ge(cw_ready, 2)
                        pe.matmul(banks[7][:, 0:16], w("cum"), oh[:, :, :], start=True, stop=True).then_inc(cwT_in_psum, 1)
                    if e >= 2:
                        down(e - 2)
                    if layer == 0 and 2 <= e < E:
                        if e == 2:
                            pe.wait_ge(lneg_ready, 1)
                        elif e <= 4:
                            pe.wait_ge(v_ready, B + e)
                        else:
                            pe.wait_ge(keys_ready, B + e - 4)
                        if e < 4:
                            context_values(1, e, 7)
                        else:
                            context_keys(1, e - 4, 7)
                if layer == 0:
                    pe.wait_ge(cw_ready, 1)
                    pe.wait_ge(keys_ready, 2 * B)
                    pe.transpose(banks[7][0:8, 0:T], cw[:, :], ident).then_inc(cwT_in_psum, 1)
                    pe.wait_ge(cwT_ready, 1)
                    pe.matmul(banks[7][:, 256:256 + D], cwT[:, :], w("f0_b2", 8), start=True, stop=True).then_inc(cwT_in_psum, 1)

            def token_attention(dve0, act0, shifted):
                pe.wait_ge(mix_dve, dve0 + 1)
                for hg in range(HG):
                    rows_ = slice(32 * hg, 32 * hg + 32)
                    for b in range(B):
                        ins = pe.matmul(banks[3 + hg][b * S:(b + 1) * S, 0:128], qk_[rows_, 0, b * S:(b + 1) * S],
                                        k_own[rows_, b, :, :], start=True, stop=True, skip_group_check=True)
                    ins.then_inc(mix_pe, 1)
                pe.wait_ge(mix_dve, dve0 + shifted + 2)
                pe.wait_ge(mix_act, act0)
                for b in range(B):
                    rows_ = slice(b * S, (b + 1) * S)
                    for hg in range(HG):
                        ins = pe.matmul(banks[VALUE_BANK[b]][32 * hg:32 * hg + 32, 0:128], o_tok[rows_, 32 * hg:32 * hg + 32],
                                        pT_sb[rows_, 4 * hg:4 * hg + 4, :], start=True, stop=True, skip_group_check=True)
                    ins.then_inc(mix_pe, 1)
                pe.wait_ge(mix_dve, dve0 + shifted + 3)
                pe.transpose(banks[7][:, 0:T], inverse[:, :, :].rearrange("p g n -> p (g n)"), ident).then_inc(mix_pe, 1)
                pe.wait_ge(mix_dve, dve0 + shifted + 4)

            def linear_attention():
                pe.wait_ge(load["late"], 16)
                pe.matmul(banks[0][:, 0:T], w("a_wq"), xnT[:, :], start=True, stop=True)
                pe.matmul(banks[0][:, T:2 * T], w("a_wk"), xnT[:, :], start=True, stop=True).then_inc(mix_pe, 1)
                pe.matmul(banks[2][:, 0:D], xnT[:, :], w("a_wv"), start=True, stop=True).then_inc(mix_pe, 1)
                token_attention(0, 1, 0)
                pe.matmul(banks[2][:, 0:D], oT[:, :], w("a_wo"), start=True, stop=True).then_inc(mix_pe, 1)

            def causal_attention():
                for bank, a in ((banks[0], 0), (banks[1], 128)):
                    pe.matmul(bank[:, 0:T], w("r_wq", 128, a, a + 128), xnT[:, :], start=True, stop=True)
                    ins = pe.matmul(bank[:, T:2 * T], w("r_wk", 128, a, a + 128), xnT[:, :], start=True, stop=True)
                ins.then_inc(mix_pe, 1)
                pe.matmul(banks[2][:, 0:D], xnT[:, :], w("r_wv"), start=True, stop=True).then_inc(mix_pe, 1)
                token_attention(LIN_DVE, 2, HG)
                pe.matmul(banks[2][:, 0:D], oT[:, :], w("r_wo"), start=True, stop=True).then_inc(mix_pe, 1)

            lstm_gates = banks[0][:, :].rearrange("p (t g b) -> p g t b", t=B, g=4)

            def lstm_bias():
                pe.wait_ge(load["rows"], 16)
                for k in range(4):
                    pe.matmul(lstm_gates[:, k], row("lstm_b", k * 128, k * 128 + 128, 1), w("ones", 1),
                              start=k == 0, stop=False, skip_group_check=True)

            def lstm():
                for k in range(4):
                    ins = pe.matmul(lstm_gates[:, k], w("lstm_w", 128, k * 128, k * 128 + 128), xnT[:, :],
                                    start=False, stop=k == 3, skip_group_check=True)
                ins.then_inc(mix_pe, 1)
                pe.wait_ge(pool_set, SET_U)
                context3_keys(0)
                for t in range(1, B):
                    pe.wait_ge(mix_dve, CAU_DVE + 2 * t)
                    for k in range(4):
                        ins = pe.matmul(banks[0][:, t * 128 + k * S:t * 128 + (k + 1) * S], u_half[:, k * 128:(k + 1) * 128],
                                        h2T[:, (t - 1) * S:t * S], start=False, stop=True, skip_group_check=True)
                    ins.then_inc(mix_pe, 1)
                    context3_keys(t)
                pe.wait_ge(mix_dve, CAU_DVE + 2 * B)
                pe.transpose(banks[1][:, 0:D], h2T[:, :], ident).then_inc(mix_pe, 1)

            def context3_turned():
                pe.wait_ge(c3_pool, 1)
                for i in range(4):
                    for c in range(4):
                        ins = pe.transpose(banks[3 + i][0:DC, c * 128:(c + 1) * 128], zc[:, 4 * i + c, :], ident)
                    ins.then_inc(c3_pe, 1)

            def context3_kv(first, last):
                for i in range(first, last):
                    pe.wait_ge(c3_act, 4 + max(i - 3, 0))
                    if i == 5:
                        pe.wait_ge(y_added, Y_BASE[2])
                    if i == 6:
                        pe.wait_ge(x_ready, 6)
                    for c in range(2):
                        k = 2 * i + c
                        ins = pe.matmul(banks[3 + i % 4][:, c * 256:(c + 1) * 256], big_c[0:DC, k * 128:(k + 1) * 128],
                                        w("x3_wkv", DC), start=True, stop=True)
                    ins.then_inc(c3_pe, 1)

            def context3_keys(i):
                pe.wait_ge(c3_pool, 4)
                for c in range(4):
                    ins = pe.transpose(banks[3 + i][:, c * 128:(c + 1) * 128], kv3[:, 4 * i + c, 0:128], ident)
                ins.then_inc(c3_pe, 1)

            def cross3():
                pe.wait_ge(c3_dve, 3)
                pe.transpose(banks[7][:, 0:T], z2[:, :], ident).then_inc(q_in_psum, 1)
                pe.wait_ge(c3_dve, 4)
                pe.wait_ge(c3_act, 16)
                pe.matmul(banks[0][:, 0:384], xnT[:, :], w("x3_wqkv"), start=True, stop=True).then_inc(c3_pe, 1)
                pe.wait_ge(c3_dve, 5)
                pe.transpose(banks[1][:, 0:T], xn[:, :], ident)
                pe.transpose(banks[2][:, 0:T], z2[:, :], ident).then_inc(c3_pe, 1)
                pe.wait_ge(c3_dve, 6)
                for h in range(H3):
                    for b in range(B):
                        pe.matmul(banks[3 + h][b * S:(b + 1) * S, :], q3bd[:, h, b * S:(b + 1) * S],
                                  k3T[:, b * SK:(b + 1) * SK], start=True, stop=True)
                    pe.matmul(banks[5 + h][:, 0:T], q3bd[:, h, :], kl3T, start=True, stop=True).then_inc(c3_pe, 1)
                for h in range(H3):
                    pe.wait_ge(c3_act, 18 + h)
                    for c in range(4):
                        pe.transpose(banks[h][:, c * 128:(c + 1) * 128], big_a[:, h * 640 + c * 128:h * 640 + (c + 1) * 128], ident)
                    pe.transpose((banks[2], banks[7])[h][:, 0:T], big_a[:, h * 640 + 512:h * 640 + 640], ident).then_inc(c3_pe, 1)
                pe.wait_ge(c3_dve, 9)
                pe.transpose(banks[5][:, 0:T], inverse[:, :, :].rearrange("p g n -> p (g n)"), ident).then_inc(c3_pe, 1)
                pe.wait_ge(c3_act, 20)
                pe.wait_ge(c3_dve, 10)
                both = [(slice(64 * h, 64 * h + 64), h) for h in range(H3)]
                for p, h in both:
                    pe.matmul(banks[6][p, 0:T], qkv3[:, 256 + 64 * h:320 + 64 * h], big_b[:, 1024 + h * T:1024 + (h + 1) * T],
                              start=True, stop=False, skip_group_check=True)
                for b in range(B):
                    for c in range(CK):
                        for p, h in both:
                            ins = pe.matmul(banks[6][p, b * S:(b + 1) * S], kv3[:, b * CK + c, 128 + 64 * h:192 + 64 * h],
                                            big_b[:, h * 512 + c * 128 + b * S:h * 512 + c * 128 + (b + 1) * S],
                                            start=False, stop=c == CK - 1, skip_group_check=True)
                ins.then_inc(c3_pe, 1)
                pe.wait_ge(c3_dve, 11)
                pe.matmul(banks[0][:, 0:D], oT[:, :], w("x3_wo"), start=True, stop=True).then_inc(y_full, 1)

            def state_space():
                d = CAU_DVE + 2 * B
                pe.matmul(banks[6][:, 256:264], xnT[:, :], w("m_in", 128, 768, 776), start=True, stop=True)
                for j in range(2):
                    ins = pe.matmul(banks[0][:, j * T:(j + 1) * T], w("m_in", 128, 256 + j * 128, 384 + j * 128), xnT[:, :],
                                    start=True, stop=True)
                ins.then_inc(mix_pe, 1)
                pe.wait_ge(tapped_ready, 1)
                pe.wait_ge(mix_act, CAU_ACT + 2 * B + 1)
                for j in range(2):
                    for k in range(TAPS):
                        ins = pe.matmul(banks[4][:, j * T:(j + 1) * T], tapped[:, k, j * 128:(j + 1) * 128], xpad[:, :, k:k + S],
                                        start=k == 0, stop=k == TAPS - 1)
                ins.then_inc(mix_pe, 1)
                pe.matmul(banks[1][:, 0:256], xnT[:, :], w("m_in", 128, 0, 256), start=True, stop=True).then_inc(mix_pe, 1)
                pe.wait_ge(mix_dve, d + 2)
                for i, name in enumerate(("l_fw", "l_bw")):
                    pe.matmul(banks[2 + i][:, :], w(name), big_a[:, i * 512:i * 512 + 512], start=True, stop=True).then_inc(mix_pe, 1)
                pe.wait_ge(mix_dve, d + 5)
                pe.matmul(banks[5][:, 0:256], big_b[:, 1280:1408], cbd, start=True, stop=True).then_inc(mix_pe, 1)
                pe.wait_ge(mix_dve, d + 6)
                for j in range(2):
                    pe.transpose(banks[4][:, j * 128:(j + 1) * 128], big_b[:, 1024 + j * 128:1024 + (j + 1) * 128], ident)
                for j in range(2):
                    ins = pe.matmul(banks[6][:, 0:4], big_b[:, 1024 + j * 128:1024 + (j + 1) * 128], w("m_fc", 128, 4 * j, 4 * j + 4),
                                    start=j == 0, stop=j == 1)
                ins.then_inc(mix_pe, 1)
                pe.wait_ge(mix_dve, d + 7)
                for h in range(NH):
                    for way in range(2):
                        ins = pe.matmul(banks[0][:, h * 64:(h + 1) * 64],
                                        big_a[:, 1024 + way * 512 + h * T:1024 + way * 512 + (h + 1) * T],
                                        big_c[:, 256 + h * 64:256 + (h + 1) * 64], start=way == 0, stop=way == 1)
                ins.then_inc(mix_pe, 1)
                pe.wait_ge(mix_dve, d + 9)
                for j in range(2):
                    ins = pe.transpose(banks[1][:, j * 128:(j + 1) * 128], big_c[:, 1024 + j * 128:1024 + (j + 1) * 128], ident)
                ins.then_inc(mix_pe, 1)
                pe.wait_ge(mix_dve, d + 10)
                for j in range(2):
                    ins = pe.matmul(banks[2][:, 0:D], big_c[:, 1280 + j * 128:1280 + (j + 1) * 128],
                                    w("m_out", 128, j * 128, (j + 1) * 128), start=j == 0, stop=j == 1)
                ins.then_inc(mix_pe, 1)

            pe.wait_ge(load["early"], 16)
            pe.wait_ge(load["ctxT"], 16)
            pe.wait_ge(pool_set, SET_T)
            context_keys(0, *L0_KEYS[-1])
            turn_norm(0)
            context_attention(0)
            keep_warm(1); turn_norm(1); linear_attention()
            context_values(1, 0, 3)
            context_values(1, 1, 4)
            keep_warm(2); turn_norm(2); feed_forward(0)
            keep_warm(3); turn_norm(3); context_attention(1)
            context3_turned()
            keep_warm(4); turn_norm(4); causal_attention()
            context3_kv(0, 4)
            keep_warm(5); turn_norm(5); feed_forward(1)
            context3_kv(4, 8)
            keep_warm(6); turn_norm(6); context_attention(2)
            lstm_bias()
            keep_warm(7); turn_norm(7); lstm()
            keep_warm(8); turn_norm(8); feed_forward(2)
            keep_warm(9)
            cross3()
            keep_warm(10); turn_norm(9); state_space()
            keep_warm(11); turn_norm(10); feed_forward(3)

        @block.vector
        def _(v):
            st = Steps(v, dve_step)

            def rsqrt_guess(y, a):
                return v.tensor_scalar(y.bitcast(I32), a.bitcast(I32), -0.5, RSQRT_MAGIC, ALU.mult, ALU.add)

            def rsqrt_step(k, y, a, t):
                if k == 0:
                    return rsqrt_guess(y, a)
                if k in (1, 4):
                    return v.tensor_tensor(t, y, y, ALU.mult)
                if k in (2, 5):
                    return v.scalar_tensor_tensor(out=t, in0=t, scalar=1.0 if k == 2 else KAPPA / 4, in1=a, op0=ALU.mult, op1=ALU.mult)
                if k == 3:
                    return v.scalar_tensor_tensor(out=y, in0=t, scalar=3.0, in1=y, op0=ALU.subtract, op1=ALU.mult)
                if k == 6:
                    return v.scalar_tensor_tensor(out=t, in0=t, scalar=-10 / 3 * KAPPA, in1=t, op0=ALU.add, op1=ALU.mult)
                return v.scalar_tensor_tensor(out=y, in0=t, scalar=15 / 16, in1=y, op0=ALU.add, op1=ALU.mult)

            RSQRT_STEPS = 8

            def rsqrt(y, a, t):
                for k in range(RSQRT_STEPS):
                    st.done(rsqrt_step(k, y, a, t))

            def rsqrt_column():
                a, y, t, scaled = (nw[:, k:k + 1] for k in range(4))
                guess = st.count(rsqrt_guess(y, a))
                v.tensor_scalar(scaled, a, KAPPA / 4, None, ALU.mult)
                st.after(guess)
                st.done(v.scalar_tensor_tensor(out=t, in0=y, scalar=y, in1=a, op0=ALU.mult, op1=ALU.mult))
                st.done(rsqrt_step(3, y, a, t))
                st.done(v.scalar_tensor_tensor(out=t, in0=y, scalar=y, in1=scaled, op0=ALU.mult, op1=ALU.mult))
                st.done(rsqrt_step(6, y, a, t))
                st.done(rsqrt_step(7, y, a, t))

            def layer_norm(out, src):
                st.done(v.bn_stats(stats[:, :], src))
                st.done(v.bn_aggr(mv[:, :], stats[:, :]))
                st.done(v.tensor_scalar(nw[:, 0:1], mv[:, 1:2], LN_EPS, None, ALU.add))
                rsqrt_column()
                return v.tensor_scalar(out, src, mv[:, 0:1], nw[:, 1:2], ALU.subtract, ALU.mult)

            def norm(n):
                if n:
                    v.wait_ge(x_ready, n)
                layer_norm(xn[:, :], x[:, :]).then_inc(xn_ready, 1)

            def context3_stats(first, last):
                for k in range(first, last):
                    st.done(v.bn_stats(st3[:, k, :], ctxk[:, k, :]))
                    v.bn_aggr(mv3[:, k, :], st3[:, k, :])

            def context_attention(layer):
                g0 = NG * layer

                def bring(i):
                    v.wait_ge(qw_in_psum, i + 1)
                    out = big_b[0:DC, :].rearrange("p (b g h q) -> p g h b q", b=B, g=HG, h=4)[:, i]
                    v.tensor_copy(out, banks[QW_BANK[i]][0:DC, :].rearrange("p (h b q) -> p h b q", h=4, b=B)).then_inc(qw_dve, 1)

                if layer < 2:
                    v.wait_ge(q_in_psum, layer + 1)
                    st.done(v.tensor_scalar(qT[:, :], banks[2][:, 0:T], w(f"bq{layer}"), DH ** -0.5, ALU.add, ALU.mult))
                    for b in range(B):
                        v.tensor_tensor(big_a[:, b * 512:b * 512 + 512].rearrange("p (h q) -> p h q", h=H),
                                        qT[:, b * S:(b + 1) * S].unsqueeze(1).to_broadcast([128, H, S]),
                                        w("head16").unsqueeze(2).to_broadcast([128, H, S]), ALU.mult).then_inc(qbd_ready, 1)
                else:
                    v.wait_ge(q_in_psum, 4)
                    v.wait_ge(pool_set, SET_Z)
                    for half in range(2):
                        p = slice(64 * half, 64 * half + 64)
                        ins = v.tensor_scalar(q2bd[p, 4:8, half, :], banks[1][p, :].rearrange("p (a t) -> p a t", a=4),
                                              D2 ** -0.5, None, ALU.mult)
                    ins.then_inc(qw_dve, 1)
                    bring(1)
                if layer == 0:
                    v.wait_ge(load["rows"], 16)
                    v.wait_ge(load["ctxk"], 16)
                st.done(v.tensor_tensor(xb[:, :], x[:, :], row(f"bo{layer}"), ALU.add))

                def context3_share(i):
                    if layer == 1:
                        if i == 0:
                            st.done(v.tensor_scalar(n3[:, 0, 0:NC].unsqueeze(2), mv3[:, :, 1:2], LN_EPS, None, ALU.add))
                        elif i < RSQRT_STEPS:
                            st.done(rsqrt_step(i - 1, n3[:, 1, 0:NC], n3[:, 0, 0:NC], n3[:, 2, 0:NC]))
                        elif i == RSQRT_STEPS:
                            rsqrt_step(i - 1, n3[:, 1, 0:NC], n3[:, 0, 0:NC], n3[:, 2, 0:NC]).then_inc(c3_dve, 1)
                    else:
                        if 3 <= i < 11:
                            j = i - 3
                            v.wait_ge(c3_pool, 2)
                            v.tensor_reduce(n3[:, 0, 4 * j:4 * j + 4], k3T[:, 256 * j:256 * j + 256].rearrange("p (k d) -> p k d", d=D3),
                                            AX.X, ALU.add).then_inc(dve_step, 1)
                            st.n += 1
                        elif i == 11:
                            v.wait_ge(dve_step, st.n)
                            st.done(v.tensor_scalar(n3[:, 0, :], n3[:, 0, :], 1.0 / D3, 1e-16, ALU.mult, ALU.max))
                        elif 12 <= i < 16:
                            st.done(rsqrt_step(2 * i - 24, n3[:, 1, :], n3[:, 0, :], n3[:, 2, :]))
                            ins = rsqrt_step(2 * i - 23, n3[:, 1, :], n3[:, 0, :], n3[:, 2, :])
                            if i < 15:
                                st.done(ins)
                            else:
                                ins.then_inc(c3_dve, 1)

                for i in range(NG + 7 if layer < 2 else NG + 3):
                    if i < NG:
                        g = g0 + i
                        v.wait_ge(scores_in_psum, g + 1)
                        if layer == 0:
                            if i >= 2:
                                v.wait_ge(probs_ready, g - 1)
                            v.tensor_scalar(clipped[:, i % 2, :], banks[i % 2][:, :], -1e4, 1e4, ALU.max, ALU.min).then_inc(clip_ready, 1)
                            v.wait_ge(clip_ready, i + 1)
                            v.tensor_reduce(negmax[:, i:i + 1], clipped[:, i % 2, :], AX.X, ALU.max, negate=True).then_inc(negmax_ready, 1)
                        else:
                            v.tensor_reduce(negmax[:, i:i + 1], banks[i % 2][:, :], AX.X, ALU.max, negate=True).then_inc(negmax_ready, 1)
                    if layer == 2 and i == 1:
                        bring(3)
                    if layer > 0 and 2 <= i <= NG + 1 and (layer == 1 or i % 2 == 0):
                        j = i - 2
                        v.wait_ge(probsT_in_psum, g0 + j + 1)
                        if layer == 1:
                            if j % HG == 0 and j >= 2 * HG:
                                v.wait_ge(pc_in_psum, B * layer + j // HG - 1)
                            v.tensor_copy(probs_turned(1, j), banks[2 + j % 2][:, :]).then_inc(probsT_ready, 1)
                        else:
                            if j >= 2:
                                v.wait_ge(pc_in_psum, 2 * B + j - 1)
                            v.tensor_copy(probsT[:, j % 2, :], banks[2 + j % 2][:, :]).then_inc(probsT_ready, 1)
                    if layer == 0 and i - 1 in L0_VALUES:
                        b, bank = L0_VALUES[i - 1]
                        v.wait_ge(v_in_psum, b + 1)
                        v.tensor_copy(big_c[:, b * SK:(b + 1) * SK], banks[bank][:, :]).then_inc(v_ready, 1)
                    if layer == 0 and i == 13:
                        v.wait_ge(mean_in_psum, 1)
                        v.tensor_copy(mean_tok, banks[7][:, 0:D]).then_inc(mean_ready, 1)
                    if layer == 0 and i == NG:
                        v.wait_ge(guard_read, NG)
                        v.tensor_tensor(nan_hit[:, :], nan_sum[:, :], nan_sum[:, :], ALU.not_equal).then_inc(nan_ready, 1)
                    if layer < 2 and 6 <= i < NG + 6 and (i - 6) % 4 == 0:
                        b = (i - 6) // 4
                        v.wait_ge(probs_ready, g0 + HG * (b + 1))
                        st.done(v.reciprocal(rden[:, b * HG:(b + 1) * HG], den[:, b * HG:(b + 1) * HG]))
                        if b:
                            v.wait_ge(inverse_in_psum, B * layer + b)
                        v.tensor_tensor(inverse[:, :, :], w("head32").unsqueeze(1).to_broadcast([128, HG, 32]),
                                        rden[:, b * HG:(b + 1) * HG].unsqueeze(2).to_broadcast([128, HG, 32]),
                                        ALU.mult).then_inc(inverse_ready, 1)
                    if layer < 2 and i >= 8 and (i - 8) % 4 == 0 and i < NG + 8:
                        b = (i - 8) // 4
                        v.wait_ge(inverse_in_psum, B * layer + b + 1)
                        v.tensor_copy(turned_inverse[:, :], banks[6][:, 0:128]).then_inc(inverse_out, 1)
                    if layer < 2 and i >= 10 and (i - 10) % 4 == 0:
                        b = (i - 10) // 4
                        v.wait_ge(pc_in_psum, B * layer + b + 1)
                        v.wait_ge(inverse_out, B * layer + b + 1)
                        v.tensor_tensor(own[:, :], banks[4 + b % 2][:, 0:128], turned_inverse[:, :], ALU.mult).then_inc(own_ready, 1)
                        v.wait_ge(own_ready, B * layer + b + 1)
                        ins = v.tensor_reduce(oT[:, b * S:(b + 1) * S], own[:, :].rearrange("p (h q) -> p q h", h=HG), AX.X, ALU.add)
                        if layer == 1 and b == B - 1:
                            ins.then_inc(oT_ready, 1)
                        else:
                            st.done(ins)
                    if layer == 2 and 3 <= i <= NG + 2:
                        j = i - 3
                        v.wait_ge(probs_ready, g0 + j + 1)
                        st.done(v.reciprocal(rden[:, j:j + 1], den[:, j:j + 1]))
                        v.wait_ge(pc_in_psum, 2 * B + j + 1)
                        if j >= 4:
                            v.wait_ge(pcnT_in_psum, j - 3)
                        v.tensor_scalar(pcn[:, j % 4, :], banks[4 + j % 2][:, 0:DC], rden[:, j:j + 1], None, ALU.mult).then_inc(pcn_ready, 1)
                    if layer > 0:
                        context3_share(i)
                if layer < 2:
                    if layer == 0:
                        v.wait_ge(nan_in_psum, 1)
                        st.done(v.tensor_reduce(nan_any[:, :], banks[7][:, 256:256 + NG], AX.X, ALU.max))
                    if layer == 0:
                        v.copy_predicated(oT[:, :], nan_any[:, :].bitcast(U32).to_broadcast([128, T]),
                                          banks[7][:, 128:256]).then_inc(oT_ready, 1)
                v.wait_ge(y_full, layer + 1)
                v.tensor_tensor(x[:, :], banks[2][:, 0:D], xb[:, :], ALU.add).then_inc(x_ready, 1)

            def top2(values):
                st.done(v.max(top8[:, :], values))
                st.done(v.max_index(idx8[:, :], top8[:, :], values))
                st.done(v.tensor_copy(idxf[:, :], idx8[:, :]))

            def onehot(k, scale):
                return v.tensor_scalar(oh[:, k, :], w("iota"), idxf[:, k:k + 1], scale, ALU.is_equal, ALU.mult)

            def route_logits(layer):
                v.wait_ge(logits_in_psum, layer + 1)
                logits = banks[7][:, 256:264]
                if layer == 0:
                    st.done(v.tensor_tensor(lg[:, :], logits, row("f0_br"), ALU.add))
                else:
                    st.done(v.tensor_copy(lg[:, :], logits))
                if layer != 2:
                    v.tensor_reduce(rt[:, 0:1], lg[:, :], AX.X, ALU.max, negate=True).then_inc(lneg_ready, 1)

            def route_choice(layer):
                if layer == 2:
                    top2(lg[:, :])
                    return
                v.wait_ge(lexp_ready, {0: 1, 3: 3}[layer])
                st.done(v.reciprocal(rt[:, 2:3], rt[:, 1:2]))
                st.done(v.tensor_scalar(sc8[:, :], sc8[:, :], rt[:, 2:3], None, ALU.mult))
                top2(sc8[:, :])
                if layer == 3:
                    onehot(0, 1.0)
                    onehot(1, 1.0).then_inc(cw_ready, 1)

            def route_weights(layer):
                if layer == 2:
                    st.done(v.tensor_scalar(cw[:, :], w("iota"), idxf[:, 0:1], 0.5, ALU.is_equal, ALU.mult))
                    return
                if layer == 0:
                    for k in range(2):
                        ins = onehot(k, top8[:, k:k + 1])
                    st.done(ins)
                    v.tensor_tensor(cw[:, :], oh[:, 0, :], oh[:, 1, :], ALU.add).then_inc(cw_ready, 1)
                    v.wait_ge(cw_ready, 1)
                    return
                st.done(v.tensor_tensor(rt[:, 3:4], top8[:, 0:1], top8[:, 1:2], ALU.add))
                st.done(v.reciprocal(rt[:, 4:5], rt[:, 3:4]))
                st.done(v.tensor_scalar(rt[:, 5:7], top8[:, 0:2], rt[:, 4:5], 0.5, ALU.mult, ALU.mult))
                v.wait_ge(cwT_in_psum, 3)
                st.done(v.tensor_scalar(place[:, :], banks[7][:, 0:16], float(CAP), None, ALU.is_le))
                for k in range(2):
                    ins = v.scalar_tensor_tensor(out=oh[:, k, :], in0=oh[:, k, :], scalar=rt[:, 5 + k:6 + k],
                                                 in1=place[:, 8 * k:8 * k + 8], op0=ALU.mult, op1=ALU.mult)
                st.done(ins)
                st.done(v.tensor_tensor(cw[:, :], oh[:, 0, :], oh[:, 1, :], ALU.add))

            def route_in_groups(gated, multiplied):
                def done_after(ins, filler, e):
                    n = st.count(ins)
                    filler(e)
                    st.after(n)

                groups = sc8[:, :].rearrange("p (g e) -> p g e", g=4)
                v.wait_ge(lexp_ready, 2)
                st.done(v.reciprocal(rt[:, 2:3], rt[:, 1:2]))
                done_after(v.tensor_scalar(sc8[:, :], sc8[:, :], rt[:, 2:3], None, ALU.mult), gated, 2)
                v.wait_ge(pool_set, SET_G)
                st.done(v.tensor_reduce(grp8[:, 0:4], groups, AX.X, ALU.max))
                done_after(v.max(top8[:, :], grp8[:, :]), multiplied, 2)
                st.done(v.max_index(idx8[:, :], top8[:, :], grp8[:, :]))
                st.done(v.tensor_copy(idxf[:, :], idx8[:, :]))
                onehot(0, 1.0)
                st.done(onehot(1, 1.0))
                st.done(v.tensor_tensor(oh[:, 0, 0:4], oh[:, 0, 0:4], oh[:, 1, 0:4], ALU.add))
                done_after(v.tensor_tensor(groups, groups, oh[:, 0, 0:4].unsqueeze(2).to_broadcast([128, 4, 2]), ALU.mult), gated, 3)
                st.done(v.max(top8[:, :], sc8[:, :]))
                done_after(v.max_index(idx8[:, :], top8[:, :], sc8[:, :]), multiplied, 3)
                st.count(v.tensor_copy(idxf[:, :], idx8[:, :]))
                st.done(v.tensor_tensor(rt[:, 3:4], top8[:, 0:1], top8[:, 1:2], ALU.add))
                st.done(v.reciprocal(rt[:, 4:5], rt[:, 3:4]))
                done_after(v.tensor_scalar(rt[:, 5:7], top8[:, 0:2], rt[:, 4:5], 0.5, ALU.mult, ALU.mult), gated, 4)
                onehot(0, rt[:, 5:6])
                done_after(onehot(1, rt[:, 6:7]), multiplied, 4)
                st.done(v.tensor_tensor(cw[:, :], oh[:, 0, :], oh[:, 1, :], ALU.add))

            def feed_forward(layer):
                e0 = E * layer
                C = FFN_CHUNKS[layer] * 128
                gated_at = {}

                def hidden(e):
                    n = e0 + e
                    if layer == 0:
                        v.wait_ge(up_in_psum, n + 1)
                        if e >= 3:
                            v.wait_ge(y_in_psum, n - 2)
                        v.tensor_scalar(hid[:, e % 3, T:2 * T], banks[2 + e % 2][:, 0:T], w("f0_b1", 128, 2 * e + 1, 2 * e + 2), 0.0,
                                        ALU.add, ALU.max).then_inc(hid_ready, 1)
                        return
                    gated(e)
                    multiplied(e)

                def gated(e):
                    n = e0 + e
                    v.wait_ge(tanh_ready, n + 1 - E)
                    if e:
                        v.wait_ge(hid_ready, n)
                    gated_at[e] = st.count(v.scalar_tensor_tensor(out=act_a[:, 0:C], in0=tg[:, e % 2, 0:C], scalar=1.0,
                                                                  in1=banks[e % 2][:, 0:C], op0=ALU.add, op1=ALU.mult))

                def multiplied(e):
                    n = e0 + e
                    st.after(gated_at[e])
                    v.wait_ge(up_in_psum, n + 1)
                    if e >= 3:
                        v.wait_ge(y_in_psum, n - 2)
                    v.tensor_tensor(hid[:, e % 3, 0:C], act_a[:, 0:C], banks[2 + e % 2][:, 0:C], ALU.mult).then_inc(hid_ready, 1)

                def add(e):
                    n = e0 + e
                    v.wait_ge(y_in_psum, n + 1)
                    if e:
                        v.wait_ge(y_added, Y_BASE[layer] + e)
                    last = layer > 0 and e == E - 1
                    v.scalar_tensor_tensor(out=x[:, :], in0=banks[4 + e % 3][:, 0:D], scalar=cw[:, e:e + 1], in1=x[:, :],
                                           op0=ALU.mult, op1=ALU.add).then_inc(x_ready if last else y_added, 1)

                hidden(0)
                route_logits(layer)
                hidden(1)
                if layer == 1:
                    route_in_groups(gated, multiplied)
                    add(0)
                    add(1)
                    for e in range(5, E):
                        gated(e)
                        add(e - 3)
                        multiplied(e)
                    for e in range(E - 3, E):
                        add(e)
                    return
                route_choice(layer)
                hidden(2)
                route_weights(layer)
                for e in range(3, E):
                    hidden(e)
                    add(e - 3)
                    if layer == 0:
                        context3_stats(2 * e, 2 * e + 2)
                for e in range(E - 3, E):
                    add(e)
                if layer == 0:
                    v.wait_ge(cwT_in_psum, 1)
                    v.tensor_copy(cwT[:, :], banks[7][0:8, 0:T]).then_inc(cwT_ready, 1)
                    v.wait_ge(cwT_in_psum, 2)
                    v.wait_ge(y_added, E)
                    v.tensor_tensor(x[:, :], banks[7][:, 256:256 + D], x[:, :], ALU.add).then_inc(x_ready, 1)

            def spread_keys():
                v.tensor_tensor(k_own, qk_[:, 1, :].rearrange("p (b t) -> p b t", b=B).unsqueeze(2).to_broadcast([128, B, 4, S]),
                                w("own4").unsqueeze(1).unsqueeze(3).to_broadcast([128, B, 4, S]), ALU.mult).then_inc(mix_dve, 1)

            def turn_scores(hg):
                return v.transpose(pT_sb[:, 4 * hg:4 * hg + 4, :].rearrange("p h t -> p (h t)"),
                                   s_sb[:, 4 * hg:4 * hg + 4, :].rearrange("p h t -> p (h t)"))

            def weigh(pe0, eps):
                st.done(v.tensor_reduce(den16[:, :], s_sb[:, :, :], AX.X, ALU.add))
                if eps:
                    st.done(v.tensor_scalar(den16[:, :], den16[:, :], eps, None, ALU.add))
                st.done(v.reciprocal(den16[:, :], den16[:, :]))
                v.tensor_copy(inverse[:, :, :].rearrange("p g n -> p (g n)").rearrange("p (h d) -> p h d", h=H),
                              den16[:, :].unsqueeze(2).to_broadcast([128, H, DH])).then_inc(mix_dve, 1)
                if eps:
                    context3_stats(3, 6)
                own_values = big_b[:, 0:512].rearrange("p (b h t) -> p b h t", b=B, h=4)
                done = []
                for i in range(B + 1):
                    if i < B:
                        v.wait_ge(mix_pe, pe0 + 7 + i)
                        done.append(st.count(v.tensor_tensor(own_values[:, i], banks[VALUE_BANK[i]][:, 0:128].rearrange("p (h t) -> p h t", h=4),
                                                             w("own4").unsqueeze(2).to_broadcast([128, 4, S]), ALU.mult)))
                    if i >= 1:
                        st.after(done[i - 1])
                        last = st.count(v.tensor_reduce(z2[:, (i - 1) * S:i * S], own_values[:, i - 1].rearrange("p h t -> p t h"), AX.X, ALU.add))
                st.after(last)
                v.wait_ge(mix_pe, pe0 + 11)
                v.tensor_tensor(oT[:, :], z2[:, :], banks[7][:, 0:T], ALU.mult).then_inc(mix_dve, 1)
                v.wait_ge(mix_pe, pe0 + 12)
                v.tensor_tensor(x[:, :], banks[2][:, 0:D], x[:, :], ALU.add).then_inc(x_ready, 1)

            def linear_attention():
                v.wait_ge(mix_pe, 1)
                st.done(v.tensor_scalar(qk_[:, 0:2, :], banks[0][:, 0:2 * T].rearrange("p (a t) -> p a t", a=2), 0.0, 1e-6, ALU.max, ALU.add))
                spread_keys()
                context3_stats(0, 3)
                masked = []
                for i in range(HG + 1):
                    if i < HG:
                        v.wait_ge(mix_pe, 3 + i)
                        masked.append(st.count(v.tensor_tensor(s_sb[:, 4 * i:4 * i + 4, :], banks[3 + i][:, 0:128].rearrange("p (h t) -> p h t", h=4),
                                                               w("causal_mul").unsqueeze(1).to_broadcast([128, 4, S]), ALU.mult)))
                    if i >= 1:
                        st.after(masked[i - 1])
                        ins = turn_scores(i - 1)
                ins.then_inc(mix_dve, 1)
                weigh(0, 1e-6)

            def causal_attention():
                v.wait_ge(mix_pe, LIN_PE + 1)
                pair = lambda ap: ap.rearrange("p (a t) -> p a t", a=2)
                v.tensor_tensor(qk_[:, 0:2, :], pair(banks[0][:, 0:2 * T]), w("rope_cos").unsqueeze(1).to_broadcast([128, 2, T]), ALU.mult)
                st.done(v.tensor_tensor(qk_[:, 2:4, :], pair(banks[1][:, 0:2 * T]), w("rope_sin").unsqueeze(1).to_broadcast([128, 2, T]),
                                        ALU.mult))
                st.done(v.tensor_tensor(qk_[:, 0:2, :], qk_[:, 0:2, :], qk_[:, 2:4, :], ALU.add))
                spread_keys()
                added, highest = [], []
                for i in range(HG + 4):
                    if i < HG:
                        v.wait_ge(mix_pe, LIN_PE + 3 + i)
                        added.append(st.count(v.tensor_tensor(s_sb[:, 4 * i:4 * i + 4, :], banks[3 + i][:, 0:128].rearrange("p (h t) -> p h t", h=4),
                                                              w("causal_add").unsqueeze(1).to_broadcast([128, 4, S]), ALU.add)))
                    k = i - 1
                    if 0 <= k < HG:
                        st.after(added[k])
                        highest.append(st.count(v.tensor_reduce(den16[:, 4 * k:4 * k + 4], s_sb[:, 4 * k:4 * k + 4, :], AX.X, ALU.max)))
                    k = i - 2
                    if 0 <= k < HG:
                        st.after(highest[k])
                        v.tensor_tensor(s_sb[:, 4 * k:4 * k + 4, :], s_sb[:, 4 * k:4 * k + 4, :],
                                        den16[:, 4 * k:4 * k + 4].unsqueeze(2).to_broadcast([128, 4, S]),
                                        ALU.subtract).then_inc(mix_dve, 1)
                    k = i - 4
                    if k >= 0:
                        v.wait_ge(mix_act, 3 + k)
                        ins = turn_scores(k)
                ins.then_inc(mix_dve, 1)
                weigh(LIN_PE, None)

            def lstm():
                for t in range(B):
                    v.wait_ge(mix_act, CAU_ACT + 2 * t + 1)
                    v.scalar_tensor_tensor(out=cst[:, 1 if t else 2, :], in0=gates[:, 0, :], scalar=1.0, in1=gates[:, 3, :],
                                           op0=ALU.add, op1=ALU.mult).then_inc(dve_step if t else mix_dve, 1)
                    if t:
                        st.n += 1
                        st.done(v.scalar_tensor_tensor(out=cst[:, 0, :], in0=gates[:, 1, :], scalar=1.0, in1=cst[:, 4, :],
                                                       op0=ALU.add, op1=ALU.mult))
                        v.tensor_tensor(cst[:, 2, :], cst[:, 0, :], cst[:, 1, :], ALU.add).then_inc(mix_dve, 1)
                    v.wait_ge(mix_dve, CAU_DVE + 2 * t + 1)
                    st.done(v.tensor_scalar(cst[:, 4, :], cst[:, 2, :], 0.5, None, ALU.mult))
                    v.wait_ge(mix_act, CAU_ACT + 2 * t + 2)
                    v.scalar_tensor_tensor(out=h2T[:, t * S:(t + 1) * S], in0=gates[:, 2, :], scalar=1.0, in1=cst[:, 3, :],
                                           op0=ALU.add, op1=ALU.mult).then_inc(mix_dve, 1)
                v.wait_ge(mix_pe, CAU_PE + B + 1)
                v.scalar_tensor_tensor(out=x[:, :], in0=banks[1][:, 0:D], scalar=0.5, in1=x[:, :],
                                       op0=ALU.mult, op1=ALU.add).then_inc(x_ready, 1)

            def cross3():
                v.wait_ge(x_ready, 9)
                v.wait_ge(pool_set, SET_L3)
                st.done(v.tensor_tensor(xb[:, :], x[:, :], row("bo3"), ALU.add))
                st.done(v.bn_stats(stats[:, :], x[:, :]))
                st.done(v.bn_aggr(mv[:, :], stats[:, :]))
                st.done(v.tensor_scalar(nw[:, 0:1], mv[:, 1:2], LN_EPS, None, ALU.add))
                rsqrt_column()
                st.done(v.scalar_tensor_tensor(out=nw[:, 0:1], in0=nw[:, 1:2], scalar=nw[:, 1:2], in1=mv[:, 1:2], op0=ALU.mult, op1=ALU.mult))
                v.tensor_copy(nw[:, 4:5], nw[:, 1:2])
                st.done(v.tensor_scalar(nw[:, 0:1], nw[:, 0:1], LN_EPS, None, ALU.add))
                rsqrt_column()
                st.done(v.tensor_tensor(nw[:, 4:5], nw[:, 4:5], nw[:, 1:2], ALU.mult))
                v.tensor_scalar(z2[:, :], x[:, :], mv[:, 0:1], nw[:, 4:5], ALU.subtract, ALU.mult).then_inc(c3_dve, 1)
                v.wait_ge(q_in_psum, 5)
                v.tensor_scalar(xnT[:, :], banks[7][:, 0:T], w("l3_g"), w("l3_b"), ALU.mult, ALU.add).then_inc(c3_dve, 1)
                v.wait_ge(c3_act, 17)
                st.done(v.tensor_tensor(big_a[:, 0:256], qkv3[:, 0:256], qkv3[:, 0:256], ALU.mult))
                st.done(v.tensor_reduce(d3[:, 4:8], big_a[:, 0:256].rearrange("p (k d) -> p k d", d=D3), AX.X, ALU.add))
                st.done(v.tensor_scalar(n3[:, 0, 0:4], d3[:, 4:8], 1.0 / D3, 1e-16, ALU.mult, ALU.max))
                rsqrt(n3[:, 1, 0:4], n3[:, 0, 0:4], n3[:, 2, 0:4])
                v.tensor_tensor(xn[:, :].rearrange("p (h d) -> p h d", h=2), qkv3[:, 0:128].rearrange("p (h d) -> p h d", h=2),
                                n3[:, 1, 0:2].unsqueeze(2).to_broadcast([128, 2, D3]), ALU.mult)
                v.tensor_tensor(z2[:, :].rearrange("p (h d) -> p h d", h=2), qkv3[:, 128:256].rearrange("p (h d) -> p h d", h=2),
                                n3[:, 1, 2:4].unsqueeze(2).to_broadcast([128, 2, D3]), ALU.mult).then_inc(c3_dve, 1)
                v.wait_ge(c3_pe, 18)
                st.done(v.tensor_scalar(qT[:, :], banks[1][:, 0:T], w("qn_g"), w("kn_g"), ALU.mult, ALU.mult))
                v.tensor_copy(kl3T, banks[2][:, 0:T])
                for h in range(H3):
                    p = slice(64 * h, 64 * h + 64)
                    ins = v.tensor_scalar(q3bd[p, h, :], qT[p, :], D3 ** -0.5, None, ALU.mult)
                ins.then_inc(c3_dve, 1)
                for h in range(H3):
                    part = big_a[:, h * 640:h * 640 + 640]
                    v.wait_ge(c3_pe, 19 + h)
                    v.tensor_tensor(part[:, 0:512], banks[3 + h][:, :], mask_add, ALU.add)
                    st.done(v.tensor_tensor(part[:, 512:640], banks[5 + h][:, 0:T], w("batch_add"), ALU.add))
                    v.tensor_reduce(d3[:, h:h + 1], part, AX.X, ALU.max, negate=True).then_inc(c3_dve, 1)
                v.wait_ge(c3_act, 19)
                st.done(v.reciprocal(d3[:, 4:6], d3[:, 2:4]))
                v.tensor_copy(inverse[:, :, :].rearrange("p g n -> p (g n)").rearrange("p (h d) -> p h d", h=H3),
                              d3[:, 4:6].unsqueeze(2).to_broadcast([128, H3, D3])).then_inc(c3_dve, 1)
                v.wait_ge(c3_pe, 22)
                v.tensor_copy(big_b[:, 512:1024], banks[1][:, :])
                v.tensor_copy(big_b[:, 1024 + T:1024 + 2 * T], banks[7][:, 0:T]).then_inc(c3_dve, 1)
                v.wait_ge(c3_pe, 23)
                st.done(v.tensor_copy(turned_inverse[:, :], banks[5][:, 0:T]))
                v.wait_ge(c3_pe, 24)
                v.tensor_tensor(oT[:, :], banks[6][:, 0:T], turned_inverse[:, :], ALU.mult).then_inc(c3_dve, 1)
                v.wait_ge(y_full, 4)
                v.tensor_tensor(x[:, :], banks[0][:, 0:D], xb[:, :], ALU.add).then_inc(x_ready, 1)

            def state_space():
                m, d, a = CAU_PE + B + 1, CAU_DVE + 2 * B, CAU_ACT + 2 * B
                st.done(v.tensor_scalar(half_taps, late[:, late_at["m_cw"][0]:late_at["m_cw"][0] + 32], 0.5, None, ALU.mult))
                v.wait_ge(mix_pe, m + 1)
                v.tensor_tensor(dts[:, 0, :].rearrange("p (d h) -> p d h", d=2),
                                banks[6][:, 256:264].rearrange("p (d h) -> p d h", d=2),
                                row("dtb").unsqueeze(1).to_broadcast([128, 2, NH]), ALU.add).then_inc(mix_dve, 1)
                st.done(v.tensor_copy(convp[:, :, :, PAD:PAD + S], banks[0][:, 0:2 * T].rearrange("p (j b l) -> p j b l", j=2, b=B)))
                for k in range(TAPS):
                    for j in range(2):
                        out = big_b[:, j * T:(j + 1) * T].rearrange("p (b l) -> p b l", b=B)
                        src = convp[:, j, :, k:k + S]
                        tap = half_taps[:, 7 * j + k:7 * j + k + 1]
                        if k == 0:
                            ins = v.tensor_scalar(out, src, tap, half_taps[:, 28 + j:29 + j], ALU.mult, ALU.add)
                        else:
                            ins = v.scalar_tensor_tensor(out=out, in0=src, scalar=tap, in1=out, op0=ALU.mult, op1=ALU.add)
                    if k == TAPS - 1:
                        ins.then_inc(mix_dve, 1)
                    else:
                        st.done(ins)
                    if k == 4:
                        v.wait_ge(mix_dve, d + 1)
                        st.done(v.tensor_scalar(dts[:, 3, :], dts[:, 0, :], 0.0, None, ALU.max))
                        v.wait_ge(mix_act, a + 4)
                        st.done(v.tensor_tensor(dts[:, 3, :], dts[:, 3, :], dts[:, 2, :], ALU.add))
                        st.done(v.tensor_tensor(dts[:, 4, :].rearrange("p (d h) -> p d h", d=2), dts[:, 3, :].rearrange("p (d h) -> p d h", d=2),
                                                dts[:, 5, 0:4].unsqueeze(1).to_broadcast([128, 2, NH]), ALU.mult))
                        for i, name in enumerate(("m_fw", "m_bw")):
                            ins = v.tensor_tensor(big_a[:, i * 512:i * 512 + 512].rearrange("p (h t) -> p h t", h=NH),
                                                  w(name).unsqueeze(1).to_broadcast([128, NH, T]),
                                                  dts[:, 4, 4 * i:4 * i + 4].unsqueeze(2).to_broadcast([128, NH, T]), ALU.mult)
                        ins.then_inc(mix_dve, 1)
                v.wait_ge(mix_act, a + 5)
                v.scalar_tensor_tensor(out=big_b[:, 1280:1536], in0=big_b[:, 768:1024], scalar=1.0, in1=big_b[:, 256:512],
                                       op0=ALU.add, op1=ALU.mult).then_inc(mix_dve, 1)
                v.wait_ge(mix_dve, d + 4)
                v.tensor_copy(cbd[0:64, 0, 1:T], big_b[0:64, 1408:1535])
                v.tensor_copy(cbd[64:128, 1, 0:T - 1], big_b[64:128, 1409:1536]).then_inc(mix_dve, 1)
                v.wait_ge(mix_act, a + 9)
                v.scalar_tensor_tensor(out=big_b[:, 1024:1280], in0=big_b[:, 512:768], scalar=1.0, in1=big_b[:, 0:256],
                                       op0=ALU.add, op1=ALU.mult).then_inc(mix_dve, 1)
                v.wait_ge(mix_pe, m + 6)
                gm = big_c[:, 768:1024]
                st.done(v.tensor_tensor(gm.rearrange("p (d t) -> p d t", d=2), banks[5][:, 0:256].rearrange("p (d t) -> p d t", d=2),
                                        late[:, late_at["m_fw"][0]:late_at["m_fw"][0] + 256].rearrange("p (d t) -> p d t", d=2), ALU.mult))
                v.wait_ge(mix_pe, m + 7)
                v.tensor_copy(big_c[:, 256:512], banks[4][:, 0:256])
                st.done(v.tensor_tensor(dts[:, 5, 4:8], banks[6][:, 0:4], row("dp"), ALU.add))
                v.wait_ge(mix_act, a + 8)
                for i in range(2):
                    dec = big_a[:, 1024 + 512 * i:1536 + 512 * i].rearrange("p (h t) -> p h t", h=NH)
                    ins = v.tensor_tensor(dec, dec, gm[:, i * T:(i + 1) * T].unsqueeze(1).to_broadcast([128, NH, T]), ALU.mult)
                ins.then_inc(mix_dve, 1)
                st.done(v.tensor_tensor(big_c[:, 1536:1792].rearrange("p (h n) -> p h n", h=NH),
                                        big_c[:, 256:512].rearrange("p (h n) -> p h n", h=NH),
                                        dts[:, 5, 4:8].unsqueeze(2).to_broadcast([128, NH, 64]), ALU.mult))
                st.done(v.scalar_tensor_tensor(out=big_c[:, 1792:2048], in0=big_c[:, 0:256], scalar=1.0, in1=banks[1][:, 0:256],
                                               op0=ALU.add, op1=ALU.mult))
                v.wait_ge(mix_pe, m + 8)
                y = big_c[:, 1024:1280]
                v.tensor_tensor(y, banks[0][:, 0:256], big_c[:, 1536:1792], ALU.add).then_inc(mix_dve, 1)
                v.wait_ge(mix_act, a + 10)
                st.done(v.tensor_scalar(nw[:, 0:1], nw[:, 0:1], 1.0 / DI, 1e-5, ALU.mult, ALU.add))
                rsqrt_column()
                v.scalar_tensor_tensor(out=y, in0=y, scalar=nw[:, 1:2], in1=big_c[:, 1792:2048],
                                       op0=ALU.mult, op1=ALU.mult).then_inc(mix_dve, 1)
                v.wait_ge(mix_pe, m + 9)
                for j in range(2):
                    ins = v.tensor_scalar(big_c[:, 1280 + j * 128:1280 + (j + 1) * 128], banks[1][:, j * 128:(j + 1) * 128],
                                          w("m_nw", 128, j, j + 1), 0.5, ALU.mult, ALU.mult)
                ins.then_inc(mix_dve, 1)
                v.wait_ge(mix_pe, m + 10)
                v.tensor_tensor(x[:, :], banks[2][:, 0:D], x[:, :], ALU.add).then_inc(x_ready, 1)

            v.wait_ge(load["x"], 16)
            v.wait_ge(load["early"], 16)
            norm(0)
            context_attention(0)
            norm(1); linear_attention()
            v.wait_ge(load["late"], 16)
            norm(2); feed_forward(0)
            norm(3); context_attention(1)
            norm(4); causal_attention()
            norm(5); feed_forward(1)
            norm(6); context_attention(2)
            norm(7); lstm()
            norm(8); feed_forward(2)
            cross3()
            norm(10); state_space()
            norm(11); feed_forward(3)


def constants():
    p = np.arange(128)
    one = np.float32
    batch, t = p // S, p % S
    same = batch[:, None] == batch[None, :]
    c = {
        "ident": np.eye(128), "head16": p[:, None] // DH == np.arange(H)[None, :],
        "head32": p[:, None] // S == np.arange(32)[None, :] // DH, "own4": p[:, None] // DH % 4 == np.arange(4)[None, :],
        "ones": np.ones((128, 128)), "causal_mul": np.arange(S)[None, :] <= t[:, None],
        "causal_add": np.where(np.arange(S)[None, :] <= t[:, None], 0.0, -BIG),
        "cum": p[:, None] <= p[None, :],
        "m_fw": same & (p[:, None] < p[None, :]), "m_bw": same & (p[:, None] > p[None, :]),
        "l_fw": same & (p[:, None] > p[None, :]), "l_bw": same & (p[:, None] < p[None, :]),
        "batch_add": np.where(same, 0.0, -BIG), "iota": np.tile(np.arange(8), (128, 1)),
    }
    d = p % DH
    freq = (np.float32(10000.0) ** (-(np.arange(0, DH, 2, dtype=np.float32)) / np.float32(DH)))[d // 2]
    ang = t[None, :].astype(np.float32) * freq[:, None].astype(np.float32)
    c["rope_cos"] = np.cos(ang)
    c["rope_sin"] = np.sin(ang) * np.where(d % 2 == 0, -1.0, 1.0)[:, None]
    return {k: np.asarray(v, one) for k, v in c.items()}


def kernel(**inputs):
    import concourse.bacc as bacc
    from concourse.bass_utils import run_bass_kernel_spmd

    i = {k: np.asarray(v) for k, v in inputs.items()}
    r = lambda a: np.ascontiguousarray(a)
    col = lambda a: a.reshape(-1, 1)
    small = constants()
    for k, pre in ((0, "L0_xattn_"), (1, "L1_xattn_")):
        if k == 0:
            wk, wv, bk, bv, wq, wo = (i[pre + n] for n in ("Wk", "Wv", "bk", "bv", "Wq", "Wo"))
        else:
            kv = i[pre + "Wkv"].reshape(H, 2, DH, DC)
            bkv = i[pre + "bkv"].reshape(H, 2, DH)
            wk, wv = (kv[:, j].reshape(D, DC).T for j in range(2))
            bk, bv = (bkv[:, j].reshape(D) for j in range(2))
            wq, wo = i[pre + "Wq"].T, i[pre + "Wo"].T
        small[f"wq{k}"], small[f"wo{k}"], small[f"bq{k}"] = wq, wo, col(i[pre + "bq"])
        small[f"wk{k}"] = np.concatenate([wk, bk[None, :]], axis=0)
        small[f"wv{k}"] = np.concatenate([wv, bv[None, :]], axis=0)
    for n in ("q", "k", "v", "o"):
        small["a_w" + n] = i["L0_attn_W" + n].T
        small["r_w" + n] = i[f"L1_attn_{n}_proj"].T
    swap = np.arange(D) ^ 1
    for n in ("r_wq", "r_wk"):
        small[n] = np.concatenate([small[n], small[n][:, swap]], axis=1)
    small["f0_wr"], small["f1_wr"] = i["L0_ffn_Wr"], i["L1_ffn_gate_w"].T
    small["f2_wr"], small["f3_wr"] = i["L2_ffn_router_w"].T, i["L3_ffn_gate_w"].T
    small["f0_b1"] = i["L0_ffn_b1"].reshape(E * 2, 128).T
    small["f0_b2"] = i["L0_ffn_b2"]
    small["lstm_w"], small["lstm_u"] = i["L2_attn_w"], i["L2_attn_u"]
    small["x3_g"], small["x3_b"] = col(i["L3_xattn_ln_x_g"]), col(i["L3_xattn_ln_x_b"])
    small["l3_g"], small["l3_b"] = col(i["L3_xattn_ln_l_g"]), col(i["L3_xattn_ln_l_b"])
    small["qn_g"], small["kn_g"] = (col(np.tile(i[f"L3_xattn_{n}_g"], 2)) for n in ("qn", "kn"))
    small["x3_wqkv"] = np.concatenate([i["L3_xattn_Wq"].T, i["L3_xattn_Wlkv"].T], axis=1)
    small["x3_wkv"], small["x3_wo"] = i["L3_xattn_Wkv"].T, i["L3_xattn_Wo"].T
    ch = np.concatenate([np.arange(256), np.arange(256, 320), np.arange(384, 448), np.arange(320, 384), np.arange(448, 512)])
    order = np.concatenate([np.arange(DI), DI + ch, np.arange(768, 776)])
    small["m_in"] = i["L3_attn_W_in"][order].T
    small["m_cw"] = i["L3_attn_conv_w"][ch, 0].reshape(4, 128, TAPS).transpose(1, 0, 2).reshape(128, 28)
    small["m_cb"] = i["L3_attn_conv_b"][ch].reshape(4, 128).T
    small["m_fc"] = i["L3_attn_fc_D_w"].reshape(NH, 2, 128).transpose(2, 1, 0).reshape(128, 8)
    small["m_nw"] = i["L3_attn_norm_w"].reshape(2, 128).T
    small["m_out"] = i["L3_attn_W_out"].T.reshape(2, 128, 128).transpose(1, 0, 2).reshape(128, 256)

    def pack(table):
        out = np.zeros((128, columns(table)[1]), np.float32)
        for name, (at, n) in columns(table)[0].items():
            out[:small[name].shape[0], at:at + n] = small[name]
        return out

    def pad(a):
        return np.concatenate([a, np.zeros((E, 384 - a.shape[1], 128), a.dtype)], axis=1)

    def chunked(a):
        return r(a.reshape(E, -1, 128, 128).transpose(2, 0, 1, 3).reshape(128, E, -1))

    ctx = i["ctx_768"].reshape(B * SK, DC)
    up = lambda a: r(a.transpose(2, 0, 1))
    arrays = {
        "early": pack(EARLY), "late": pack(LATE), "x": r(i["x"].reshape(T, D)),
        "rows": r(np.concatenate([i["L0_xattn_bo"], i["L1_xattn_bo"], i["L2_xattn_b_out"], i["L3_xattn_bo"], i["L0_ffn_br"],
                                  i["L3_attn_dt_bias"], i["L3_attn_A_log"], i["L3_attn_Dp"], i["L2_attn_bias"]])[None, :]),
        "ctxT": r(ctx.T), "ctxk": r(ctx.reshape(NC, 128, DC).transpose(1, 0, 2)),
        "mask": r(i["mask_BxS2_bk0"]), "taps": r(i["L3_attn_conv_w"][ch[256:], 0].T.reshape(1, -1)),
        "f0_w1": r(i["L0_ffn_W1"].transpose(1, 0, 2)), "f0_w2": chunked(i["L0_ffn_W2"]),
        "f1_w13": up(i["L1_ffn_w13_weight"]), "f1_w2": chunked(i["L1_ffn_w2_weight"].transpose(0, 2, 1)),
        "f2_wg": up(pad(i["L2_ffn_gate_w"])), "f2_wu": up(pad(i["L2_ffn_up_w"])),
        "f2_wd": chunked(pad(i["L2_ffn_down_w"].transpose(0, 2, 1))),
        "f3_wg": up(i["L3_ffn_wi_gate"]), "f3_wu": up(i["L3_ffn_wi_up"]), "f3_wd": chunked(i["L3_ffn_wo"].transpose(0, 2, 1)),
        "x2_wq": r(i["L2_xattn_w_q"]), "x2_wkT": r(i["L2_xattn_w_k"].T.reshape(8, 128, DC).transpose(1, 0, 2)),
        "x2_wv": r(i["L2_xattn_w_v"]), "x2_wo": r(i["L2_xattn_w_out"].reshape(8, 128, 128).transpose(1, 0, 2)),
    }
    nc = bacc.Bacc("TRN2", target_bir_lowering=False, num_devices=1)
    feeds = {f"in_{n}": a for n, a in arrays.items()}
    dram = {n: nc.dram_tensor(f"in_{n}", a.shape, mybir.dt.from_np(a.dtype), kind="ExternalInput").ap()
            for n, a in arrays.items()}
    dram["out"] = nc.dram_tensor("out_x", (T, D), F32, kind="ExternalOutput").ap()
    build(nc, dram)
    got = run_bass_kernel_spmd(nc, [feeds], core_ids=[0]).results[0]["out_x"]
    return got.reshape(B, S, D)
```
